# Optimizing a Trainium2 kernel written in Bass

```python
import numpy as np
import jax
import jax.numpy as jnp

def _softmax(x, axis=-1):
    return jax.nn.softmax(x, axis=axis)

def _gelu(x):
    return jax.nn.gelu(x, approximate=True)

def _silu(x):
    return jax.nn.silu(x)

def _sigmoid(x):
    return jax.nn.sigmoid(x)

def _layernorm(x, axis=-1, eps=1e-05):
    m = jnp.mean(x, axis=axis, keepdims=True)
    v = jnp.var(x, axis=axis, keepdims=True)
    return (x - m) / jnp.sqrt(v + eps)

def _scatter_add(tgt, idx, src, axis=0):
    return tgt.at[idx].add(src)

def _segment_sum(src, seg, n):
    return jax.ops.segment_sum(src, seg, n)
kernel_name = 'mk_gnn_preln_d4_gnn_r32_b4c809'

def setup_inputs(seed: int=0):
    np.random.seed(seed)
    _w = jnp.asarray

    def _rec_inputs():
        import jax
        import jax.numpy as jnp
        _gk = jax.random.key(seed)
        x = -0.0003713 + 1 * jax.random.normal(jax.random.fold_in(_gk, 1), (3125, 128), jnp.float32)
        _s = jax.random.randint(jax.random.fold_in(_gk, 2), (25000,), 0, 3125, jnp.int32)
        _d = jax.random.randint(jax.random.fold_in(_gk, 3), (25000,), 0, 3125, jnp.int32)
        _loop = jnp.arange(3125, dtype=jnp.int32)
        src = jnp.concatenate([_s, _d, _loop])
        dst = jnp.concatenate([_d, _s, _loop])
        _o = jnp.argsort(dst, stable=True)
        src = src[_o]
        dst = dst[_o]
        edge_attr_3 = 0.00117183 + 1.0004 * jax.random.normal(jax.random.fold_in(_gk, 13), (53125, 3), jnp.float32)
        edge_type_4 = jax.random.randint(jax.random.fold_in(_gk, 15), (53125,), 0, 4, jnp.int32)
        return (x, src, dst, edge_attr_3, edge_type_4)
    x, src, dst, edge_attr_3, edge_type_4 = _rec_inputs()

    def _L0_gnn_setup():
        import jax, jax.numpy as jnp
        import numpy as np
        N_NODES = 3125
        N_EDGES = 50000
        D = 128
        H = 8
        DH = D // H
        DFF = 2 * D
        EPS_LN = 1e-05

        def _ln(x, g, b):
            mu = jnp.mean(x, axis=-1, keepdims=True)
            var = jnp.var(x, axis=-1, keepdims=True)
            return (x - mu) * jax.lax.rsqrt(var + EPS_LN) * g + b
        key = jax.random.key(seed)
        ks = jax.random.split(key, 12)
        s = 1.0 / np.sqrt(D)
        inp = {'h': jax.random.normal(ks[0], (N_NODES, D), jnp.float32), 'src': jax.random.randint(ks[1], (N_EDGES,), 0, N_NODES, jnp.int32), 'dst': jax.random.randint(ks[2], (N_EDGES,), 0, N_NODES, jnp.int32), 'Wq': jax.random.normal(ks[3], (D, D), jnp.float32) * s, 'Wk': jax.random.normal(ks[4], (D, D), jnp.float32) * s, 'Wv': jax.random.normal(ks[5], (D, D), jnp.float32) * s, 'Wo': jax.random.normal(ks[6], (D, D), jnp.float32) * s, 'bo': jnp.zeros((D,), jnp.float32), 'ln1_g': jnp.ones((D,), jnp.float32), 'ln1_b': jnp.zeros((D,), jnp.float32), 'W1': jax.random.normal(ks[7], (D, DFF), jnp.float32) * s, 'b1': jnp.zeros((DFF,), jnp.float32), 'W2': jax.random.normal(ks[8], (DFF, D), jnp.float32) * (1.0 / np.sqrt(DFF)), 'b2': jnp.zeros((D,), jnp.float32), 'ln2_g': jnp.ones((D,), jnp.float32), 'ln2_b': jnp.zeros((D,), jnp.float32)}
        return inp
    _L0_gnn_all = _L0_gnn_setup()
    _L0_gnn_in = {k: v for k, v in _L0_gnn_all.items() if k in ('Wq', 'Wk', 'Wv', 'Wo', 'bo', 'ln1_g', 'ln1_b', 'W1', 'b1', 'W2', 'b2', 'ln2_g', 'ln2_b')}
    del _L0_gnn_all

    def _L1_gnn_setup():
        import jax, jax.numpy as jnp
        import numpy as np
        N_NODES = 50000
        N_EDGES = 25000
        IN_FEAT = 128
        INTER_DIM = 128
        OUT_FEAT = 128
        EDGE_W_DIM = 3
        key = jax.random.key(seed)
        ks = jax.random.split(key, 8)
        h = jax.random.normal(ks[0], (N_NODES, IN_FEAT), dtype=jnp.float32)
        edge_src = jax.random.randint(ks[1], (N_EDGES,), 0, N_NODES, dtype=jnp.int32)
        edge_dst = jax.random.randint(ks[2], (N_EDGES,), 0, N_NODES, dtype=jnp.int32)
        edge_w = jax.random.normal(ks[3], (N_EDGES, EDGE_W_DIM), dtype=jnp.float32)
        gain = float(np.sqrt(2.0))
        W1 = jax.random.normal(ks[4], (INTER_DIM, IN_FEAT + EDGE_W_DIM), dtype=jnp.float32)
        W1 = W1 * (gain * np.sqrt(2.0 / (INTER_DIM + IN_FEAT + EDGE_W_DIM)))
        b1 = jnp.zeros((INTER_DIM,), dtype=jnp.float32)
        W2 = jax.random.normal(ks[5], (OUT_FEAT, IN_FEAT + INTER_DIM), dtype=jnp.float32)
        W2 = W2 * (gain * np.sqrt(2.0 / (OUT_FEAT + IN_FEAT + INTER_DIM)))
        b2 = jnp.zeros((OUT_FEAT,), dtype=jnp.float32)
        return {'h': h, 'edge_src': edge_src, 'edge_dst': edge_dst, 'edge_w': edge_w, 'W1': W1, 'b1': b1, 'W2': W2, 'b2': b2}
    _L1_gnn_all = _L1_gnn_setup()
    _L1_gnn_in = {k: v for k, v in _L1_gnn_all.items() if k in ('W1', 'b1', 'W2', 'b2')}
    del _L1_gnn_all

    def _L2_gnn_setup():
        import jax, jax.numpy as jnp
        import numpy as np
        N_NODES = 3125
        N_EDGES = 100000
        FEAT = 128
        K = 4

        def spmm(x, edge_index, deg_inv_sqrt, num_nodes):
            src, dst = (edge_index[0], edge_index[1])
            norm = deg_inv_sqrt[src] * deg_inv_sqrt[dst]
            msg = x[src] * norm[:, None]
            return jax.ops.segment_sum(msg, dst, num_segments=num_nodes)
        key = jax.random.key(seed)
        k1, k2, k3, k4 = jax.random.split(key, 4)
        x = jax.random.normal(k1, (N_NODES, FEAT), dtype=jnp.float32)
        edge_index_with_loops = jax.random.randint(k2, (2, N_EDGES), 0, N_NODES, dtype=jnp.int32)
        deg_inv_sqrt = jax.random.uniform(k3, (N_NODES,), dtype=jnp.float32)
        weights = jax.random.normal(k4, (K, FEAT, FEAT), dtype=jnp.float32) * 0.01
        return {'x': x, 'edge_index_with_loops': edge_index_with_loops, 'deg_inv_sqrt': deg_inv_sqrt, 'num_nodes': N_NODES, 'weights': weights}
    _L2_gnn_all = _L2_gnn_setup()
    _L2_gnn_in = {k: v for k, v in _L2_gnn_all.items() if k in ('weights',)}
    del _L2_gnn_all

    def _L3_gnn_setup():
        import jax, jax.numpy as jnp
        import numpy as np
        N_NODES = 50000
        N_EDGES = 25000
        IN_DIM = 128
        OUT_DIM = 32
        N_HEADS = 4
        N_REL = 4
        NEG_SLOPE = 0.2
        LN_EPS = 1e-05
        key = jax.random.key(seed)
        ks = jax.random.split(key, 8)
        x = jax.random.normal(ks[0], (N_NODES, IN_DIM), dtype=jnp.float32)
        edge_index = jax.random.randint(ks[1], (2, N_EDGES), 0, N_NODES)
        edge_type = jax.random.randint(ks[2], (N_EDGES,), 0, N_REL)
        W = jax.random.normal(ks[3], (N_REL, IN_DIM, N_HEADS * OUT_DIM), dtype=jnp.float32) * 0.1
        attn_src = jax.random.normal(ks[4], (N_REL, N_HEADS, OUT_DIM), dtype=jnp.float32) * 0.1
        attn_dst = jax.random.normal(ks[5], (N_REL, N_HEADS, OUT_DIM), dtype=jnp.float32) * 0.1
        bias = jnp.zeros((N_HEADS * OUT_DIM,), dtype=jnp.float32)
        ln_gamma = jnp.ones((N_HEADS * OUT_DIM,), dtype=jnp.float32)
        ln_beta = jnp.zeros((N_HEADS * OUT_DIM,), dtype=jnp.float32)
        return {'x': x, 'edge_index': edge_index, 'edge_type': edge_type, 'W': W, 'attn_src': attn_src, 'attn_dst': attn_dst, 'bias': bias, 'ln_gamma': ln_gamma, 'ln_beta': ln_beta}
    _L3_gnn_all = _L3_gnn_setup()
    _L3_gnn_in = {k: v for k, v in _L3_gnn_all.items() if k in ('W', 'attn_src', 'attn_dst', 'bias', 'ln_gamma', 'ln_beta')}
    del _L3_gnn_all
    return {'x': x, 'src': src, 'dst': dst, 'edge_attr_3': edge_attr_3, 'edge_type_4': edge_type_4, 'L0_gnn_Wq': _L0_gnn_in['Wq'], 'L0_gnn_Wk': _L0_gnn_in['Wk'], 'L0_gnn_Wv': _L0_gnn_in['Wv'], 'L0_gnn_Wo': _L0_gnn_in['Wo'], 'L0_gnn_bo': _L0_gnn_in['bo'], 'L0_gnn_ln1_g': _L0_gnn_in['ln1_g'], 'L0_gnn_ln1_b': _L0_gnn_in['ln1_b'], 'L0_gnn_W1': _L0_gnn_in['W1'], 'L0_gnn_b1': _L0_gnn_in['b1'], 'L0_gnn_W2': _L0_gnn_in['W2'], 'L0_gnn_b2': _L0_gnn_in['b2'], 'L0_gnn_ln2_g': _L0_gnn_in['ln2_g'], 'L0_gnn_ln2_b': _L0_gnn_in['ln2_b'], 'L1_gnn_W1': _L1_gnn_in['W1'], 'L1_gnn_b1': _L1_gnn_in['b1'], 'L1_gnn_W2': _L1_gnn_in['W2'], 'L1_gnn_b2': _L1_gnn_in['b2'], 'L2_gnn_weights': _L2_gnn_in['weights'], 'L3_gnn_W': _L3_gnn_in['W'], 'L3_gnn_attn_src': _L3_gnn_in['attn_src'], 'L3_gnn_attn_dst': _L3_gnn_in['attn_dst'], 'L3_gnn_bias': _L3_gnn_in['bias'], 'L3_gnn_ln_gamma': _L3_gnn_in['ln_gamma'], 'L3_gnn_ln_beta': _L3_gnn_in['ln_beta']}

def reference(x, src, dst, edge_attr_3, edge_type_4, L0_gnn_Wq, L0_gnn_Wk, L0_gnn_Wv, L0_gnn_Wo, L0_gnn_bo, L0_gnn_ln1_g, L0_gnn_ln1_b, L0_gnn_W1, L0_gnn_b1, L0_gnn_W2, L0_gnn_b2, L0_gnn_ln2_g, L0_gnn_ln2_b, L1_gnn_W1, L1_gnn_b1, L1_gnn_W2, L1_gnn_b2, L2_gnn_weights, L3_gnn_W, L3_gnn_attn_src, L3_gnn_attn_dst, L3_gnn_bias, L3_gnn_ln_gamma, L3_gnn_ln_beta):
    import jax
    import jax.numpy as jnp

    def _L0_gnn_ref(h, src, dst, Wq, Wk, Wv, Wo, bo, ln1_g, ln1_b, W1, b1, W2, b2, ln2_g, ln2_b):
        import jax, jax.numpy as jnp
        import numpy as np
        N_NODES = 3125
        N_EDGES = 50000
        D = 128
        H = 8
        DH = D // H
        DFF = 2 * D
        EPS_LN = 1e-05

        def _ln(x, g, b):
            mu = jnp.mean(x, axis=-1, keepdims=True)
            var = jnp.var(x, axis=-1, keepdims=True)
            return (x - mu) * jax.lax.rsqrt(var + EPS_LN) * g + b
        n = h.shape[0]
        Q = (h @ Wq).reshape(n, H, DH)
        K = (h @ Wk).reshape(n, H, DH)
        V = (h @ Wv).reshape(n, H, DH)
        score = jnp.einsum('ehd,ehd->eh', K[src], Q[dst]) / np.sqrt(DH)
        score = jnp.exp(jnp.clip(score, -5.0, 5.0))
        m = V[src] * score[:, :, None]
        wV = jax.ops.segment_sum(m, dst, num_segments=n)
        z = jax.ops.segment_sum(score, dst, num_segments=n)
        h_attn = (wV / (z[:, :, None] + 1e-06)).reshape(n, D)
        x = h + (h_attn @ Wo + bo)
        x = _ln(x, ln1_g, ln1_b)
        y = jax.nn.relu(x @ W1 + b1) @ W2 + b2
        x = _ln(x + y, ln2_g, ln2_b)
        return x

    def _L1_gnn_ref(h, edge_src, edge_dst, edge_w, W1, b1, W2, b2):
        import jax, jax.numpy as jnp
        import numpy as np
        N_NODES = 50000
        N_EDGES = 25000
        IN_FEAT = 128
        INTER_DIM = 128
        OUT_FEAT = 128
        EDGE_W_DIM = 3
        n_nodes = h.shape[0]
        m = jnp.concatenate([h[edge_src], edge_w], axis=1)
        tmp = m @ W1.T + b1
        tmp = jnp.where(tmp >= 0, tmp, 0.01 * tmp)
        sums = jax.ops.segment_sum(tmp, edge_dst, num_segments=n_nodes)
        counts = jax.ops.segment_sum(jnp.ones((tmp.shape[0],), dtype=tmp.dtype), edge_dst, num_segments=n_nodes)
        h_N = sums / jnp.maximum(counts, 1.0)[:, None]
        h_total = jnp.concatenate([h, h_N], axis=1)
        return jax.nn.relu(h_total @ W2.T + b2)

    def _L2_gnn_ref(x, edge_index_with_loops, deg_inv_sqrt, num_nodes, weights):
        import jax, jax.numpy as jnp
        import numpy as np
        N_NODES = 3125
        N_EDGES = 100000
        FEAT = 128
        K = 4

        def spmm(x, edge_index, deg_inv_sqrt, num_nodes):
            src, dst = (edge_index[0], edge_index[1])
            norm = deg_inv_sqrt[src] * deg_inv_sqrt[dst]
            msg = x[src] * norm[:, None]
            return jax.ops.segment_sum(msg, dst, num_segments=num_nodes)
        Kk = weights.shape[0]
        T = [x]
        if Kk > 1:
            T.append(spmm(x, edge_index_with_loops, deg_inv_sqrt, num_nodes))
        for k in range(2, Kk):
            T.append(2.0 * spmm(T[k - 1], edge_index_with_loops, deg_inv_sqrt, num_nodes) - T[k - 2])
        Ts = jnp.stack(T, axis=0)
        return jnp.einsum('knf,kfo->no', Ts, weights)

    def _L3_gnn_ref(x, edge_index, edge_type, W, attn_src, attn_dst, bias, ln_gamma, ln_beta):
        import jax, jax.numpy as jnp
        import numpy as np
        N_NODES = 50000
        N_EDGES = 25000
        IN_DIM = 128
        OUT_DIM = 32
        N_HEADS = 4
        N_REL = 4
        NEG_SLOPE = 0.2
        LN_EPS = 1e-05
        N = x.shape[0]
        R, H, D = attn_src.shape
        src = edge_index[0]
        dst = edge_index[1]
        out = jnp.zeros((N, H * D), dtype=x.dtype)
        for r in range(R):
            mask = (edge_type == r)[:, None]
            h = (x @ W[r]).reshape(N, H, D)
            e_src = jnp.einsum('ehd,hd->eh', h[src], attn_src[r])
            e_dst = jnp.einsum('ehd,hd->eh', h[dst], attn_dst[r])
            e = jax.nn.leaky_relu(e_src + e_dst, negative_slope=NEG_SLOPE)
            e_for_max = jnp.where(mask, e, -1e+30)
            e_max = jnp.maximum(jax.ops.segment_max(e_for_max, dst, num_segments=N), 0.0)
            e_exp = jnp.where(mask, jnp.exp(e - e_max[dst]), 0.0)
            e_sum = jax.ops.segment_sum(e_exp, dst, num_segments=N)
            alpha = e_exp / (e_sum[dst] + 1e-08)
            msg = alpha[:, :, None] * h[src]
            out_rel = jax.ops.segment_sum(msg, dst, num_segments=N)
            out = out + out_rel.reshape(N, H * D)
        out = out + bias
        out = out + x
        mu = jnp.mean(out, axis=-1, keepdims=True)
        var = jnp.mean(jnp.square(out - mu), axis=-1, keepdims=True)
        out = (out - mu) * jax.lax.rsqrt(var + LN_EPS) * ln_gamma + ln_beta
        return out
    edge_index = jnp.stack([src, dst])
    deg = jnp.maximum(jax.ops.segment_sum(jnp.ones(dst.shape, jnp.float32), dst, num_segments=3125), 1.0)
    deg_isqrt = deg ** (-0.5)
    h = jnp.maximum(_layernorm(x, axis=-1), 0.0)
    x = x + _L0_gnn_ref(h, src, dst, L0_gnn_Wq, L0_gnn_Wk, L0_gnn_Wv, L0_gnn_Wo, L0_gnn_bo, L0_gnn_ln1_g, L0_gnn_ln1_b, L0_gnn_W1, L0_gnn_b1, L0_gnn_W2, L0_gnn_b2, L0_gnn_ln2_g, L0_gnn_ln2_b)
    h = jnp.maximum(_layernorm(x, axis=-1), 0.0)
    x = x + _L1_gnn_ref(h, src, dst, edge_attr_3, L1_gnn_W1, L1_gnn_b1, L1_gnn_W2, L1_gnn_b2)
    h = jnp.maximum(_layernorm(x, axis=-1), 0.0)
    x = x + _L2_gnn_ref(h, edge_index, deg_isqrt, 3125, L2_gnn_weights)
    h = jnp.maximum(_layernorm(x, axis=-1), 0.0)
    x = x + _L3_gnn_ref(h, edge_index, edge_type_4, L3_gnn_W, L3_gnn_attn_src, L3_gnn_attn_dst, L3_gnn_bias, L3_gnn_ln_gamma, L3_gnn_ln_beta)
    return x

_drawn_inputs = setup_inputs


def setup_inputs(seed=0):
    import zlib

    import numpy as np

    out = dict(_drawn_inputs(seed))
    spreads = {'L0_gnn_bo': (0.0, 0.1),
     'L0_gnn_ln1_g': (1.0, 0.2),
     'L0_gnn_ln1_b': (0.0, 0.1),
     'L0_gnn_b1': (0.0, 0.278),
     'L0_gnn_b2': (0.0, 0.1),
     'L0_gnn_ln2_g': (1.0, 0.2),
     'L0_gnn_ln2_b': (0.0, 0.1),
     'L1_gnn_b1': (0.0, 0.425),
     'L1_gnn_b2': (0.0, 0.1),
     'L3_gnn_bias': (0.0, 0.299),
     'L3_gnn_ln_gamma': (1.0, 0.2),
     'L3_gnn_ln_beta': (0.0, 0.1)}
    factors = {'edge_attr_3': 4.076, 'L3_gnn_attn_dst': 9.102}
    for name, (base, spread) in spreads.items():
        noise = np.random.default_rng([zlib.crc32(name.encode()), seed]).standard_normal(out[name].shape)
        drawn = base * np.exp(spread * noise) if base else spread * noise
        out[name] = jnp.asarray(drawn.astype(out[name].dtype))
    for name, factor in factors.items():
        out[name] = (out[name] * factor).astype(out[name].dtype)
    return out
```

```python
import numpy as np
from contextlib import ExitStack
import concourse.bass as bass
from concourse import mybir

F32, I32 = mybir.dt.float32, mybir.dt.int32
ALU, ACT, AX = mybir.AluOpType, mybir.ActivationFunctionType, mybir.AxisListType

P = 128
N = 3125
NB = -(-N // P)
NP = NB * P
NX = NP + P
E = 53125
G = 8
W = 96
M = -(-E // (2 * G * P)) * 2
T = M * G
EP = T * P
Q_MAX = -(-N // W)
H0 = 8
Z0 = H0 + 1
R, H3 = 4, 4
RH = R * H3
GN = 8
GW = 3
NG = NX // GN
GQ_MAX = -(-(-(-N // GN)) // GW)
GX = NG + GW * GQ_MAX + GW
FAR = 1 << 20
CHUNK = 512
EPS = 1e-5


def done(step):
    return step + 3


def prev_done(step):
    return step + 2


def free(step):
    return step + 1


def bc(ap, axis, shape):
    return ap.unsqueeze(axis).to_broadcast(shape)


def chunks():
    return [(lo, min(CHUNK, NP - lo)) for lo in range(0, NP, CHUNK)]


def chain(engine, semaphore):
    n = [0]

    def link(instruction):
        n[0] += 1
        instruction.then_inc(semaphore, 1)
        engine.wait_ge(semaphore, n[0])
    return link


class Names:
    pass


class Memory:

    def __init__(self, nc):
        self.nc, self.stack = nc, ExitStack()
        self.stage = f"{nc.next_id()}"

    def __enter__(self):
        return self

    def __exit__(self, *error):
        return self.stack.__exit__(*error)

    def sb(self, name, shape, dtype=F32):
        return self.stack.enter_context(self.nc.sbuf_tensor(f"{name}_{self.stage}", shape, dtype))

    def two(self, name, shape, dtype=F32):
        return [self.sb(f"{name}{k}", shape, dtype) for k in range(2)]

    def ps(self, name, shape=(P, CHUNK)):
        return self.stack.enter_context(self.nc.psum_tensor(f"{name}_{self.stage}", list(shape), F32))

    def sem(self, name):
        return self.nc.alloc_semaphore(f"{name}_{self.stage}")

    def block(self):
        return self.stack.enter_context(self.nc.Block())


def prepare(nc, d, r):
    with Memory(nc) as mem:
        macro_dst = mem.sb("macro_dst", [M, G * P], I32)
        tile_dst = mem.sb("tile_dst", [T // 4, 4, P], I32)
        macro_f = mem.sb("macro_f", [M, 2])
        macro_i = mem.sb("macro_i", [M, 2], I32)
        tile_f = mem.sb("tile_f", [T // 4, 4, 2])
        tile_i = mem.sb("tile_i", [T // 4, 4, 2], I32)
        macro_row = mem.sb("macro_row", [P, M, 2], I32)
        tile_row = mem.sb("tile_row", [P, T, 2], I32)
        macro_rf = mem.sb("macro_rf", [P, M, 2])
        tile_rf = mem.sb("tile_rf", [P, T, 2])
        span = mem.sb("span", [P, M])
        gspan = mem.sb("gspan", [P, T])
        widest = mem.sb("widest", [P, 2])
        steps = mem.sb("steps", [P, Q_MAX])
        gsteps = mem.sb("gsteps", [P, GQ_MAX])
        count = mem.sb("count", [P, 2])
        dst_f = mem.sb("dst_f", [P, T])
        src_f = mem.sb("src_f", [P, T])
        type_f = mem.sb("type_f", [P, T])
        dst_i = mem.sb("dst_i", [P, T], I32)
        src_i = mem.sb("src_i", [P, T], I32)
        type_i = mem.sb("type_i", [P, T], I32)
        key_i = mem.sb("key_i", [P, T], I32)
        base_f = mem.sb("base_f", [1, Q_MAX, M])
        iota_p = mem.sb("iota_p", [P, P])
        iota_q = mem.sb("iota_q", [P, 1])
        zero = mem.sb("zero", [P, P])
        loaded, order, extremes, stored, back, iotas, key_done, zero_done = map(
            mem.sem, ("loaded", "order", "extremes", "stored", "back", "iotas", "key_done", "zero_done"))
        block = mem.block()

        @block.sync
        def _(sp):
            sp.dma_start(macro_dst[:, :], d["dst_sorted"].rearrange("(m e) -> m e", m=M)).then_inc(loaded, 16)
            sp.dma_start(tile_dst[:, :, :], d["dst_sorted"].rearrange("(a b e) -> a b e", b=4, e=P)).then_inc(loaded, 16)
            sp.dma_start(dst_i[:, :], d["dst"]).then_inc(loaded, 16)
            sp.dma_start(src_i[:, :], d["src"]).then_inc(loaded, 16)
            sp.dma_start(type_i[:, :], d["edge_type"]).then_inc(loaded, 16)
            sp.dma_start(r.x[:, :, :], d["x"]).then_inc(loaded, 16)
            sp.wait_ge(zero_done, 1)
            for table in (d["q_table"], d["ed_table"][:, :], d["rs_table"][:, :]):
                width = table.shape[1]
                sp.dma_start(table[NP:NX, :], zero[:, 0:width]).then_inc(stored, 16)
            sp.wait_ge(extremes, 1)
            sp.dma_start(d["macro_bounds"].rearrange("(m k) -> m k", k=2), macro_i[:, :]).then_inc(stored, 16)
            sp.dma_start(d["tile_bounds"].rearrange("(a b) -> a b", b=8), tile_i[:, :, :].rearrange("a b k -> a (b k)")).then_inc(stored, 16)
            sp.wait_ge(stored, 80)
            sp.dma_start(macro_row[:, :, :].rearrange("p m k -> p (m k)"), d["macro_bounds"].partition_broadcast(P)).then_inc(back, 16)
            sp.dma_start(tile_row[:, :, :].rearrange("p t k -> p (t k)"), d["tile_bounds"].partition_broadcast(P)).then_inc(back, 16)
            sp.wait_ge(key_done, 1)
            sp.dma_start(d["key"], key_i[:, :]).then_inc(stored, 16)
            sp.wait_ge(stored, 96)

        @block.gpsimd
        def _(pool):
            for out, step in ((r.iota_w[:, :], 1), (r.iota_g[:, :], 1), (steps[:, :], W), (gsteps[:, :], GW),
                              (r.iota_r[:, :], 1), (iota_p[:, :], 1)):
                pool.iota(out, [[step, out.shape[1]]], base=0, channel_multiplier=0,
                          allow_small_or_imprecise_dtypes=True).then_inc(iotas, 1)
            pool.iota(iota_q[:, :], [[0, 1]], base=0, channel_multiplier=1,
                      allow_small_or_imprecise_dtypes=True).then_inc(iotas, 1)

        @block.vector
        def _(dve):
            link = chain(dve, order)
            link(dve.memset(zero[:, :], 0.0))
            dve.sem_inc(zero_done, 1)
            dve.wait_ge(loaded, 96)
            dve.tensor_reduce(macro_f[:, 0:1], macro_dst[:, :], AX.X, ALU.min)
            dve.tensor_reduce(macro_f[:, 1:2], macro_dst[:, :], AX.X, ALU.max)
            dve.tensor_reduce(tile_f[:, :, 0], tile_dst[:, :, :], AX.X, ALU.min)
            link(dve.tensor_reduce(tile_f[:, :, 1], tile_dst[:, :, :], AX.X, ALU.max))
            dve.tensor_copy(macro_i[:, :], macro_f[:, :])
            link(dve.tensor_copy(tile_i[:, :, :], tile_f[:, :, :]))
            link(dve.tensor_scalar(tile_i[:, :, :], tile_i[:, :, :], 3, None, ALU.arith_shift_right))
            dve.sem_inc(extremes, 1)
            dve.tensor_copy(src_f[:, :], src_i[:, :])
            dve.tensor_copy(dst_f[:, :], dst_i[:, :])
            link(dve.tensor_copy(type_f[:, :], type_i[:, :]))
            link(dve.scalar_tensor_tensor(src_f[:, :], type_f[:, :], float(NP), src_f[:, :], ALU.mult, ALU.add))
            link(dve.tensor_copy(key_i[:, :], src_f[:, :]))
            dve.sem_inc(key_done, 1)
            dve.wait_ge(iotas, 7)
            dve.tensor_tensor(r.type_hot[:, :, :], bc(type_f[:, :], 2, [P, T, R]), bc(r.iota_r[:, :], 1, [P, T, R]), ALU.is_equal)
            dve.tensor_scalar(r.ident[:, :], iota_p[:, :], iota_q[:, :], None, ALU.is_equal)
            dve.wait_ge(back, 32)
            dve.tensor_copy(macro_rf[:, :, :], macro_row[:, :, :])
            dve.tensor_copy(r.tile_group[:, :], tile_row[0:1, :, 0])
            link(dve.tensor_copy(tile_rf[:, :, :], tile_row[:, :, :]))
            dve.tensor_tensor(r.rel[:, :, :], dst_f[:, :].rearrange("p (m g) -> p m g", g=G),
                              bc(macro_rf[:, :, 0], 2, [P, M, G]), ALU.subtract)
            dve.scalar_tensor_tensor(r.group_rel[:, :], tile_rf[:, :, 0], -float(GN), dst_f[:, :], ALU.mult, ALU.add)
            dve.tensor_tensor(span[:, :], macro_rf[:, :, 1], macro_rf[:, :, 0], ALU.subtract)
            link(dve.tensor_tensor(gspan[:, :], tile_rf[:, :, 1], tile_rf[:, :, 0], ALU.subtract))
            dve.tensor_reduce(widest[:, 0:1], span[:, :], AX.X, ALU.max)
            link(dve.tensor_reduce(widest[:, 1:2], gspan[:, :], AX.X, ALU.max))
            dve.tensor_scalar(steps[:, :], steps[:, :], widest[:, 0:1], None, ALU.is_le)
            link(dve.tensor_scalar(gsteps[:, :], gsteps[:, :], widest[:, 1:2], None, ALU.is_le))
            dve.tensor_reduce(count[:, 0:1], steps[:, :], AX.X, ALU.add)
            link(dve.tensor_reduce(count[:, 1:2], gsteps[:, :], AX.X, ALU.add))
            dve.tensor_copy(r.passes[:, :], count[:, :])
            for q in range(Q_MAX):
                last = dve.tensor_scalar(base_f[:, q, :], macro_rf[0:1, :, 0], float(q * W), float(NP), ALU.add, ALU.min)
            link(last)
            link(dve.tensor_copy(r.base[:, :], base_f[:, :, :].rearrange("o q m -> o (q m)")))


def normalise(nc, r, src, out, relu=False, weight=None, shift=None, residual=None, load=()):
    with Memory(nc) as mem:
        centred, square = mem.sb("centred", [P, NB, P]), mem.sb("square", [P, NB, P])
        stat, root, inv = mem.sb("stat", [P, NB]), mem.sb("root", [P, NB]), mem.sb("inv", [P, NB])
        order, var_done, root_done, loaded = map(mem.sem, ("order", "var_done", "root_done", "loaded"))
        block = mem.block()
        shape = [P, NB, P]

        @block.sync
        def _(sp):
            for to, of in load:
                sp.dma_start(to, of).then_inc(loaded, 16)
            if load:
                sp.wait_ge(loaded, 16 * len(load))

        @block.vector
        def _(dve):
            link = chain(dve, order)
            link(dve.tensor_reduce(stat[:, :], src, AX.X, ALU.add))
            link(dve.tensor_scalar(stat[:, :], stat[:, :], 1.0 / P, None, ALU.mult))
            link(dve.tensor_tensor(centred[:, :, :], src, bc(stat[:, :], 2, shape), ALU.subtract))
            link(dve.tensor_tensor(square[:, :, :], centred[:, :, :], centred[:, :, :], ALU.mult))
            link(dve.tensor_reduce(stat[:, :], square[:, :, :], AX.X, ALU.add))
            link(dve.tensor_scalar(stat[:, :], stat[:, :], 1.0 / P, EPS, ALU.mult, ALU.add))
            dve.sem_inc(var_done, 1)
            dve.wait_ge(root_done, 1)
            link(dve.reciprocal(inv[:, :], root[:, :]))
            if relu:
                link(dve.tensor_tensor(square[:, :, :], centred[:, :, :], bc(inv[:, :], 2, shape), ALU.mult))
                link(dve.tensor_scalar(out, square[:, :, :], 0.0, None, ALU.max))
                return
            link(dve.tensor_tensor(square[:, :, :], centred[:, :, :], bc(inv[:, :], 2, shape), ALU.mult))
            if load:
                dve.wait_ge(loaded, 16 * len(load))
            link(dve.tensor_tensor(centred[:, :, :], square[:, :, :], bc(weight, 1, shape), ALU.mult))
            link(dve.tensor_tensor(out if residual is None else square[:, :, :], centred[:, :, :], bc(shift, 1, shape), ALU.add))
            if residual is not None:
                link(dve.tensor_tensor(residual, residual, square[:, :, :], ALU.add))

        @block.scalar
        def _(act):
            act.wait_ge(var_done, 1)
            act.activation(root[:, :], stat[:, :], ACT.Sqrt).then_inc(root_done, 1)


def turn(nc, r, src, out, scale=None, back=False, store=None):
    groups = [(b, min(4, NB - b)) for b in range(0, NB, 4)]
    with Memory(nc) as mem:
        scaled = mem.sb("scaled", [P, NP]) if scale is not None else None
        ps = [mem.ps(f"turned{k}") for k in range(2)]
        scale_done, turned, copied, stored = map(mem.sem, ("scale_done", "turned", "copied", "stored"))
        block = mem.block()
        source = scaled[:, :] if scale is not None else src
        if len(source.shape) == 3:
            source = source.rearrange("p b f -> p (b f)")
        if len(out.shape) == 3:
            out = out.rearrange("p b f -> p (b f)")

        @block.tensor
        def _(pe):
            for n, (b, width) in enumerate(groups):
                if scale is not None:
                    pe.wait_ge(scale_done, n + 1)
                if n >= 2:
                    pe.wait_ge(copied, n - 1)
                for j in range(width):
                    last = pe.transpose(ps[n % 2][:, j * P:(j + 1) * P], source[:, (b + j) * P:(b + j + 1) * P], r.ident[:, :])
                last.then_inc(turned, 1)

        @block.scalar
        def _(act):
            for n, (b, width) in enumerate(groups):
                act.wait_ge(turned, n + 1)
                act.activation(out[:, b * P:(b + width) * P], ps[n % 2][:, 0:width * P], ACT.Copy).then_inc(copied, 1)

        @block.vector
        def _(dve):
            if scale is not None:
                for b, width in groups:
                    part = slice(b * P, (b + width) * P)
                    dve.tensor_tensor(scaled[:, part], src[:, part], scale[:, part], ALU.mult).then_inc(scale_done, 1)

        @block.sync
        def _(sp):
            if store is not None:
                for n, (b, width) in enumerate(groups):
                    sp.wait_ge(copied, n + 1)
                    sp.dma_start(store[b * P:(b + width) * P, :].rearrange("(b p) f -> p b f", p=P),
                                 out[:, b * P:(b + width) * P].rearrange("p (b f) -> p b f", f=P)).then_inc(stored, 16)
                sp.wait_ge(stored, 16 * len(groups))


def project(nc, left, right, out, load=(), add=None, stores=()):
    width = right[0].shape[1]
    with Memory(nc) as mem:
        ps = [mem.ps(f"product{k}") for k in range(4)]
        loaded, multiplied, copied, stored = map(mem.sem, ("loaded", "multiplied", "copied", "stored"))
        block = mem.block()

        @block.sync
        def _(sp):
            for to, of in load:
                sp.dma_start(to, of).then_inc(loaded, 16)
            n = 0
            for b0 in range(0, NB, 5):
                sp.wait_ge(copied, b0 + 5)
                for to, of in stores:
                    sp.dma_start(to(b0, b0 + 5), of(b0, b0 + 5)).then_inc(stored, 16)
                    n += 1
            if n:
                sp.wait_ge(stored, 16 * n)

        @block.tensor
        def _(pe):
            if load:
                pe.wait_ge(loaded, 16 * len(load))
            for b in range(NB):
                if b >= 4:
                    pe.wait_ge(copied, b - 3)
                for n, (lhs, rhs) in enumerate(zip(left, right)):
                    last = pe.matmul(ps[b % 4][:, 0:width], lhs[:, b * P:(b + 1) * P], rhs, start=n == 0, stop=n == len(left) - 1)
                last.then_inc(multiplied, 1)

        @block.vector
        def _(dve):
            if load:
                dve.wait_ge(loaded, 16 * len(load))
            for b in range(NB):
                dve.wait_ge(multiplied, b + 1)
                if add is None:
                    dve.tensor_copy(out[:, b, :], ps[b % 4][:, 0:width]).then_inc(copied, 1)
                else:
                    dve.tensor_tensor(out[:, b, :], ps[b % 4][:, 0:width], add(b), ALU.add).then_inc(copied, 1)


def rows_of(table):
    return lambda lo, hi: table[lo * P:hi * P, :].rearrange("(b p) f -> p b f", p=P)


def edge_buffers(mem, r, name, transposed):
    b = Names()
    b.hot = mem.two("hot", [P, G, W])
    b.hot_done, b.seg_done, b.acc_done = map(mem.sem, ("hot_done", "seg_done", "acc_done"))
    if transposed:
        b.hot_t = mem.two("hot_t", [W, G * P])
        b.turn_done, b.copy_done, b.look_done = map(mem.sem, ("turn_done", "copy_done", "look_done"))
        b.win_in = [mem.sem(f"win_in{k}") for k in range(2)]
        b.ps_t = mem.ps("ps_t", [W, G * P])
    return b


def make_hot(dve, r, b, m, k, step):
    dve.wait_ge(b.seg_done, free(step))
    rel = r.rel[:, bass.ds(m, 1), :].rearrange("p o g -> p (o g)")
    dve.tensor_tensor(b.hot[k][:, :, :], bc(r.window[:, :], 1, [P, G, W]), bc(rel, 2, [P, G, W]),
                      ALU.is_equal).then_inc(b.hot_done, 1)


def turn_hot(pe, r, b, k, step):
    pe.wait_ge(b.hot_done, done(step))
    pe.wait_ge(b.copy_done, prev_done(step))
    for j in range(G):
        last = pe.transpose(b.ps_t[:, j * P:(j + 1) * P], b.hot[k][:, j, :], r.ident[:, :])
    last.then_inc(b.turn_done, 1)


def copy_hot(act, b, k, step):
    act.wait_ge(b.turn_done, done(step))
    act.wait_ge(b.look_done, free(step))
    act.activation(b.hot_t[k][:, :], b.ps_t[:, :], ACT.Copy).then_inc(b.copy_done, 1)


def load_window(sp, r, b, table, to, m, k, step):
    base = sp.value_load(r.base[0:1, bass.ds(step, 1)], min_val=0, max_val=NP)
    sp.wait_ge(b.look_done, free(step))
    sp.dma_start(to[k], table[bass.ds(base, W), :]).then_inc(b.win_in[k], 16)


def passes_loop(engine, r, credits, stages, each_pass=None):
    count = engine.value_load(r.passes[0:1, 0:1], min_val=1, max_val=Q_MAX)
    for semaphore in credits:
        engine.sem_inc(semaphore, 2)
    lags = [lag for lag, _ in stages]
    with engine.Fori(0, count) as q:
        def tick(t, k, i):
            for lag, stage in stages:
                if i is None:
                    m = t - lag
                    if 0 <= m < M:
                        stage(m, m % 2, q * (M // 2) + m // 2, q * M + m)
                else:
                    m, par = i * 2 + (k - lag), (k - lag) % 2
                    stage(m, par, q * (M // 2) + i + (k - lag - par) // 2, q * M + m)
        tick(0, 0, None)
        tick(1, 1, None)
        with engine.Fori(1, M // 2) as i:
            for k in range(2):
                tick(None, k, i)
        if max(lags):
            tick(M, 0, None)
            tick(M + 1, 1, None)
        if each_pass is not None:
            each_pass(q)


def gather_rows(pool, rows, table, idx, rows_in, ticket):
    pool.sem_inc(ticket, 1)
    for j in range(G):
        pool.indirect_dma_start(rows[:, j, :], None, table, bass.IndirectOffsetOnAxis(idx[:, j:j + 1], 0)).then_inc(rows_in, 16)


def move_window(dve, r, moved, q):
    dve.tensor_scalar(r.window[:, :], r.window[:, :], float(W), None, ALU.add).then_inc(moved, 1)
    dve.wait_ge(moved, q + 2)


def start_window(dve, r, moved):
    dve.tensor_copy(r.window[:, :], r.iota_w[:, :]).then_inc(moved, 1)
    dve.wait_ge(moved, 1)


def attention_edges(nc, d, r):
    with Memory(nc) as mem:
        b = edge_buffers(mem, r, "l0", True)
        idx = mem.two("idx", [P, G], I32)
        kv = mem.two("kv", [P, G, 2 * P])
        q_win = mem.two("q_win", [W, P])
        prod = mem.sb("prod", [P, G * H0, P // H0])
        score = mem.sb("score", [P, G, H0])
        clipped = mem.two("clipped", [P, G, H0])
        weight = mem.two("weight", [P, G, Z0])
        msg = mem.two("msg", [P, G, P])
        ps_q = mem.ps("ps_q", [P, G * P])
        ps_s = [mem.ps(f"ps_s{k}") for k in range(2)]
        ps_z = [mem.ps(f"ps_z{k}") for k in range(2)]
        idx_in = [mem.sem(f"idx_in{k}") for k in range(2)]
        rows_in = [mem.sem(f"rows_in{k}") for k in range(2)]
        prod_done, sum_done, clip_done, exp_done, msg_done, ticket, moved, ones_set, cleared = map(
            mem.sem, ("prod_done", "sum_done", "clip_done", "exp_done", "msg_done", "ticket", "moved", "ones_set", "cleared"))
        block = mem.block()

        @block.sync
        def _(sp):
            def load(m, k, pair, step):
                sp.wait_ge(prod_done, free(step))
                sp.dma_start(idx[k][:, :], d["src"][:, bass.ds(m * G, G)]).then_inc(idx_in[k], 16)
                load_window(sp, r, b, d["q_table"], [w[:, :] for w in q_win], m, k, step)
            passes_loop(sp, r, (), [(0, load)])

        @block.gpsimd
        def _(pool):
            def gather(m, k, pair, step):
                pool.wait_ge(idx_in[k], pair * 16 + 16)
                pool.wait_ge(msg_done, free(step))
                gather_rows(pool, kv[k], d["kv_table"], idx[k], rows_in[k], ticket)
            passes_loop(pool, r, (), [(0, gather)])

        @block.vector
        def _(dve):
            for k in range(2):
                dve.memset(weight[k][:, :, H0:Z0], 1.0).then_inc(ones_set, 1)
            dve.memset(r.acc[:, :], 0.0).then_inc(cleared, 1)
            dve.memset(r.z[:, :], 0.0).then_inc(cleared, 1)
            dve.wait_ge(cleared, 2)
            start_window(dve, r, moved)

            def hot(m, k, pair, step):
                make_hot(dve, r, b, m, k, step)

            def messages(m, k, pair, step):
                dve.wait_ge(b.look_done, done(step))
                dve.wait_ge(rows_in[k], (pair * 16 + 16) * G)
                dve.tensor_tensor(prod[:, :, :], kv[k][:, :, 0:P].rearrange("p g (h c) -> p g h c", h=H0),
                                  ps_q[:, :].rearrange("p (g h c) -> p g h c", g=G, h=H0), ALU.mult).then_inc(prod_done, 1)
                dve.wait_ge(prod_done, done(step))
                dve.tensor_reduce(score[:, :, :].rearrange("p g h -> p (g h)"), prod[:, :, :], AX.X, ALU.add).then_inc(sum_done, 1)
                dve.wait_ge(sum_done, done(step))
                dve.tensor_scalar(clipped[k][:, :, :], score[:, :, :], 20.0, -20.0, ALU.min, ALU.max).then_inc(clip_done, 1)
                dve.wait_ge(exp_done, done(step))
                dve.tensor_tensor(msg[k][:, :, :].rearrange("p g (h c) -> p g h c", h=H0),
                                  kv[k][:, :, P:2 * P].rearrange("p g (h c) -> p g h c", h=H0),
                                  weight[k][:, :, 0:H0].unsqueeze(3).to_broadcast([P, G, H0, P // H0]), ALU.mult).then_inc(msg_done, 1)

            def accumulate(m, k, pair, step):
                base = dve.value_load(r.base[0:1, bass.ds(step, 1)], min_val=0, max_val=NP)
                dve.wait_ge(b.seg_done, done(step))
                dve.wait_ge(b.acc_done, prev_done(step))
                z = r.z[0:Z0, bass.ds(base, W)]
                dve.tensor_tensor(z, z, ps_z[k][0:Z0, 0:W], ALU.add)
                a = r.acc[:, bass.ds(base, W)]
                dve.tensor_tensor(a, a, ps_s[k][:, 0:W], ALU.add).then_inc(b.acc_done, 1)
            passes_loop(dve, r, (b.hot_done, prod_done, sum_done, clip_done, msg_done, b.acc_done),
                        [(0, hot), (1, messages), (2, accumulate)], lambda q: move_window(dve, r, moved, q))

        @block.scalar
        def _(act):
            act.wait_ge(ones_set, 2)

            def copy(m, k, pair, step):
                copy_hot(act, b, k, step)

            def exps(m, k, pair, step):
                act.wait_ge(clip_done, done(step))
                act.wait_ge(b.seg_done, free(step))
                act.activation(weight[k][:, :, 0:H0], clipped[k][:, :, :], ACT.Exp, scale=0.25).then_inc(exp_done, 1)
            passes_loop(act, r, (b.copy_done, exp_done), [(0, copy), (1, exps)])

        @block.tensor
        def _(pe):
            def turn_and_look(m, k, pair, step):
                turn_hot(pe, r, b, k, step)
                pe.wait_ge(b.copy_done, done(step))
                pe.wait_ge(b.win_in[k], pair * 16 + 16)
                pe.wait_ge(prod_done, prev_done(step))
                for j in range(G):
                    last = pe.matmul(ps_q[:, j * P:(j + 1) * P], b.hot_t[k][:, j * P:(j + 1) * P], q_win[k][:, :], start=True, stop=True)
                last.then_inc(b.look_done, 1)

            def sums(m, k, pair, step):
                pe.wait_ge(msg_done, done(step))
                pe.wait_ge(b.acc_done, free(step))
                for j in range(G):
                    pe.matmul(ps_s[k][:, 0:W], msg[k][:, j, :], b.hot[k][:, j, :], start=j == 0, stop=j == G - 1)
                for j in range(G):
                    last = pe.matmul(ps_z[k][0:Z0, 0:W], weight[k][:, j, :], b.hot[k][:, j, :], start=j == 0, stop=j == G - 1)
                last.then_inc(b.seg_done, 1)
            passes_loop(pe, r, (b.turn_done, b.look_done, b.seg_done), [(0, turn_and_look), (1, sums)])


def attention_nodes(nc, d, r, mem0):
    with Memory(nc) as mem:
        head_rows, count_rows = mem.sb("head_rows", [Z0, P]), mem.sb("count_rows", [Z0, P])
        inv = mem.two("inv", [P, CHUNK])
        cnt = mem.two("cnt", [P, CHUNK])
        ps_h = [mem.ps(f"ps_h{k}") for k in range(2)]
        ps_c = [mem.ps(f"ps_c{k}") for k in range(2)]
        made, multiplied, order, inv_done, root_done = map(mem.sem, ("made", "multiplied", "order", "inv_done", "root_done"))
        block = mem.block()

        @block.gpsimd
        def _(pool):
            pool.memset(head_rows[:, :], 1.0).then_inc(made, 1)
            pool.memset(count_rows[:, :], 1.0).then_inc(made, 1)
            pool.wait_ge(made, 2)
            pool.affine_select(out=head_rows[:, :], in_=head_rows[:, :], compare_op=ALU.is_ge, fill=0.0, base=0,
                               pattern=[[1, P]], channel_multiplier=-(P // H0)).then_inc(made, 1)
            pool.wait_ge(made, 3)
            pool.affine_select(out=head_rows[:, :], in_=head_rows[:, :], compare_op=ALU.is_ge, fill=0.0, base=P // H0 - 1,
                               pattern=[[-1, P]], channel_multiplier=P // H0).then_inc(made, 1)
            pool.affine_select(out=count_rows[:, :], in_=count_rows[:, :], compare_op=ALU.is_ge, fill=0.0, base=-H0,
                               pattern=[[0, P]], channel_multiplier=1).then_inc(made, 1)

        @block.tensor
        def _(pe):
            pe.wait_ge(made, 5)
            for n, (lo, width) in enumerate(chunks()):
                if n >= 2:
                    pe.wait_ge(inv_done, n - 1)
                pe.matmul(ps_h[n % 2][:, 0:width], head_rows[:, :], r.z[0:Z0, lo:lo + width], start=True, stop=True)
                pe.matmul(ps_c[n % 2][:, 0:width], count_rows[:, :], r.z[0:Z0, lo:lo + width], start=True, stop=True).then_inc(multiplied, 1)

        @block.vector
        def _(dve):
            link = chain(dve, order)
            for n, (lo, width) in enumerate(chunks()):
                k, part = n % 2, slice(lo, lo + width)
                dve.wait_ge(multiplied, n + 1)
                dve.tensor_scalar(cnt[k][:, 0:width], ps_c[k][:, 0:width], 1.0, None, ALU.max)
                link(dve.tensor_scalar(inv[k][:, 0:width], ps_h[k][:, 0:width], 1e-6, None, ALU.add))
                dve.sem_inc(inv_done, 1)
                link(dve.reciprocal(inv[k][:, 0:width], inv[k][:, 0:width]))
                dve.tensor_tensor(r.attn[:, part], r.acc[:, part], inv[k][:, 0:width], ALU.mult)
                link(dve.reciprocal(r.inv_count[:, part], cnt[k][:, 0:width]))
            dve.sem_inc(root_done, 1)

        @block.scalar
        def _(act):
            act.wait_ge(root_done, 1)
            act.activation(r.root_count[:, :], r.inv_count[:, :], ACT.Sqrt)


def hidden(nc, r, src, weights, bias, out):
    with Memory(nc) as mem:
        ps = [mem.ps(f"ps{k}") for k in range(4)]
        multiplied, copied = map(mem.sem, ("multiplied", "copied"))
        block = mem.block()
        parts = [(half, lo, width) for lo, width in chunks() for half in range(2)]

        @block.tensor
        def _(pe):
            for n, (half, lo, width) in enumerate(parts):
                if n >= 4:
                    pe.wait_ge(copied, n - 3)
                pe.matmul(ps[n % 4][:, 0:width], weights[:, half * P:(half + 1) * P], src[:, lo:lo + width], start=True, stop=True).then_inc(multiplied, 1)

        @block.scalar
        def _(act):
            for n, (half, lo, width) in enumerate(parts):
                act.wait_ge(multiplied, n + 1)
                act.activation(out[half][:, lo:lo + width], ps[n % 4][:, 0:width], ACT.Relu, bias=bias[:, half:half + 1]).then_inc(copied, 1)


def attention_layer(nc, d, r):
    with Memory(nc) as mem:
        w = mem.sb("w_qkv", [P, 3 * P])
        out = mem.sb("kvq", [P, NB, 3 * P])
        project(nc, [r.ht], [w[:, :]], out, load=[(w[:, 0:P], d["l0_wk"]), (w[:, P:2 * P], d["l0_wv"]), (w[:, 2 * P:3 * P], d["l0_wq"])],
                stores=[(rows_of(d["kv_table"]), lambda lo, hi: out[:, lo:hi, 0:2 * P]),
                        (rows_of(d["q_table"]), lambda lo, hi: out[:, lo:hi, 2 * P:3 * P])])
    attention_edges(nc, d, r)
    with Memory(nc) as mem:
        r.attn = mem.sb("attn", [P, NP])
        attention_nodes(nc, d, r, mem)
        w_o, x1, sums = mem.sb("w_o", [P, P]), mem.sb("x1", [P, NB, P]), None
        rows = mem.sb("rows", [P, 6, P])
        w_1, w_2, bias = mem.sb("w_1", [P, 2 * P]), mem.sb("w_2", [P, 2, P]), mem.sb("bias", [P, 2])
        ready = mem.sem("ready")
        load = [(rows[:, n, :], v.partition_broadcast(P)) for n, v in
                enumerate((d["l0_bo"], d["l0_ln1_g"], d["l0_ln1_b"], d["l0_b2"], d["l0_ln2_g"], d["l0_ln2_b"]))]
        load += [(w_o[:, :], d["l0_wo"]), (w_1[:, :], d["l0_w1"]), (w_2[:, :, :], d["l0_w2"]), (bias[:, :], d["l0_b1"])]
        add_rows(nc, r.h, rows[:, 0, :], load)
        project(nc, [r.attn], [w_o[:, :]], x1, add=lambda b: r.h[:, b, :])
        normalise(nc, r, x1[:, :, :], x1[:, :, :], weight=rows[:, 1, :], shift=rows[:, 2, :])
        turn(nc, r, x1[:, :, :], r.ht[:, :])
        hid = mem.two("hid", [P, NP])
        hidden(nc, r, r.ht, w_1, bias, hid)
        add_rows(nc, x1, rows[:, 3, :])
        project(nc, hid, [w_2[:, 0, :], w_2[:, 1, :]], x1, add=lambda b: x1[:, b, :])
        normalise(nc, r, x1[:, :, :], None, weight=rows[:, 4, :], shift=rows[:, 5, :], residual=r.x[:, :, :])


def add_rows(nc, to, row, load=()):
    with Memory(nc) as mem:
        loaded = mem.sem("loaded")
        added = mem.sem("added")
        block = mem.block()

        @block.sync
        def _(sp):
            for out, of in load:
                sp.dma_start(out, of).then_inc(loaded, 16)
            if load:
                sp.wait_ge(loaded, 16 * len(load))

        @block.vector
        def _(dve):
            if load:
                dve.wait_ge(loaded, 16 * len(load))
            dve.tensor_tensor(to[:, :, :], to[:, :, :], bc(row, 1, [P, NB, P]), ALU.add).then_inc(added, 1)
            dve.wait_ge(added, 1)


def mean_edges(nc, d, r, w_e):
    with Memory(nc) as mem:
        b = edge_buffers(mem, r, "l1", False)
        idx = mem.two("idx", [P, G], I32)
        rows = mem.two("rows", [P, G, P])
        attr = mem.two("attr", [3, G * P])
        pre = mem.two("pre", [P, G, P])
        msg = mem.two("msg", [P, G, P])
        ps_e = [mem.ps(f"ps_e{k}", [P, G * P]) for k in range(2)]
        ps_s = [mem.ps(f"ps_s{k}") for k in range(2)]
        idx_in = [mem.sem(f"idx_in{k}") for k in range(2)]
        rows_in = [mem.sem(f"rows_in{k}") for k in range(2)]
        attr_in = [mem.sem(f"attr_in{k}") for k in range(2)]
        edge_done, pre_done, msg_done, ticket, moved, cleared = map(
            mem.sem, ("edge_done", "pre_done", "msg_done", "ticket", "moved", "cleared"))
        block = mem.block()

        @block.sync
        def _(sp):
            def load(m, k, pair, step):
                sp.wait_ge(edge_done, free(step))
                sp.dma_start(idx[k][:, :], d["src"][:, bass.ds(m * G, G)]).then_inc(idx_in[k], 16)
                sp.dma_start(attr[k][:, :], d["edge_attr"][:, bass.ds(m * (G * P), G * P)]).then_inc(attr_in[k], 16)
            passes_loop(sp, r, (), [(0, load)])

        @block.gpsimd
        def _(pool):
            def gather(m, k, pair, step):
                pool.wait_ge(idx_in[k], pair * 16 + 16)
                pool.wait_ge(edge_done, free(step))
                gather_rows(pool, rows[k], d["row_table"], idx[k], rows_in[k], ticket)
            passes_loop(pool, r, (), [(0, gather)])

        @block.tensor
        def _(pe):
            def edges(m, k, pair, step):
                pe.wait_ge(rows_in[k], (pair * 16 + 16) * G)
                pe.wait_ge(attr_in[k], pair * 16 + 16)
                pe.wait_ge(pre_done, free(step))
                for j in range(G):
                    pe.matmul(ps_e[k][:, j * P:(j + 1) * P], attr[k][:, j * P:(j + 1) * P], w_e[:, :], start=True, stop=False)
                    last = pe.matmul(ps_e[k][:, j * P:(j + 1) * P], r.ident[:, :], rows[k][:, j, :], start=False, stop=True)
                last.then_inc(edge_done, 1)

            def sums(m, k, pair, step):
                pe.wait_ge(msg_done, done(step))
                pe.wait_ge(b.hot_done, done(step))
                pe.wait_ge(b.acc_done, free(step))
                for j in range(G):
                    last = pe.matmul(ps_s[k][:, 0:W], msg[k][:, j, :], b.hot[k][:, j, :], start=j == 0, stop=j == G - 1)
                last.then_inc(b.seg_done, 1)
            passes_loop(pe, r, (edge_done, b.seg_done), [(0, edges), (1, sums)])

        @block.scalar
        def _(act):
            def copy(m, k, pair, step):
                act.wait_ge(edge_done, done(step))
                act.wait_ge(msg_done, free(step))
                act.activation(pre[k][:, :, :].rearrange("p g f -> p (g f)"), ps_e[k][:, :], ACT.Copy).then_inc(pre_done, 1)
            passes_loop(act, r, (pre_done,), [(0, copy)])

        @block.vector
        def _(dve):
            dve.memset(r.acc[:, :], 0.0).then_inc(cleared, 1)
            dve.wait_ge(cleared, 1)
            start_window(dve, r, moved)

            def hot(m, k, pair, step):
                make_hot(dve, r, b, m, k, step)

            def leaky(m, k, pair, step):
                dve.wait_ge(pre_done, done(step))
                dve.wait_ge(b.seg_done, free(step))
                dve.scalar_tensor_tensor(msg[k][:, :, :], pre[k][:, :, :], 0.01, pre[k][:, :, :], ALU.mult, ALU.max).then_inc(msg_done, 1)

            def accumulate(m, k, pair, step):
                add_window(dve, r, b, ps_s[k][:, 0:W], r.acc, step)
            passes_loop(dve, r, (b.hot_done, msg_done, b.acc_done), [(0, hot), (1, leaky), (2, accumulate)],
                        lambda q: move_window(dve, r, moved, q))


def add_window(dve, r, b, sums, to, step):
    base = dve.value_load(r.base[0:1, bass.ds(step, 1)], min_val=0, max_val=NP)
    dve.wait_ge(b.seg_done, done(step))
    dve.wait_ge(b.acc_done, prev_done(step))
    part = to[0:sums.shape[0], bass.ds(base, W)]
    dve.tensor_tensor(part, part, sums, ALU.add).then_inc(b.acc_done, 1)


def combine(nc, terms, out):
    with Memory(nc) as mem:
        order = mem.sem("order")
        block = mem.block()

        @block.vector
        def _(dve):
            terms(dve, chain(dve, order))


def mean_layer(nc, d, r):
    with Memory(nc) as mem:
        w_x, w_e, w_2 = mem.sb("w_x", [P, P]), mem.sb("w_e", [3, P]), mem.sb("w_2", [P, 2, P])
        rows, out = mem.sb("rows", [P, 2, P]), mem.sb("out", [P, NB, P])
        project(nc, [r.ht], [w_x[:, :]], out,
                load=[(w_x[:, :], d["l1_w1"][0:P, :]), (w_e[:, :], d["l1_w1"][P:P + 3, :]), (w_2[:, :, :], d["l1_w2"]),
                      (rows[:, 0, :], d["l1_b1"].partition_broadcast(P)), (rows[:, 1, :], d["l1_b2"].partition_broadcast(P))],
                add=lambda b: rows[:, 0, :], stores=[(rows_of(d["row_table"]), lambda lo, hi: out[:, lo:hi, :])])
        mean_edges(nc, d, r, w_e)
        mean = mem.sb("mean", [P, NP])

        def divide(dve, link):
            link(dve.tensor_tensor(mean[:, :], r.acc[:, 0:NP], r.inv_count[:, :], ALU.mult))
        combine(nc, divide, None)
        project(nc, [r.ht, mean], [w_2[:, 0, :], w_2[:, 1, :]], out, add=lambda b: rows[:, 1, :])

        def finish(dve, link):
            link(dve.scalar_tensor_tensor(r.x[:, :, :], out[:, :, :], 0.0, r.x[:, :, :], ALU.max, ALU.add))
        combine(nc, finish, None)


def sum_edges(nc, d, r):
    with Memory(nc) as mem:
        b = edge_buffers(mem, r, "l2", False)
        idx = mem.two("idx", [P, G], I32)
        rows = mem.two("rows", [P, G, P])
        ps_s = [mem.ps(f"ps_s{k}") for k in range(2)]
        idx_in = [mem.sem(f"idx_in{k}") for k in range(2)]
        rows_in = [mem.sem(f"rows_in{k}") for k in range(2)]
        ticket, moved, cleared = map(mem.sem, ("ticket", "moved", "cleared"))
        block = mem.block()

        @block.sync
        def _(sp):
            def load(m, k, pair, step):
                sp.wait_ge(b.seg_done, free(step))
                sp.dma_start(idx[k][:, :], d["src"][:, bass.ds(m * G, G)]).then_inc(idx_in[k], 16)
            passes_loop(sp, r, (), [(0, load)])

        @block.gpsimd
        def _(pool):
            def gather(m, k, pair, step):
                pool.wait_ge(idx_in[k], pair * 16 + 16)
                pool.wait_ge(b.seg_done, free(step))
                gather_rows(pool, rows[k], d["row_table"], idx[k], rows_in[k], ticket)
            passes_loop(pool, r, (), [(0, gather)])

        @block.tensor
        def _(pe):
            def sums(m, k, pair, step):
                pe.wait_ge(b.hot_done, done(step))
                pe.wait_ge(b.acc_done, free(step))
                pe.wait_ge(rows_in[k], (pair * 16 + 16) * G)
                for j in range(G):
                    last = pe.matmul(ps_s[k][:, 0:W], rows[k][:, j, :], b.hot[k][:, j, :], start=j == 0, stop=j == G - 1)
                last.then_inc(b.seg_done, 1)
            passes_loop(pe, r, (b.seg_done,), [(0, sums)])

        @block.vector
        def _(dve):
            dve.memset(r.acc[:, :], 0.0).then_inc(cleared, 1)
            dve.wait_ge(cleared, 1)
            start_window(dve, r, moved)

            def hot(m, k, pair, step):
                make_hot(dve, r, b, m, k, step)

            def accumulate(m, k, pair, step):
                add_window(dve, r, b, ps_s[k][:, 0:W], r.acc, step)
            passes_loop(dve, r, (b.hot_done, b.acc_done), [(0, hot), (1, accumulate)],
                        lambda q: move_window(dve, r, moved, q))


def chebyshev_layer(nc, d, r):
    with Memory(nc) as mem:
        w = mem.sb("w", [P, 4, P])
        t = [r.ht] + [mem.sb(f"t{k}", [P, NP]) for k in range(1, 4)]
        out = mem.sb("out", [P, NB, P])
        for k in range(1, 4):
            turn(nc, r, t[k - 1], out[:, :, :], scale=r.root_count, store=d["row_table"])
            sum_edges(nc, d, r)

            def recur(dve, link):
                link(dve.tensor_tensor(t[k][:, :], r.acc[:, 0:NP], r.root_count[:, :], ALU.mult))
                if k > 1:
                    link(dve.scalar_tensor_tensor(t[k][:, :], t[k][:, :], 2.0, t[k - 2][:, :], ALU.mult, ALU.subtract))
            combine(nc, recur, None)
        project(nc, t, [w[:, k, :] for k in range(4)], r.x, load=[(w[:, :, :], d["l2_w"])], add=lambda b: r.x[:, b, :])


def relation_select(dve, r, b, values, picked, m, k, step, sem_done, sem_sum, tmp):
    hot = r.type_hot[:, bass.ds(m * G, G), :]
    dve.tensor_tensor(tmp[:, :, :, :], values.rearrange("p g (r h) -> p g h r", r=R),
                      hot.unsqueeze(2).to_broadcast([P, G, H3, R]), ALU.mult).then_inc(sem_done, 1)
    dve.wait_ge(sem_done, done(step))
    dve.tensor_reduce(picked[:, :, :], tmp[:, :, :, :], AX.X, ALU.add).then_inc(sem_sum, 1)
    dve.wait_ge(sem_sum, done(step))


def relation_scores(nc, d, r):
    with Memory(nc) as mem:
        b = edge_buffers(mem, r, "l3a", True)
        idx = mem.two("idx", [P, G], I32)
        rows = mem.two("rows", [P, G, H3])
        win = mem.two("win", [W, RH + 1])
        tmp = mem.sb("tmp", [P, G, H3, R])
        picked, total, slope, gated = (mem.sb(n, [P, G, H3]) for n in ("picked", "total", "slope", "gated"))
        ps_q = mem.ps("ps_q", [P, CHUNK])
        look = ps_q[:, 0:G * (RH + 1)].rearrange("p (g c) -> p g c", g=G)
        idx_in = [mem.sem(f"idx_in{k}") for k in range(2)]
        rows_in = [mem.sem(f"rows_in{k}") for k in range(2)]
        mul_done, pick_done, add_done, slope_done, gate_done, e_done, ticket, moved, cleared, ones_set = map(
            mem.sem, ("mul_done", "pick_done", "add_done", "slope_done", "gate_done", "e_done", "ticket", "moved", "cleared", "ones_set"))
        block = mem.block()

        @block.sync
        def _(sp):
            sp.wait_ge(ones_set, 2)

            def load(m, k, pair, step):
                sp.wait_ge(add_done, free(step))
                sp.dma_start(idx[k][:, :], d["key"][:, bass.ds(m * G, G)]).then_inc(idx_in[k], 16)
                load_window(sp, r, b, d["ed_table"], [w[:, 0:RH] for w in win], m, k, step)
            passes_loop(sp, r, (), [(0, load)])

        @block.gpsimd
        def _(pool):
            def gather(m, k, pair, step):
                pool.wait_ge(idx_in[k], pair * 16 + 16)
                pool.wait_ge(add_done, free(step))
                gather_rows(pool, rows[k], d["es_table"], idx[k], rows_in[k], ticket)
            passes_loop(pool, r, (), [(0, gather)])

        @block.scalar
        def _(act):
            passes_loop(act, r, (b.copy_done,), [(0, lambda m, k, pair, step: copy_hot(act, b, k, step))])

        @block.tensor
        def _(pe):
            def turn_and_look(m, k, pair, step):
                turn_hot(pe, r, b, k, step)
                pe.wait_ge(b.copy_done, done(step))
                pe.wait_ge(b.win_in[k], pair * 16 + 16)
                pe.wait_ge(gate_done, prev_done(step))
                for j in range(G):
                    last = pe.matmul(look[:, j, :], b.hot_t[k][:, j * P:(j + 1) * P], win[k][:, :], start=True, stop=True)
                last.then_inc(b.look_done, 1)
            passes_loop(pe, r, (b.turn_done, b.look_done), [(0, turn_and_look)])

        @block.vector
        def _(dve):
            for k in range(2):
                dve.memset(win[k][:, RH:RH + 1], 1.0).then_inc(ones_set, 1)
            dve.memset(r.e[:, :, :], 0.0).then_inc(cleared, 1)
            dve.wait_ge(cleared, 1)
            start_window(dve, r, moved)

            def hot(m, k, pair, step):
                dve.wait_ge(b.turn_done, free(step))
                rel = r.rel[:, bass.ds(m, 1), :].rearrange("p o g -> p (o g)")
                dve.tensor_tensor(b.hot[k][:, :, :], bc(r.window[:, :], 1, [P, G, W]), bc(rel, 2, [P, G, W]),
                                  ALU.is_equal).then_inc(b.hot_done, 1)

            def scores(m, k, pair, step):
                dve.wait_ge(b.look_done, done(step))
                relation_select(dve, r, b, look[:, :, 0:RH], picked, m, k, step, mul_done, pick_done, tmp)
                dve.wait_ge(rows_in[k], (pair * 16 + 16) * G)
                dve.tensor_tensor(total[:, :, :], rows[k][:, :, :], picked[:, :, :], ALU.add).then_inc(add_done, 1)
                dve.wait_ge(add_done, done(step))
                dve.scalar_tensor_tensor(slope[:, :, :], total[:, :, :], 0.2, total[:, :, :], ALU.mult, ALU.max).then_inc(slope_done, 1)
                dve.wait_ge(slope_done, done(step))
                dve.tensor_tensor(gated[:, :, :], slope[:, :, :], look[:, :, RH:RH + 1].to_broadcast([P, G, H3]), ALU.mult).then_inc(gate_done, 1)
                dve.wait_ge(gate_done, done(step))
                dve.wait_ge(e_done, prev_done(step))
                e = r.e[:, bass.ds(m * G, G), :]
                dve.tensor_tensor(e, e, gated[:, :, :], ALU.add).then_inc(e_done, 1)
            passes_loop(dve, r, (b.hot_done, mul_done, pick_done, add_done, slope_done, gate_done, e_done),
                        [(0, hot), (1, scores)], lambda q: move_window(dve, r, moved, q))


def relation_maxima(nc, d, r):
    with Memory(nc) as mem:
        top = mem.sb("top", [P, GX])
        ghot = mem.sb("ghot", [P, G, GW * GN])
        val = mem.sb("val", [P, G, R, H3])
        spread = mem.two("spread", [P, GW * GN, RH])
        best = mem.two("best", [P, GW])
        gwin = mem.sb("gwin", [P, GW * GN])
        top_rows = mem.sb("top_rows", [P, 4, P])
        ps = [mem.ps(f"ps{k}") for k in range(2)]
        ps_o = mem.ps("ps_o")
        cleared, moved, ghot_done, val_done, spread_done, turn_done, best_done, top_done, end_turned, end_copied, stored = map(
            mem.sem, ("cleared", "moved", "ghot_done", "val_done", "spread_done", "turn_done", "best_done", "top_done", "end_turned", "end_copied", "stored"))
        block = mem.block()

        @block.vector
        def _(dve):
            dve.memset(top[:, :], 0.0).then_inc(cleared, 1)
            dve.tensor_copy(gwin[:, :], r.iota_g[:, :]).then_inc(moved, 1)
            dve.wait_ge(cleared, 1)
            dve.wait_ge(moved, 1)
            for s in (spread_done, best_done, top_done):
                dve.sem_inc(s, 2)
            count = dve.value_load(r.passes[0:1, 1:2], min_val=1, max_val=GQ_MAX)
            with dve.Fori(0, count) as q:
                with dve.Fori(0, M) as m:
                    step = q * M + m
                    first = dve.snap(step * G)
                    rel = r.group_rel[:, bass.ds(m * G, G)]
                    dve.tensor_tensor(ghot[:, :, :], bc(gwin[:, :], 1, [P, G, GW * GN]), bc(rel, 2, [P, G, GW * GN]), ALU.is_equal).then_inc(ghot_done, 1)
                    dve.tensor_tensor(val[:, :, :, :], bc(r.type_hot[:, bass.ds(m * G, G), :], 3, [P, G, R, H3]),
                                      bc(r.e[:, bass.ds(m * G, G), :], 2, [P, G, R, H3]), ALU.mult).then_inc(val_done, 1)
                    dve.wait_ge(ghot_done, step + 1)
                    dve.wait_ge(val_done, step + 1)

                    def spread_tile(j):
                        tile = first + j
                        dve.wait_ge(turn_done, free(tile))
                        dve.tensor_tensor(spread[j % 2][:, :, :], bc(ghot[:, j, :], 2, [P, GW * GN, RH]),
                                          bc(val[:, j, :, :].rearrange("p r h -> p (r h)"), 1, [P, GW * GN, RH]), ALU.mult).then_inc(spread_done, 1)

                    def take_tile(j):
                        tile = first + j
                        group = dve.value_load(r.tile_group[0:1, bass.ds(m * G + j, 1)], min_val=0, max_val=NG - 1)
                        dve.wait_ge(turn_done, done(tile))
                        dve.tensor_reduce(best[j % 2][:, :], ps[j % 2][:, 0:GW * P].rearrange("p (g e) -> p g e", g=GW), AX.X, ALU.max).then_inc(best_done, 1)
                        dve.wait_ge(best_done, done(tile))
                        dve.wait_ge(top_done, prev_done(tile))
                        part = top[:, bass.ds(group + q * GW, GW)]
                        dve.tensor_tensor(part, part, best[j % 2][:, :], ALU.max).then_inc(top_done, 1)
                    spread_tile(0)
                    for j in range(G):
                        if j + 1 < G:
                            spread_tile(j + 1)
                        take_tile(j)
                dve.tensor_scalar(gwin[:, :], gwin[:, :], float(GW * GN), None, ALU.add).then_inc(moved, 1)
                dve.wait_ge(moved, q + 2)
            dve.sem_inc(end_copied, 1)

        @block.tensor
        def _(pe):
            pe.sem_inc(turn_done, 2)
            count = pe.value_load(r.passes[0:1, 1:2], min_val=1, max_val=GQ_MAX)
            with pe.Fori(0, count) as q:
                with pe.Fori(0, M) as m:
                    first = pe.snap((q * M + m) * G)
                    for j in range(G):
                        tile = first + j
                        pe.wait_ge(spread_done, done(tile))
                        pe.wait_ge(best_done, free(tile))
                        flat = spread[j % 2][:, :, :].rearrange("p n c -> p (n c)")
                        for g in range(GW):
                            last = pe.transpose(ps[j % 2][:, g * P:(g + 1) * P], flat[:, g * P:(g + 1) * P], r.ident[:, :])
                        last.then_inc(turn_done, 1)
            pe.wait_ge(end_copied, 1)
            for n in range(4):
                width = min(P, NG - n * P)
                last = pe.transpose(ps_o[0:width, n * P:(n + 1) * P], top[:, n * P:n * P + width], r.ident[:, :])
            last.then_inc(end_turned, 1)

        @block.scalar
        def _(act):
            act.wait_ge(end_turned, 1)
            for n in range(4):
                width = min(P, NG - n * P)
                act.activation(top_rows[0:width, n, :], ps_o[0:width, n * P:(n + 1) * P], ACT.Copy).then_inc(end_copied, 1)

        @block.sync
        def _(sp):
            sp.wait_ge(end_copied, 5)
            for n in range(4):
                width = min(P, NG - n * P)
                sp.dma_start(d["top_table"][n * P * GN:(n * P + width) * GN, :].rearrange("(g a) c -> g (a c)", a=GN), top_rows[0:width, n, :]).then_inc(stored, 16)
            sp.wait_ge(stored, 64)


def relation_exps(nc, d, r):
    with Memory(nc) as mem:
        b = edge_buffers(mem, r, "l3b", True)
        win = mem.two("win", [W, RH + 1])
        tmp = mem.sb("tmp", [P, G, H3, R])
        picked, less = (mem.sb(n, [P, G, H3]) for n in ("picked", "less"))
        gated, power = mem.two("gated", [P, G, H3]), mem.two("power", [P, G, H3])
        kept = mem.sb("kept", [P, G, H3])
        gate = mem.two("gate", [P, G])
        placed = mem.two("placed", [P, G, R, H3])
        ps_q = mem.ps("ps_q", [P, CHUNK])
        ps_z = [mem.ps(f"ps_z{k}") for k in range(2)]
        look = ps_q[:, 0:G * (RH + 1)].rearrange("p (g c) -> p g c", g=G)
        mul_done, pick_done, less_done, copy2_done, gate_done, exp_done, kept_done, a_done, place_done, moved, cleared, ones_set = map(
            mem.sem, ("mul_done", "pick_done", "less_done", "copy2_done", "gate_done", "exp_done", "kept_done", "a_done", "place_done", "moved", "cleared", "ones_set"))
        block = mem.block()

        @block.sync
        def _(sp):
            sp.wait_ge(ones_set, 2)
            passes_loop(sp, r, (), [(0, lambda m, k, pair, step: load_window(sp, r, b, d["top_table"], [w[:, 0:RH] for w in win], m, k, step))])

        @block.scalar
        def _(act):
            def exps(m, k, pair, step):
                act.wait_ge(gate_done, done(step))
                act.wait_ge(place_done, free(step))
                act.activation(power[k][:, :, :], gated[k][:, :, :], ACT.Exp).then_inc(exp_done, 1)
            passes_loop(act, r, (b.copy_done, exp_done), [(0, lambda m, k, pair, step: copy_hot(act, b, k, step)), (1, exps)])

        @block.tensor
        def _(pe):
            def turn_and_look(m, k, pair, step):
                turn_hot(pe, r, b, k, step)
                pe.wait_ge(b.copy_done, done(step))
                pe.wait_ge(b.win_in[k], pair * 16 + 16)
                pe.wait_ge(gate_done, prev_done(step))
                for j in range(G):
                    last = pe.matmul(look[:, j, :], b.hot_t[k][:, j * P:(j + 1) * P], win[k][:, :], start=True, stop=True)
                last.then_inc(b.look_done, 1)

            def sums(m, k, pair, step):
                pe.wait_ge(place_done, done(step))
                pe.wait_ge(b.acc_done, free(step))
                for j in range(G):
                    last = pe.matmul(ps_z[k][0:RH, 0:W], placed[k][:, j, :, :].rearrange("p r h -> p (r h)"), b.hot[k][:, j, :], start=j == 0, stop=j == G - 1)
                last.then_inc(b.seg_done, 1)
            passes_loop(pe, r, (b.turn_done, b.look_done, b.seg_done), [(0, turn_and_look), (1, sums)])

        @block.vector
        def _(dve):
            for k in range(2):
                dve.memset(win[k][:, RH:RH + 1], 1.0).then_inc(ones_set, 1)
            dve.memset(r.z[:, :], 0.0).then_inc(cleared, 1)
            dve.memset(r.a[:, :, :], 0.0).then_inc(cleared, 1)
            dve.wait_ge(cleared, 2)
            start_window(dve, r, moved)

            def hot(m, k, pair, step):
                make_hot(dve, r, b, m, k, step)

            def scores(m, k, pair, step):
                dve.wait_ge(b.look_done, done(step))
                relation_select(dve, r, b, look[:, :, 0:RH], picked, m, k, step, mul_done, pick_done, tmp)
                dve.tensor_tensor(less[:, :, :], r.e[:, bass.ds(m * G, G), :], picked[:, :, :], ALU.subtract).then_inc(less_done, 1)
                dve.tensor_copy(gate[k][:, :], look[:, :, RH]).then_inc(copy2_done, 1)
                dve.wait_ge(less_done, done(step))
                dve.wait_ge(copy2_done, done(step))
                dve.tensor_tensor(gated[k][:, :, :], less[:, :, :], bc(gate[k][:, :], 2, [P, G, H3]), ALU.mult).then_inc(gate_done, 1)

            def place(m, k, pair, step):
                dve.wait_ge(exp_done, done(step))
                dve.wait_ge(b.seg_done, free(step))
                dve.tensor_tensor(placed[k][:, :, :, :], bc(r.type_hot[:, bass.ds(m * G, G), :], 3, [P, G, R, H3]),
                                  bc(power[k][:, :, :], 2, [P, G, R, H3]), ALU.mult)
                dve.tensor_tensor(kept[:, :, :], power[k][:, :, :], bc(gate[k][:, :], 2, [P, G, H3]), ALU.mult).then_inc(place_done, 1)
                dve.wait_ge(place_done, done(step))
                dve.wait_ge(a_done, prev_done(step))
                a = r.a[:, bass.ds(m * G, G), :]
                dve.tensor_tensor(a, a, kept[:, :, :], ALU.add).then_inc(a_done, 1)

            def accumulate(m, k, pair, step):
                add_window(dve, r, b, ps_z[k][0:RH, 0:W], r.z, step)
            passes_loop(dve, r, (b.hot_done, mul_done, pick_done, less_done, copy2_done, gate_done, place_done, a_done, b.acc_done),
                        [(0, hot), (1, scores), (1, place), (2, accumulate)], lambda q: move_window(dve, r, moved, q))


def relation_scale(nc, d, r):
    with Memory(nc) as mem:
        inv = mem.sb("inv", [RH, NP])
        out = mem.sb("out", [P, NB, RH])
        ps = mem.ps("ps")
        order, ready, turned, copied, stored = map(mem.sem, ("order", "ready", "turned", "copied", "stored"))
        block = mem.block()

        @block.vector
        def _(dve):
            link = chain(dve, order)
            link(dve.tensor_scalar(inv[:, :], r.z[0:RH, 0:NP], 1e-8, None, ALU.add))
            link(dve.reciprocal(inv[:, :], inv[:, :]))
            dve.sem_inc(ready, 1)

        @block.tensor
        def _(pe):
            pe.wait_ge(ready, 1)
            for b in range(NB):
                last = pe.transpose(ps[:, b * RH:(b + 1) * RH], inv[:, b * P:(b + 1) * P], r.ident[0:RH, 0:RH])
            last.then_inc(turned, 1)

        @block.scalar
        def _(act):
            act.wait_ge(turned, 1)
            act.activation(out[:, :, :].rearrange("p b c -> p (b c)"), ps[:, 0:NB * RH], ACT.Copy).then_inc(copied, 1)

        @block.sync
        def _(sp):
            sp.wait_ge(copied, 1)
            sp.dma_start(rows_of(d["rs_table"])(0, NB), out[:, :, :]).then_inc(stored, 16)
            sp.wait_ge(stored, 16)


def relation_edges(nc, d, r):
    with Memory(nc) as mem:
        b = edge_buffers(mem, r, "l3c", True)
        idx = mem.two("idx", [P, G], I32)
        rows = mem.two("rows", [P, G, P])
        msg = mem.two("msg", [P, G, P])
        win = mem.two("win", [W, RH])
        tmp = mem.sb("tmp", [P, G, H3, R])
        picked, alpha = (mem.sb(n, [P, G, H3]) for n in ("picked", "alpha"))
        ps_q = mem.ps("ps_q", [P, CHUNK])
        look = ps_q[:, 0:G * RH].rearrange("p (g c) -> p g c", g=G)
        ps_s = [mem.ps(f"ps_s{k}") for k in range(2)]
        idx_in = [mem.sem(f"idx_in{k}") for k in range(2)]
        rows_in = [mem.sem(f"rows_in{k}") for k in range(2)]
        mul_done, pick_done, alpha_done, msg_done, ticket, moved, cleared = map(
            mem.sem, ("mul_done", "pick_done", "alpha_done", "msg_done", "ticket", "moved", "cleared"))
        block = mem.block()

        @block.sync
        def _(sp):
            def load(m, k, pair, step):
                sp.wait_ge(msg_done, free(step))
                sp.dma_start(idx[k][:, :], d["key"][:, bass.ds(m * G, G)]).then_inc(idx_in[k], 16)
                load_window(sp, r, b, d["rs_table"], [w[:, :] for w in win], m, k, step)
            passes_loop(sp, r, (), [(0, load)])

        @block.gpsimd
        def _(pool):
            def gather(m, k, pair, step):
                pool.wait_ge(idx_in[k], pair * 16 + 16)
                pool.wait_ge(msg_done, free(step))
                gather_rows(pool, rows[k], d["h_table"], idx[k], rows_in[k], ticket)
            passes_loop(pool, r, (), [(0, gather)])

        @block.scalar
        def _(act):
            passes_loop(act, r, (b.copy_done,), [(0, lambda m, k, pair, step: copy_hot(act, b, k, step))])

        @block.tensor
        def _(pe):
            def turn_and_look(m, k, pair, step):
                turn_hot(pe, r, b, k, step)
                pe.wait_ge(b.copy_done, done(step))
                pe.wait_ge(b.win_in[k], pair * 16 + 16)
                pe.wait_ge(mul_done, prev_done(step))
                for j in range(G):
                    last = pe.matmul(look[:, j, :], b.hot_t[k][:, j * P:(j + 1) * P], win[k][:, :], start=True, stop=True)
                last.then_inc(b.look_done, 1)

            def sums(m, k, pair, step):
                pe.wait_ge(msg_done, done(step))
                pe.wait_ge(b.acc_done, free(step))
                for j in range(G):
                    last = pe.matmul(ps_s[k][:, 0:W], msg[k][:, j, :], b.hot[k][:, j, :], start=j == 0, stop=j == G - 1)
                last.then_inc(b.seg_done, 1)
            passes_loop(pe, r, (b.turn_done, b.look_done, b.seg_done), [(0, turn_and_look), (1, sums)])

        @block.vector
        def _(dve):
            dve.memset(r.acc[:, :], 0.0).then_inc(cleared, 1)
            dve.wait_ge(cleared, 1)
            start_window(dve, r, moved)

            def hot(m, k, pair, step):
                make_hot(dve, r, b, m, k, step)

            def messages(m, k, pair, step):
                dve.wait_ge(b.look_done, done(step))
                relation_select(dve, r, b, look, picked, m, k, step, mul_done, pick_done, tmp)
                dve.tensor_tensor(alpha[:, :, :], r.a[:, bass.ds(m * G, G), :], picked[:, :, :], ALU.mult).then_inc(alpha_done, 1)
                dve.wait_ge(alpha_done, done(step))
                dve.wait_ge(b.seg_done, free(step))
                dve.wait_ge(rows_in[k], (pair * 16 + 16) * G)
                dve.tensor_tensor(msg[k][:, :, :].rearrange("p g (h c) -> p g h c", h=H3),
                                  rows[k][:, :, :].rearrange("p g (h c) -> p g h c", h=H3),
                                  alpha[:, :, :].unsqueeze(3).to_broadcast([P, G, H3, P // H3]), ALU.mult).then_inc(msg_done, 1)

            def accumulate(m, k, pair, step):
                add_window(dve, r, b, ps_s[k][:, 0:W], r.acc, step)
            passes_loop(dve, r, (b.hot_done, mul_done, pick_done, alpha_done, msg_done, b.acc_done),
                        [(0, hot), (1, messages), (2, accumulate)], lambda q: move_window(dve, r, moved, q))


def relation_layer(nc, d, r):
    with Memory(nc) as mem:
        w, w_a, attn = mem.sb("w", [P, R * P]), mem.sb("w_a", [P, 2 * RH]), mem.sb("attn", [P, 2, R * P])
        tmp = mem.sb("tmp", [P, R * P])
        load = [(w[:, :], d["l3_w"])] + [(attn[:, n, :], v.partition_broadcast(P)) for n, v in enumerate((d["l3_attn_src"], d["l3_attn_dst"]))]
        with Memory(nc) as inner:
            loaded, order = inner.sem("loaded"), inner.sem("order")
            block = inner.block()

            @block.sync
            def _(sp):
                for to, of in load:
                    sp.dma_start(to, of).then_inc(loaded, 16)

            @block.vector
            def _(dve):
                link = chain(dve, order)
                dve.wait_ge(loaded, 48)
                for n in range(2):
                    link(dve.tensor_tensor(tmp[:, :], w[:, :], attn[:, n, :], ALU.mult))
                    link(dve.tensor_reduce(w_a[:, n * RH:(n + 1) * RH], tmp[:, :].rearrange("p (c k) -> p c k", k=P // H3), AX.X, ALU.add))
        with Memory(nc) as inner:
            out = inner.sb("out", [P, NB, R * P])
            project(nc, [r.ht], [w[:, :]], out,
                    stores=[(lambda lo, hi, k=k: d["h_table"][k * NP + lo * P:k * NP + hi * P, :].rearrange("(b p) f -> p b f", p=P),
                             lambda lo, hi, k=k: out[:, lo:hi, k * P:(k + 1) * P]) for k in range(R)])
            ea = inner.sb("ea", [P, NB, 2 * RH])
            project(nc, [r.ht], [w_a[:, :]], ea,
                    stores=[(rows_of(d["ed_table"]), lambda lo, hi: ea[:, lo:hi, RH:2 * RH])] +
                           [(lambda lo, hi, k=k: d["es_table"][k * NP + lo * P:k * NP + hi * P, :].rearrange("(b p) f -> p b f", p=P),
                             lambda lo, hi, k=k: ea[:, lo:hi, k * H3:(k + 1) * H3]) for k in range(R)])
    with Memory(nc) as mem:
        r.e, r.a = mem.sb("e", [P, T, H3]), mem.sb("a", [P, T, H3])
        relation_scores(nc, d, r)
        relation_maxima(nc, d, r)
        relation_exps(nc, d, r)
        relation_scale(nc, d, r)
        relation_edges(nc, d, r)
    with Memory(nc) as mem:
        rows, out = mem.sb("rows", [P, 3, P]), mem.sb("out", [P, NB, P])
        turn(nc, r, r.acc[:, 0:NP], out[:, :, :])
        add_rows(nc, out, rows[:, 0, :], [(rows[:, n, :], v.partition_broadcast(P)) for n, v in
                                          enumerate((d["l3_bias"], d["l3_ln_gamma"], d["l3_ln_beta"]))])

        def skip(dve, link):
            link(dve.tensor_tensor(out[:, :, :], out[:, :, :], r.h[:, :, :], ALU.add))
        combine(nc, skip, None)
        normalise(nc, r, out[:, :, :], None, weight=rows[:, 1, :], shift=rows[:, 2, :], residual=r.x[:, :, :])


def build(nc, d):
    r = Names()
    with Memory(nc) as mem:
        r.x = mem.sb("x_nodes", [P, NB, P])
        r.h = mem.sb("h_nodes", [P, NB, P])
        r.ht = mem.sb("h_features", [P, NP])
        r.acc = mem.sb("acc", [P, NX])
        r.z = mem.sb("z", [RH, NX])
        r.inv_count = mem.sb("inv_count", [P, NP])
        r.root_count = mem.sb("root_count", [P, NP])
        r.rel = mem.sb("rel", [P, M, G])
        r.group_rel = mem.sb("group_rel", [P, T])
        r.type_hot = mem.sb("type_hot", [P, T, R])
        r.iota_w = mem.sb("iota_w", [P, W])
        r.iota_g = mem.sb("iota_g", [P, GW * GN])
        r.iota_r = mem.sb("iota_r", [P, R])
        r.window = mem.sb("window", [P, W])
        r.ident = mem.sb("ident", [P, P])
        r.passes = mem.sb("passes", [P, 2], I32)
        r.base = mem.sb("base", [1, Q_MAX * M], I32)
        r.tile_group = mem.sb("tile_group", [1, T], I32)
        before = nc.snapshot_sems()
        prepare(nc, d, r)
        for layer in (attention_layer, mean_layer, chebyshev_layer, relation_layer):
            normalise(nc, r, r.x[:, :, :], r.h[:, :, :], relu=True)
            turn(nc, r, r.h[:, :, :], r.ht[:, :])
            layer(nc, d, r)
            nc.clear_and_free_semaphores(nc.allocated_since(before))
            nc.all_engine_barrier()
            before = nc.snapshot_sems()
        stored = mem.sem("out_stored")
        block = mem.block()

        @block.sync
        def _(sp):
            sp.dma_start(d["out"], r.x[:, :, :]).then_inc(stored, 16)
            sp.wait_ge(stored, 16)


def kernel(**inputs):
    import concourse.bacc as bacc
    from concourse.bass_utils import run_bass_kernel_spmd

    nc = bacc.Bacc("TRN2", target_bir_lowering=False, num_devices=1)
    d = {}
    arrays = {}

    def put(name, a):
        a = np.ascontiguousarray(a)
        arrays["in_" + name] = a
        d[name] = nc.dram_tensor("in_" + name, a.shape, mybir.dt.from_np(a.dtype), kind="ExternalInput").ap()

    def by_tile(a, value):
        return np.pad(np.asarray(a), (0, EP - E), constant_values=value).reshape(T, P).T

    g = {k: np.asarray(v) for k, v in inputs.items()}
    put("x", np.pad(g["x"], ((0, NP - N), (0, 0))).reshape(NB, P, P).transpose(1, 0, 2))
    put("src", by_tile(g["src"], 0))
    put("dst", by_tile(g["dst"], FAR))
    put("edge_type", by_tile(g["edge_type_4"], 0))
    put("dst_sorted", np.pad(g["dst"], (0, EP - E), mode="edge"))
    put("edge_attr", np.pad(g["edge_attr_3"], ((0, EP - E), (0, 0))).T)
    for name in ("Wq", "Wk", "Wv", "Wo", "bo", "ln1_g", "ln1_b", "W1", "b2", "ln2_g", "ln2_b"):
        put("l0_" + name.lower(), g["L0_gnn_" + name])
    put("l0_b1", g["L0_gnn_b1"].reshape(2, P).T)
    put("l0_w2", g["L0_gnn_W2"].reshape(2, P, P).transpose(1, 0, 2))
    put("l1_w1", g["L1_gnn_W1"].T)
    put("l1_w2", g["L1_gnn_W2"].T.reshape(2, P, P).transpose(1, 0, 2))
    put("l1_b1", g["L1_gnn_b1"])
    put("l1_b2", g["L1_gnn_b2"])
    put("l2_w", g["L2_gnn_weights"].transpose(1, 0, 2))
    put("l3_w", g["L3_gnn_W"].transpose(1, 0, 2).reshape(P, R * P))
    put("l3_attn_src", g["L3_gnn_attn_src"].reshape(-1))
    put("l3_attn_dst", g["L3_gnn_attn_dst"].reshape(-1))
    for name in ("bias", "ln_gamma", "ln_beta"):
        put("l3_" + name, g["L3_gnn_" + name])
    for name, shape, dtype in (("macro_bounds", [2 * M], I32), ("tile_bounds", [2 * T], I32), ("key", [P, T], I32),
                               ("kv_table", [NP, 2 * P], F32), ("q_table", [NX, P], F32), ("row_table", [NP, P], F32),
                               ("h_table", [R * NP, P], F32), ("es_table", [R * NP, H3], F32), ("ed_table", [NX, RH], F32),
                               ("top_table", [NX, RH], F32), ("rs_table", [NX, RH], F32)):
        d[name] = nc.dram_tensor(name, shape, dtype).ap()
    d["out"] = nc.dram_tensor("out", (P, NB, P), F32, kind="ExternalOutput").ap()
    build(nc, d)
    res = run_bass_kernel_spmd(nc, [arrays], core_ids=[0])
    return res.results[0]["out"].transpose(1, 0, 2).reshape(NP, P)[:N]
```

```python
import numpy as np
from contextlib import ExitStack
import concourse.bass as bass
from concourse import mybir

F32, BF16, I32, I16 = mybir.dt.float32, mybir.dt.bfloat16, mybir.dt.int32, mybir.dt.int16
ALU, ACT, AX = mybir.AluOpType, mybir.ActivationFunctionType, mybir.AxisListType

P = 128
N = 3125
NB = -(-N // P)
NP = NB * P
NX = NP + P
E = 53125
G = 8
W = 96
M = -(-E // (2 * G * P)) * 2
T = M * G
EP = T * P
Q_MAX = -(-N // W)
H0 = 8
Z0 = H0 + 1
R, H3 = 4, 4
RH = R * H3
HALF = G // 2
GN = 8
GW = 3
NG = NX // GN
GQ_MAX = -(-(-(-N // GN)) // GW)
GX = NG + GW * GQ_MAX + GW
PASS_MAX = GQ_MAX
BASE_ROWS = PASS_MAX + PASS_MAX % 2
ROW = P + H3
PARTS = 3
TAG = GW * GN + PARTS * RH
BIG = 1e30
KIND = 1 << 13
FAR = 1 << 20
CHUNK = 512
EPS = 1e-5


def done(step):
    return step + 3


def prev_done(step):
    return step + 2


def free(step):
    return step + 1


def bc(ap, axis, shape):
    return ap.unsqueeze(axis).to_broadcast(shape)


def chunks():
    return [(lo, min(CHUNK, NP - lo)) for lo in range(0, NP, CHUNK)]


def chain(engine, semaphore):
    n = [0]

    def link(instruction):
        n[0] += 1
        instruction.then_inc(semaphore, 1)
        engine.wait_ge(semaphore, n[0])
    return link


class Names:
    pass


class Memory:

    def __init__(self, nc):
        self.nc, self.stack = nc, ExitStack()
        self.stage = f"{nc.next_id()}"

    def __enter__(self):
        return self

    def __exit__(self, *error):
        return self.stack.__exit__(*error)

    def sb(self, name, shape, dtype=F32):
        return self.stack.enter_context(self.nc.sbuf_tensor(f"{name}_{self.stage}", shape, dtype))

    def two(self, name, shape, dtype=F32):
        return [self.sb(f"{name}{k}", shape, dtype) for k in range(2)]

    def ps(self, name, shape=(P, CHUNK), dtype=F32):
        return self.stack.enter_context(self.nc.psum_tensor(f"{name}_{self.stage}", list(shape), dtype))

    def sem(self, name):
        return self.nc.alloc_semaphore(f"{name}_{self.stage}")

    def block(self):
        return self.stack.enter_context(self.nc.Block())


def prepare(nc, d, r):
    with Memory(nc) as mem:
        macro_dst = mem.sb("macro_dst", [M, G * P], I32)
        tile_dst = mem.sb("tile_dst", [T // 4, 4, P], I32)
        macro_f = mem.sb("macro_f", [M, 2])
        macro_i = mem.sb("macro_i", [M, 2], I32)
        tile_f = mem.sb("tile_f", [T // 4, 4, 2])
        tile_i = mem.sb("tile_i", [T // 4, 4, 2], I32)
        macro_row = mem.sb("macro_row", [P, M, 2], I32)
        tile_row = mem.sb("tile_row", [P, T, 2], I32)
        macro_rf = mem.sb("macro_rf", [P, M, 2])
        tile_rf = mem.sb("tile_rf", [P, T, 2])
        span = mem.sb("span", [P, M])
        gspan = mem.sb("gspan", [P, T])
        widest = mem.sb("widest", [P, 2])
        offset = mem.sb("offset", [BASE_ROWS // 2, 2])
        offset_lo = mem.sb("offset_lo", [BASE_ROWS // 2, 2, M])
        base_rows = mem.sb("base_rows", [BASE_ROWS // 2, 2, M], I16)
        steps = mem.sb("steps", [P, Q_MAX])
        gsteps = mem.sb("gsteps", [P, GQ_MAX])
        count = mem.sb("count", [P, 3])
        dst_f = mem.sb("dst_f", [P, T])
        src_f = mem.sb("src_f", [P, T])
        type_f = mem.sb("type_f", [P, T])
        dst_i = mem.sb("dst_i", [P, T], I32)
        src_i = mem.sb("src_i", [P, T], I32)
        type_i = mem.sb("type_i", [P, T], I32)
        key_i = mem.sb("key_i", [P, T], I32)
        iota_p = mem.sb("iota_p", [P, P])
        iota_q = mem.sb("iota_q", [P, 1])
        zero = mem.sb("zero", [P, P])
        loaded, order, extremes, stored, back, iotas, key_done, zero_done, bases_made, base_out = map(
            mem.sem, ("loaded", "order", "extremes", "stored", "back", "iotas", "key_done", "zero_done", "bases_made", "base_out"))
        block = mem.block()

        @block.sync
        def _(sp):
            sp.dma_start(macro_dst[:, :], d["dst_sorted"].rearrange("(m e) -> m e", m=M)).then_inc(loaded, 16)
            sp.dma_start(tile_dst[:, :, :], d["dst_sorted"].rearrange("(a b e) -> a b e", b=4, e=P)).then_inc(loaded, 16)
            sp.dma_start(dst_i[:, :], d["dst"]).then_inc(loaded, 16)
            sp.dma_start(src_i[:, :], d["src"]).then_inc(loaded, 16)
            sp.dma_start(type_i[:, :], d["edge_type"]).then_inc(loaded, 16)
            sp.dma_start(r.x[:, :, :], d["x"]).then_inc(loaded, 16)
            sp.wait_ge(zero_done, 1)
            for table in (d["q_table"], d["ed_table"]):
                width = table.shape[1]
                sp.dma_start(table[NP:NX, :], zero[:, 0:width]).then_inc(stored, 16)
            sp.wait_ge(extremes, 1)
            sp.dma_start(d["macro_bounds"].rearrange("(m k) -> m k", k=2), macro_i[:, :]).then_inc(stored, 16)
            sp.dma_start(d["tile_bounds"].rearrange("(a b) -> a b", b=8), tile_i[:, :, :].rearrange("a b k -> a (b k)")).then_inc(stored, 16)
            sp.wait_ge(stored, 64)
            sp.dma_start(macro_row[:, :, :].rearrange("p m k -> p (m k)"), d["macro_bounds"].partition_broadcast(P)).then_inc(back, 16)
            sp.dma_start(tile_row[:, :, :].rearrange("p t k -> p (t k)"), d["tile_bounds"].partition_broadcast(P)).then_inc(back, 16)
            sp.wait_ge(bases_made, 1)
            sp.dma_start(d["base_table"].rearrange("(p k) -> p k", p=BASE_ROWS // 2), base_rows[:, :, :].rearrange("p j m -> p (j m)")).then_inc(base_out, 16)
            sp.wait_ge(base_out, 16)
            sp.dma_start(r.base[:, :], d["base_table"].unsqueeze(0)).then_inc(base_out, 16)
            sp.wait_ge(base_out, 32)
            sp.wait_ge(key_done, 1)
            sp.dma_start(d["key"], key_i[:, :]).then_inc(stored, 16)
            sp.wait_ge(stored, 80)

        @block.gpsimd
        def _(pool):
            for out, step in ((r.iota_w[:, :], 1), (r.iota_g[:, :], 1), (steps[:, :], W), (gsteps[:, :], GW),
                              (r.iota_r[:, :], 1), (iota_p[:, :], 1)):
                pool.iota(out, [[step, out.shape[1]]], base=0, channel_multiplier=0,
                          allow_small_or_imprecise_dtypes=True).then_inc(iotas, 1)
            pool.iota(offset[:, :], [[W, 2]], base=0, channel_multiplier=2 * W,
                      allow_small_or_imprecise_dtypes=True).then_inc(iotas, 1)
            pool.iota(iota_q[:, :], [[0, 1]], base=0, channel_multiplier=1,
                      allow_small_or_imprecise_dtypes=True).then_inc(iotas, 1)

        @block.vector
        def _(dve):
            link = chain(dve, order)
            link(dve.memset(zero[:, :], 0.0))
            dve.sem_inc(zero_done, 1)
            dve.wait_ge(loaded, 96)
            dve.tensor_reduce(macro_f[:, 0:1], macro_dst[:, :], AX.X, ALU.min)
            dve.tensor_reduce(macro_f[:, 1:2], macro_dst[:, :], AX.X, ALU.max)
            dve.tensor_reduce(tile_f[:, :, 0], tile_dst[:, :, :], AX.X, ALU.min)
            link(dve.tensor_reduce(tile_f[:, :, 1], tile_dst[:, :, :], AX.X, ALU.max))
            dve.tensor_copy(macro_i[:, :], macro_f[:, :])
            link(dve.tensor_copy(tile_i[:, :, :], tile_f[:, :, :]))
            link(dve.tensor_scalar(tile_i[:, :, :], tile_i[:, :, :], 3, None, ALU.arith_shift_right))
            dve.sem_inc(extremes, 1)
            dve.tensor_copy(src_f[:, :], src_i[:, :])
            dve.tensor_copy(dst_f[:, :], dst_i[:, :])
            link(dve.tensor_copy(type_f[:, :], type_i[:, :]))
            link(dve.scalar_tensor_tensor(src_f[:, :], type_f[:, :], float(NP), src_f[:, :], ALU.mult, ALU.add))
            link(dve.tensor_copy(key_i[:, :], src_f[:, :]))
            dve.sem_inc(key_done, 1)
            dve.wait_ge(iotas, 8)
            dve.tensor_tensor(r.type_hot[:, :, :], bc(type_f[:, :], 2, [P, T, R]), bc(r.iota_r[:, :], 1, [P, T, R]), ALU.is_equal)
            dve.tensor_scalar(r.ident[:, :], iota_p[:, :], iota_q[:, :], None, ALU.is_equal)
            dve.wait_ge(back, 32)
            dve.tensor_copy(macro_rf[:, :, :], macro_row[:, :, :])
            dve.tensor_copy(r.tile_group[:, :], tile_row[0:1, :, 0])
            link(dve.tensor_copy(tile_rf[:, :, :], tile_row[:, :, :]))
            half = BASE_ROWS // 2
            for j in range(2):
                last = dve.tensor_scalar(offset_lo[:, j, :], macro_rf[0:half, :, 0], offset[:, j:j + 1], float(NP), ALU.add, ALU.min)
            link(last)
            link(dve.tensor_copy(base_rows[:, :, :], offset_lo[:, :, :]))
            dve.sem_inc(bases_made, 1)
            dve.tensor_tensor(r.rel[:, :, :], dst_f[:, :].rearrange("p (m g) -> p m g", g=G),
                              bc(macro_rf[:, :, 0], 2, [P, M, G]), ALU.subtract)
            dve.scalar_tensor_tensor(r.group_rel[:, :], tile_rf[:, :, 0], -float(GN), dst_f[:, :], ALU.mult, ALU.add)
            dve.tensor_tensor(span[:, :], macro_rf[:, :, 1], macro_rf[:, :, 0], ALU.subtract)
            link(dve.tensor_tensor(gspan[:, :], tile_rf[:, :, 1], tile_rf[:, :, 0], ALU.subtract))
            dve.tensor_reduce(widest[:, 0:1], span[:, :], AX.X, ALU.max)
            link(dve.tensor_reduce(widest[:, 1:2], gspan[:, :], AX.X, ALU.max))
            dve.tensor_scalar(steps[:, :], steps[:, :], widest[:, 0:1], None, ALU.is_le)
            link(dve.tensor_scalar(gsteps[:, :], gsteps[:, :], widest[:, 1:2], None, ALU.is_le))
            dve.tensor_reduce(count[:, 0:1], steps[:, :], AX.X, ALU.add)
            link(dve.tensor_reduce(count[:, 1:2], gsteps[:, :], AX.X, ALU.add))
            link(dve.tensor_tensor(count[:, 1:2], count[:, 0:1], count[:, 1:2], ALU.max))
            link(dve.tensor_scalar(count[:, 2:3], count[:, 1:2], 1.5, 1.0, ALU.is_gt, ALU.add))
            dve.tensor_copy(r.passes[:, :], count[:, :])
            dve.scalar_tensor_tensor(r.typed_rel[:, :], type_f[:, :], float(KIND), r.rel[:, :, :].rearrange("p m g -> p (m g)"), ALU.mult, ALU.add)


def normalise(nc, r, src, out, relu=False, weight=None, shift=None, residual=None, load=()):
    with Memory(nc) as mem:
        centred, square = mem.sb("centred", [P, NB, P]), mem.sb("square", [P, NB, P])
        stat, root, inv = mem.sb("stat", [P, NB]), mem.sb("root", [P, NB]), mem.sb("inv", [P, NB])
        order, var_done, root_done, loaded = map(mem.sem, ("order", "var_done", "root_done", "loaded"))
        block = mem.block()
        shape = [P, NB, P]

        @block.sync
        def _(sp):
            for to, of in load:
                sp.dma_start(to, of).then_inc(loaded, 16)
            if load:
                sp.wait_ge(loaded, 16 * len(load))

        @block.vector
        def _(dve):
            link = chain(dve, order)
            link(dve.tensor_reduce(stat[:, :], src, AX.X, ALU.add))
            link(dve.tensor_scalar(stat[:, :], stat[:, :], 1.0 / P, None, ALU.mult))
            link(dve.tensor_tensor(centred[:, :, :], src, bc(stat[:, :], 2, shape), ALU.subtract))
            link(dve.tensor_tensor(square[:, :, :], centred[:, :, :], centred[:, :, :], ALU.mult))
            link(dve.tensor_reduce(stat[:, :], square[:, :, :], AX.X, ALU.add))
            link(dve.tensor_scalar(stat[:, :], stat[:, :], 1.0 / P, EPS, ALU.mult, ALU.add))
            dve.sem_inc(var_done, 1)
            dve.wait_ge(root_done, 1)
            link(dve.reciprocal(inv[:, :], root[:, :]))
            if relu:
                link(dve.tensor_tensor(square[:, :, :], centred[:, :, :], bc(inv[:, :], 2, shape), ALU.mult))
                link(dve.tensor_scalar(out, square[:, :, :], 0.0, None, ALU.max))
                return
            link(dve.tensor_tensor(square[:, :, :], centred[:, :, :], bc(inv[:, :], 2, shape), ALU.mult))
            if load:
                dve.wait_ge(loaded, 16 * len(load))
            link(dve.tensor_tensor(centred[:, :, :], square[:, :, :], bc(weight, 1, shape), ALU.mult))
            link(dve.tensor_tensor(out if residual is None else square[:, :, :], centred[:, :, :], bc(shift, 1, shape), ALU.add))
            if residual is not None:
                link(dve.tensor_tensor(residual, residual, square[:, :, :], ALU.add))

        @block.scalar
        def _(act):
            act.wait_ge(var_done, 1)
            act.activation(root[:, :], stat[:, :], ACT.Sqrt).then_inc(root_done, 1)


def turn(nc, r, src, out, scale=None, back=False, store=None):
    groups = [(b, min(4, NB - b)) for b in range(0, NB, 4)]
    with Memory(nc) as mem:
        scaled = mem.sb("scaled", [P, NP]) if scale is not None else None
        ps = [mem.ps(f"turned{k}") for k in range(2)]
        scale_done, turned, copied, stored = map(mem.sem, ("scale_done", "turned", "copied", "stored"))
        block = mem.block()
        source = scaled[:, :] if scale is not None else src
        if len(source.shape) == 3:
            source = source.rearrange("p b f -> p (b f)")
        if len(out.shape) == 3:
            out = out.rearrange("p b f -> p (b f)")

        @block.tensor
        def _(pe):
            for n, (b, width) in enumerate(groups):
                if scale is not None:
                    pe.wait_ge(scale_done, n + 1)
                if n >= 2:
                    pe.wait_ge(copied, n - 1)
                for j in range(width):
                    last = pe.transpose(ps[n % 2][:, j * P:(j + 1) * P], source[:, (b + j) * P:(b + j + 1) * P], r.ident[:, :])
                last.then_inc(turned, 1)

        @block.scalar
        def _(act):
            for n, (b, width) in enumerate(groups):
                act.wait_ge(turned, n + 1)
                act.activation(out[:, b * P:(b + width) * P], ps[n % 2][:, 0:width * P], ACT.Copy).then_inc(copied, 1)

        @block.vector
        def _(dve):
            if scale is not None:
                for b, width in groups:
                    part = slice(b * P, (b + width) * P)
                    dve.tensor_tensor(scaled[:, part], src[:, part], scale[:, part], ALU.mult).then_inc(scale_done, 1)

        @block.sync
        def _(sp):
            if store is not None:
                for n, (b, width) in enumerate(groups):
                    sp.wait_ge(copied, n + 1)
                    sp.dma_start(store[b * P:(b + width) * P, :].rearrange("(b p) f -> p b f", p=P),
                                 out[:, b * P:(b + width) * P].rearrange("p (b f) -> p b f", f=P)).then_inc(stored, 16)
                sp.wait_ge(stored, 16 * len(groups))


def project(nc, left, right, out, load=(), add=None, stores=()):
    width = right[0].shape[1]
    with Memory(nc) as mem:
        ps = [mem.ps(f"product{k}") for k in range(4)]
        loaded, multiplied, copied, stored = map(mem.sem, ("loaded", "multiplied", "copied", "stored"))
        block = mem.block()

        @block.sync
        def _(sp):
            for to, of in load:
                sp.dma_start(to, of).then_inc(loaded, 16)
            n = 0
            for b0 in range(0, NB, 5):
                sp.wait_ge(copied, b0 + 5)
                for to, of in stores:
                    sp.dma_start(to(b0, b0 + 5), of(b0, b0 + 5)).then_inc(stored, 16)
                    n += 1
            if n:
                sp.wait_ge(stored, 16 * n)

        @block.tensor
        def _(pe):
            if load:
                pe.wait_ge(loaded, 16 * len(load))
            for b in range(NB):
                if b >= 4:
                    pe.wait_ge(copied, b - 3)
                for n, (lhs, rhs) in enumerate(zip(left, right)):
                    last = pe.matmul(ps[b % 4][:, 0:width], lhs[:, b * P:(b + 1) * P], rhs, start=n == 0, stop=n == len(left) - 1)
                last.then_inc(multiplied, 1)

        @block.vector
        def _(dve):
            if load:
                dve.wait_ge(loaded, 16 * len(load))
            for b in range(NB):
                dve.wait_ge(multiplied, b + 1)
                if add is None:
                    dve.tensor_copy(out[:, b, :], ps[b % 4][:, 0:width]).then_inc(copied, 1)
                else:
                    dve.tensor_tensor(out[:, b, :], ps[b % 4][:, 0:width], add(b), ALU.add).then_inc(copied, 1)


def rows_of(table):
    return lambda lo, hi: table[lo * P:hi * P, :].rearrange("(b p) f -> p b f", p=P)


def edge_buffers(mem, r, transposed):
    b = Names()
    b.hot = mem.two("hot", [P, G, W])
    b.hot_done, b.seg_done, b.acc_done, b.unit_done, b.part_done = map(mem.sem, ("hot_done", "seg_done", "acc_done", "unit_done", "part_done"))
    if transposed:
        b.hot_t = mem.two("hot_t", [W, G * P])
        b.turn_done, b.copy_done, b.look_done = map(mem.sem, ("turn_done", "copy_done", "look_done"))
        b.win_in = [mem.sem(f"win_in{k}") for k in range(2)]
        b.ps_t = mem.ps("ps_t", [W, G * P])
    return b


def make_hot(dve, r, b, m, k, step, hot=None, used=None, made=None):
    hot, used, made = hot or b.hot, used or b.seg_done, made or b.hot_done
    dve.wait_ge(used, free(step))
    rel = r.rel[:, bass.ds(m, 1), :].rearrange("p o g -> p (o g)")
    dve.tensor_tensor(hot[k][:, :, :], bc(r.window[:, :], 1, [P, G, W]), bc(rel, 2, [P, G, W]),
                      ALU.is_equal).then_inc(made, 1)


def turn_hot(pe, r, b, k, step, hot=None, made=None):
    pe.wait_ge(made or b.hot_done, done(step))
    pe.wait_ge(b.copy_done, prev_done(step))
    for j in range(G):
        last = pe.transpose(b.ps_t[:, j * P:(j + 1) * P], (hot or b.hot)[k][:, j, :], r.ident[:, :])
    last.then_inc(b.turn_done, 1)


def copy_hot(act, b, k, step):
    act.wait_ge(b.turn_done, done(step))
    act.wait_ge(b.look_done, free(step))
    act.activation(b.hot_t[k][:, :], b.ps_t[:, :], ACT.Copy).then_inc(b.copy_done, 1)


def load_window(sp, r, b, table, to, m, k, step, q):
    base = load_base(sp, r, m, q)
    sp.wait_ge(b.look_done, free(step))
    sp.dma_start(to[k], table[bass.ds(base, W), :]).then_inc(b.win_in[k], 16)


def load_base(engine, r, m, q):
    return engine.value_load(r.base[0:1, bass.ds(q * M + m, 1)], min_val=0, max_val=NP)


def passes_loop(engine, r, credits, stages, each_pass=None, cycles=False, each_cycle=None):
    which = 1 if cycles else 0
    count = engine.value_load(r.passes[0:1, which:which + 1], min_val=1, max_val=PASS_MAX)
    for semaphore in credits:
        engine.sem_inc(semaphore, 2)

    def passes(n0):
        with engine.Fori(0, count) as q:
            n = q if n0 is None else engine.snap(n0 + q)
            pairs, steps = engine.snap(n * (M // 2)), engine.snap(n * M)

            def tick(t, k, i):
                for lag, stage in stages:
                    if i is None:
                        m = t - lag
                        if 0 <= m < M:
                            stage(m, m % 2, pairs + m // 2, steps + m, q)
                    else:
                        m, par = i * 2 + (k - lag), (k - lag) % 2
                        stage(m, par, pairs + (i + (k - lag - par) // 2), steps + m, q)
            tick(0, 0, None)
            tick(1, 1, None)
            with engine.Fori(1, M // 2) as i:
                for k in range(2):
                    tick(None, k, i)
            if max(lag for lag, _ in stages):
                tick(M, 0, None)
                tick(M + 1, 1, None)
            if each_pass is not None:
                each_pass(n, q)
    if not cycles:
        passes(None)
        return
    rounds = engine.value_load(r.passes[0:1, 2:3], min_val=1, max_val=2)
    with engine.Fori(0, rounds) as c:
        passes(engine.snap(c * count))
        if each_cycle is not None:
            each_cycle(c)


def gather_rows(pool, rows, table, idx, rows_in, ticket):
    pool.sem_inc(ticket, 1)
    for j in range(G):
        pool.indirect_dma_start(rows[:, j, :], None, table, bass.IndirectOffsetOnAxis(idx[:, j:j + 1], 0)).then_inc(rows_in, 16)


def move_window(dve, r, moved, q):
    dve.tensor_scalar(r.window[:, :], r.window[:, :], float(W), None, ALU.add).then_inc(moved, 1)
    dve.wait_ge(moved, q + 2)


def start_window(dve, r, moved):
    dve.tensor_copy(r.window[:, :], r.iota_w[:, :]).then_inc(moved, 1)
    dve.wait_ge(moved, 1)


def attention_edges(nc, d, r):
    with Memory(nc) as mem:
        b = edge_buffers(mem, r, True)
        turned_hot = mem.two("turned_hot", [P, G, W])
        idx = mem.two("idx", [P, G], I32)
        kv = mem.two("kv", [P, G, 2 * P])
        q_win = mem.two("q_win", [W, P])
        prod = mem.sb("prod", [P, G * H0, P // H0])
        score = mem.sb("score", [P, G, H0])
        clipped = mem.two("clipped", [P, G, H0])
        weight = mem.two("weight", [P, G, Z0])
        msg = mem.two("msg", [P, G, P])
        ps_q = mem.ps("ps_q", [P, G * P])
        ps_s = [mem.ps(f"ps_s{k}") for k in range(2)]
        ps_z = [mem.ps(f"ps_z{k}") for k in range(2)]
        idx_in = [mem.sem(f"idx_in{k}") for k in range(2)]
        rows_in = [mem.sem(f"rows_in{k}") for k in range(2)]
        turned_hot_done, prod_done, sum_done, clip_done, exp_done, msg_done, ticket, moved, ones_set, cleared = map(
            mem.sem, ("turned_hot_done", "prod_done", "sum_done", "clip_done", "exp_done", "msg_done", "ticket", "moved", "ones_set", "cleared"))
        block = mem.block()

        @block.sync
        def _(sp):
            def load(m, k, pair, step, q):
                sp.wait_ge(prod_done, free(step))
                sp.dma_start(idx[k][:, :], d["src"][:, bass.ds(m * G, G)]).then_inc(idx_in[k], 16)
                load_window(sp, r, b, d["q_table"], [w[:, :] for w in q_win], m, k, step, q)
            passes_loop(sp, r, (), [(0, load)])

        @block.gpsimd
        def _(pool):
            def gather(m, k, pair, step, q):
                pool.wait_ge(idx_in[k], pair * 16 + 16)
                pool.wait_ge(msg_done, free(step))
                gather_rows(pool, kv[k], d["kv_table"], idx[k], rows_in[k], ticket)
            passes_loop(pool, r, (), [(0, gather)])

        @block.vector
        def _(dve):
            for k in range(2):
                dve.memset(weight[k][:, :, H0:Z0], 1.0).then_inc(ones_set, 1)
            dve.memset(r.acc[:, :], 0.0).then_inc(cleared, 1)
            dve.memset(r.z[:, :], 0.0).then_inc(cleared, 1)
            dve.wait_ge(cleared, 2)
            start_window(dve, r, moved)

            def hot_to_turn(m, k, pair, step, q):
                make_hot(dve, r, b, m, k, step, turned_hot, b.turn_done, turned_hot_done)

            def hot(m, k, pair, step, q):
                make_hot(dve, r, b, m, k, step, b.hot, b.seg_done, b.hot_done)

            def messages(m, k, pair, step, q):
                dve.wait_ge(b.look_done, done(step))
                dve.wait_ge(rows_in[k], (pair * 16 + 16) * G)
                dve.tensor_tensor(prod[:, :, :], kv[k][:, :, 0:P].rearrange("p g (h c) -> p g h c", h=H0),
                                  ps_q[:, :].rearrange("p (g h c) -> p g h c", g=G, h=H0), ALU.mult).then_inc(prod_done, 1)
                dve.wait_ge(prod_done, done(step))
                dve.tensor_reduce(score[:, :, :].rearrange("p g h -> p (g h)"), prod[:, :, :], AX.X, ALU.add).then_inc(sum_done, 1)
                dve.wait_ge(sum_done, done(step))
                dve.tensor_scalar(clipped[k][:, :, :], score[:, :, :], 20.0, -20.0, ALU.min, ALU.max).then_inc(clip_done, 1)
                dve.wait_ge(exp_done, done(step))
                dve.tensor_tensor(msg[k][:, :, :].rearrange("p g (h c) -> p g h c", h=H0),
                                  kv[k][:, :, P:2 * P].rearrange("p g (h c) -> p g h c", h=H0),
                                  weight[k][:, :, 0:H0].unsqueeze(3).to_broadcast([P, G, H0, P // H0]), ALU.mult).then_inc(msg_done, 1)

            def accumulate(m, k, pair, step, q):
                base = load_base(dve, r, m, q)
                dve.wait_ge(b.seg_done, done(step))
                dve.wait_ge(b.acc_done, prev_done(step))
                z = r.z[0:Z0, bass.ds(base, W)]
                dve.tensor_tensor(z, z, ps_z[k][0:Z0, 0:W], ALU.add)
                a = r.acc[:, bass.ds(base, W)]
                dve.tensor_tensor(a, a, ps_s[k][:, 0:W], ALU.add).then_inc(b.acc_done, 1)
            passes_loop(dve, r, (b.hot_done, turned_hot_done, prod_done, sum_done, clip_done, msg_done, b.acc_done),
                        [(0, hot_to_turn), (1, messages), (1, hot), (2, accumulate)], lambda n, q: move_window(dve, r, moved, n))

        @block.scalar
        def _(act):
            act.wait_ge(ones_set, 2)

            def copy(m, k, pair, step, q):
                copy_hot(act, b, k, step)

            def exps(m, k, pair, step, q):
                act.wait_ge(clip_done, done(step))
                act.wait_ge(b.seg_done, free(step))
                act.activation(weight[k][:, :, 0:H0], clipped[k][:, :, :], ACT.Exp, scale=0.25).then_inc(exp_done, 1)
            passes_loop(act, r, (b.copy_done, exp_done), [(0, copy), (1, exps)])

        @block.tensor
        def _(pe):
            def turn(m, k, pair, step, q):
                turn_hot(pe, r, b, k, step, turned_hot, turned_hot_done)

            def look_up(m, k, pair, step, q):
                pe.wait_ge(b.copy_done, done(step))
                pe.wait_ge(b.win_in[k], pair * 16 + 16)
                pe.wait_ge(prod_done, prev_done(step))
                for j in range(G):
                    last = pe.matmul(ps_q[:, j * P:(j + 1) * P], b.hot_t[k][:, j * P:(j + 1) * P], q_win[k][:, :], start=True, stop=True)
                last.then_inc(b.look_done, 1)

            def sums(m, k, pair, step, q):
                pe.wait_ge(msg_done, done(step))
                pe.wait_ge(b.hot_done, done(step))
                pe.wait_ge(b.acc_done, free(step))
                for j in range(G):
                    pe.matmul(ps_s[k][:, 0:W], msg[k][:, j, :], b.hot[k][:, j, :], start=j == 0, stop=j == G - 1)
                for j in range(G):
                    last = pe.matmul(ps_z[k][0:Z0, 0:W], weight[k][:, j, :], b.hot[k][:, j, :], start=j == 0, stop=j == G - 1)
                last.then_inc(b.seg_done, 1)
            passes_loop(pe, r, (b.turn_done, b.look_done, b.seg_done), [(0, turn), (2, sums), (0, look_up)])


def attention_nodes(nc, d, r, mem0):
    with Memory(nc) as mem:
        head_rows, count_rows = mem.sb("head_rows", [Z0, P]), mem.sb("count_rows", [Z0, P])
        inv = mem.two("inv", [P, CHUNK])
        cnt = mem.two("cnt", [P, CHUNK])
        ps_h = [mem.ps(f"ps_h{k}") for k in range(2)]
        ps_c = [mem.ps(f"ps_c{k}") for k in range(2)]
        made, multiplied, order, inv_done, root_done = map(mem.sem, ("made", "multiplied", "order", "inv_done", "root_done"))
        block = mem.block()

        @block.gpsimd
        def _(pool):
            pool.memset(head_rows[:, :], 1.0).then_inc(made, 1)
            pool.memset(count_rows[:, :], 1.0).then_inc(made, 1)
            pool.wait_ge(made, 2)
            pool.affine_select(out=head_rows[:, :], in_=head_rows[:, :], compare_op=ALU.is_ge, fill=0.0, base=0,
                               pattern=[[1, P]], channel_multiplier=-(P // H0)).then_inc(made, 1)
            pool.wait_ge(made, 3)
            pool.affine_select(out=head_rows[:, :], in_=head_rows[:, :], compare_op=ALU.is_ge, fill=0.0, base=P // H0 - 1,
                               pattern=[[-1, P]], channel_multiplier=P // H0).then_inc(made, 1)
            pool.affine_select(out=count_rows[:, :], in_=count_rows[:, :], compare_op=ALU.is_ge, fill=0.0, base=-H0,
                               pattern=[[0, P]], channel_multiplier=1).then_inc(made, 1)

        @block.tensor
        def _(pe):
            pe.wait_ge(made, 5)
            for n, (lo, width) in enumerate(chunks()):
                if n >= 2:
                    pe.wait_ge(inv_done, n - 1)
                pe.matmul(ps_h[n % 2][:, 0:width], head_rows[:, :], r.z[0:Z0, lo:lo + width], start=True, stop=True)
                pe.matmul(ps_c[n % 2][:, 0:width], count_rows[:, :], r.z[0:Z0, lo:lo + width], start=True, stop=True).then_inc(multiplied, 1)

        @block.vector
        def _(dve):
            link = chain(dve, order)
            for n, (lo, width) in enumerate(chunks()):
                k, part = n % 2, slice(lo, lo + width)
                dve.wait_ge(multiplied, n + 1)
                dve.tensor_scalar(cnt[k][:, 0:width], ps_c[k][:, 0:width], 1.0, None, ALU.max)
                link(dve.tensor_scalar(inv[k][:, 0:width], ps_h[k][:, 0:width], 1e-6, None, ALU.add))
                dve.sem_inc(inv_done, 1)
                link(dve.reciprocal(inv[k][:, 0:width], inv[k][:, 0:width]))
                dve.tensor_tensor(r.attn[:, part], r.acc[:, part], inv[k][:, 0:width], ALU.mult)
                link(dve.reciprocal(r.inv_count[:, part], cnt[k][:, 0:width]))
            dve.sem_inc(root_done, 1)

        @block.scalar
        def _(act):
            act.wait_ge(root_done, 1)
            act.activation(r.root_count[:, :], r.inv_count[:, :], ACT.Sqrt)


def hidden(nc, r, src, weights, bias, out):
    with Memory(nc) as mem:
        ps = [mem.ps(f"ps{k}") for k in range(4)]
        multiplied, copied = map(mem.sem, ("multiplied", "copied"))
        block = mem.block()
        parts = [(half, lo, width) for lo, width in chunks() for half in range(2)]

        @block.tensor
        def _(pe):
            for n, (half, lo, width) in enumerate(parts):
                if n >= 4:
                    pe.wait_ge(copied, n - 3)
                pe.matmul(ps[n % 4][:, 0:width], weights[:, half * P:(half + 1) * P], src[:, lo:lo + width], start=True, stop=True).then_inc(multiplied, 1)

        @block.scalar
        def _(act):
            for n, (half, lo, width) in enumerate(parts):
                act.wait_ge(multiplied, n + 1)
                act.activation(out[half][:, lo:lo + width], ps[n % 4][:, 0:width], ACT.Relu, bias=bias[:, half:half + 1]).then_inc(copied, 1)


def attention_layer(nc, d, r):
    with Memory(nc) as mem:
        w = mem.sb("w_qkv", [P, 3 * P])
        out = mem.sb("kvq", [P, NB, 3 * P])
        project(nc, [r.ht], [w[:, :]], out, load=[(w[:, 0:P], d["l0_wk"]), (w[:, P:2 * P], d["l0_wv"]), (w[:, 2 * P:3 * P], d["l0_wq"])],
                stores=[(rows_of(d["kv_table"]), lambda lo, hi: out[:, lo:hi, 0:2 * P]),
                        (rows_of(d["q_table"]), lambda lo, hi: out[:, lo:hi, 2 * P:3 * P])])
    attention_edges(nc, d, r)
    with Memory(nc) as mem:
        r.attn = mem.sb("attn", [P, NP])
        attention_nodes(nc, d, r, mem)
        w_o, x1, sums = mem.sb("w_o", [P, P]), mem.sb("x1", [P, NB, P]), None
        rows = mem.sb("rows", [P, 6, P])
        w_1, w_2, bias = mem.sb("w_1", [P, 2 * P]), mem.sb("w_2", [P, 2, P]), mem.sb("bias", [P, 2])
        ready = mem.sem("ready")
        load = [(rows[:, n, :], v.partition_broadcast(P)) for n, v in
                enumerate((d["l0_bo"], d["l0_ln1_g"], d["l0_ln1_b"], d["l0_b2"], d["l0_ln2_g"], d["l0_ln2_b"]))]
        load += [(w_o[:, :], d["l0_wo"]), (w_1[:, :], d["l0_w1"]), (w_2[:, :, :], d["l0_w2"]), (bias[:, :], d["l0_b1"])]
        add_rows(nc, r.h, rows[:, 0, :], load)
        project(nc, [r.attn], [w_o[:, :]], x1, add=lambda b: r.h[:, b, :])
        normalise(nc, r, x1[:, :, :], x1[:, :, :], weight=rows[:, 1, :], shift=rows[:, 2, :])
        turn(nc, r, x1[:, :, :], r.ht[:, :])
        hid = mem.two("hid", [P, NP])
        hidden(nc, r, r.ht, w_1, bias, hid)
        add_rows(nc, x1, rows[:, 3, :])
        project(nc, hid, [w_2[:, 0, :], w_2[:, 1, :]], x1, add=lambda b: x1[:, b, :])
        normalise(nc, r, x1[:, :, :], None, weight=rows[:, 4, :], shift=rows[:, 5, :], residual=r.x[:, :, :])


def add_rows(nc, to, row, load=()):
    with Memory(nc) as mem:
        loaded = mem.sem("loaded")
        added = mem.sem("added")
        block = mem.block()

        @block.sync
        def _(sp):
            for out, of in load:
                sp.dma_start(out, of).then_inc(loaded, 16)
            if load:
                sp.wait_ge(loaded, 16 * len(load))

        @block.vector
        def _(dve):
            if load:
                dve.wait_ge(loaded, 16 * len(load))
            dve.tensor_tensor(to[:, :, :], to[:, :, :], bc(row, 1, [P, NB, P]), ALU.add).then_inc(added, 1)
            dve.wait_ge(added, 1)


def mean_edges(nc, d, r, w_e):
    with Memory(nc) as mem:
        b = edge_buffers(mem, r, False)
        idx = mem.two("idx", [P, G], I32)
        rows = mem.two("rows", [P, G, P])
        attr = mem.two("attr", [3, G * P])
        pre = mem.two("pre", [P, G, P])
        msg = mem.two("msg", [P, G, P])
        ps_e = [mem.ps(f"ps_e{k}", [P, G * P]) for k in range(2)]
        ps_s = [mem.ps(f"ps_s{k}") for k in range(2)]
        idx_in = [mem.sem(f"idx_in{k}") for k in range(2)]
        rows_in = [mem.sem(f"rows_in{k}") for k in range(2)]
        attr_in = [mem.sem(f"attr_in{k}") for k in range(2)]
        edge_done, pre_done, msg_done, ticket, moved, cleared = map(
            mem.sem, ("edge_done", "pre_done", "msg_done", "ticket", "moved", "cleared"))
        block = mem.block()

        @block.sync
        def _(sp):
            def load(m, k, pair, step, q):
                sp.wait_ge(pre_done, free(step))
                sp.dma_start(idx[k][:, :], d["src"][:, bass.ds(m * G, G)]).then_inc(idx_in[k], 16)
                sp.dma_start(attr[k][:, :], d["edge_attr"][:, bass.ds(m * (G * P), G * P)]).then_inc(attr_in[k], 16)
            passes_loop(sp, r, (), [(0, load)])

        @block.gpsimd
        def _(pool):
            def gather(m, k, pair, step, q):
                pool.wait_ge(idx_in[k], pair * 16 + 16)
                pool.wait_ge(pre_done, free(step))
                gather_rows(pool, rows[k], d["row_table"], idx[k], rows_in[k], ticket)
            passes_loop(pool, r, (), [(0, gather)])

        @block.tensor
        def _(pe):
            def edges(m, k, pair, step, q):
                pe.wait_ge(attr_in[k], pair * 16 + 16)
                pe.wait_ge(pre_done, free(step))
                for j in range(G):
                    last = pe.matmul(ps_e[k][:, j * P:(j + 1) * P], attr[k][:, j * P:(j + 1) * P], w_e[:, :], start=True, stop=True)
                last.then_inc(edge_done, 1)

            def sums(m, k, pair, step, q):
                pe.wait_ge(msg_done, done(step))
                pe.wait_ge(b.hot_done, done(step))
                pe.wait_ge(b.acc_done, free(step))
                for j in range(G):
                    last = pe.matmul(ps_s[k][:, 0:W], msg[k][:, j, :], b.hot[k][:, j, :], start=j == 0, stop=j == G - 1)
                last.then_inc(b.seg_done, 1)
            passes_loop(pe, r, (edge_done, b.seg_done), [(0, edges), (1, sums)])

        @block.vector
        def _(dve):
            dve.memset(r.acc[:, :], 0.0).then_inc(cleared, 1)
            dve.wait_ge(cleared, 1)
            start_window(dve, r, moved)

            def hot(m, k, pair, step, q):
                make_hot(dve, r, b, m, k, step)

            def leaky(m, k, pair, step, q):
                dve.wait_ge(edge_done, done(step))
                dve.wait_ge(rows_in[k], (pair * 16 + 16) * G)
                dve.tensor_tensor(pre[k][:, :, :], rows[k][:, :, :], ps_e[k][:, :].rearrange("p (g f) -> p g f", g=G), ALU.add).then_inc(pre_done, 1)
                dve.wait_ge(pre_done, done(step))
                dve.wait_ge(b.seg_done, free(step))
                dve.scalar_tensor_tensor(msg[k][:, :, :], pre[k][:, :, :], 0.01, pre[k][:, :, :], ALU.mult, ALU.max).then_inc(msg_done, 1)

            def accumulate(m, k, pair, step, q):
                add_window(dve, r, b, ps_s[k][:, 0:W], r.acc, m, step, q)
            passes_loop(dve, r, (b.hot_done, pre_done, msg_done, b.acc_done), [(0, hot), (1, leaky), (2, accumulate)],
                        lambda n, q: move_window(dve, r, moved, n))


def add_window(dve, r, b, sums, to, m, step, q):
    base = load_base(dve, r, m, q)
    dve.wait_ge(b.seg_done, done(step))
    dve.wait_ge(b.acc_done, prev_done(step))
    part = to[0:sums.shape[0], bass.ds(base, W)]
    dve.tensor_tensor(part, part, sums, ALU.add).then_inc(b.acc_done, 1)


def combine(nc, terms, out):
    with Memory(nc) as mem:
        order = mem.sem("order")
        block = mem.block()

        @block.vector
        def _(dve):
            terms(dve, chain(dve, order))


def mean_layer(nc, d, r):
    with Memory(nc) as mem:
        w_x, w_e, w_2 = mem.sb("w_x", [P, P]), mem.sb("w_e", [3, P]), mem.sb("w_2", [P, 2, P])
        rows, out = mem.sb("rows", [P, 2, P]), mem.sb("out", [P, NB, P])
        project(nc, [r.ht], [w_x[:, :]], out,
                load=[(w_x[:, :], d["l1_w1"][0:P, :]), (w_e[:, :], d["l1_w1"][P:P + 3, :]), (w_2[:, :, :], d["l1_w2"]),
                      (rows[:, 0, :], d["l1_b1"].partition_broadcast(P)), (rows[:, 1, :], d["l1_b2"].partition_broadcast(P))],
                add=lambda b: rows[:, 0, :], stores=[(rows_of(d["row_table"]), lambda lo, hi: out[:, lo:hi, :])])
        mean_edges(nc, d, r, w_e)
        mean = mem.sb("mean", [P, NP])

        def divide(dve, link):
            link(dve.tensor_tensor(mean[:, :], r.acc[:, 0:NP], r.inv_count[:, :], ALU.mult))
        combine(nc, divide, None)
        project(nc, [r.ht, mean], [w_2[:, 0, :], w_2[:, 1, :]], out, add=lambda b: rows[:, 1, :])

        def finish(dve, link):
            link(dve.scalar_tensor_tensor(r.x[:, :, :], out[:, :, :], 0.0, r.x[:, :, :], ALU.max, ALU.add))
        combine(nc, finish, None)


def sum_edges(nc, d, r):
    with Memory(nc) as mem:
        b = edge_buffers(mem, r, False)
        idx = mem.two("idx", [P, G], I32)
        rows = mem.two("rows", [P, G, P])
        ps_s = [mem.ps(f"ps_s{k}") for k in range(2)]
        idx_in = [mem.sem(f"idx_in{k}") for k in range(2)]
        rows_in = [mem.sem(f"rows_in{k}") for k in range(2)]
        ticket, moved, cleared = map(mem.sem, ("ticket", "moved", "cleared"))
        block = mem.block()

        @block.sync
        def _(sp):
            def load(m, k, pair, step, q):
                sp.wait_ge(b.seg_done, free(step))
                sp.dma_start(idx[k][:, :], d["src"][:, bass.ds(m * G, G)]).then_inc(idx_in[k], 16)
            passes_loop(sp, r, (), [(0, load)])

        @block.gpsimd
        def _(pool):
            def gather(m, k, pair, step, q):
                pool.wait_ge(idx_in[k], pair * 16 + 16)
                pool.wait_ge(b.seg_done, free(step))
                gather_rows(pool, rows[k], d["row_table"], idx[k], rows_in[k], ticket)
            passes_loop(pool, r, (), [(0, gather)])

        @block.tensor
        def _(pe):
            def sums(m, k, pair, step, q):
                pe.wait_ge(b.hot_done, done(step))
                pe.wait_ge(b.acc_done, free(step))
                pe.wait_ge(rows_in[k], (pair * 16 + 16) * G)
                for j in range(G):
                    last = pe.matmul(ps_s[k][:, 0:W], rows[k][:, j, :], b.hot[k][:, j, :], start=j == 0, stop=j == G - 1)
                last.then_inc(b.seg_done, 1)
            passes_loop(pe, r, (b.seg_done,), [(0, sums)])

        @block.vector
        def _(dve):
            dve.memset(r.acc[:, :], 0.0).then_inc(cleared, 1)
            dve.wait_ge(cleared, 1)
            start_window(dve, r, moved)

            def hot(m, k, pair, step, q):
                make_hot(dve, r, b, m, k, step)

            def accumulate(m, k, pair, step, q):
                add_window(dve, r, b, ps_s[k][:, 0:W], r.acc, m, step, q)
            passes_loop(dve, r, (b.hot_done, b.acc_done), [(0, hot), (1, accumulate)],
                        lambda n, q: move_window(dve, r, moved, n))


def chebyshev_layer(nc, d, r):
    with Memory(nc) as mem:
        w = mem.sb("w", [P, 4, P])
        t = [r.ht] + [mem.sb(f"t{k}", [P, NP]) for k in range(1, 4)]
        out = mem.sb("out", [P, NB, P])
        for k in range(1, 4):
            turn(nc, r, t[k - 1], out[:, :, :], scale=r.root_count, store=d["row_table"])
            sum_edges(nc, d, r)

            def recur(dve, link):
                link(dve.tensor_tensor(t[k][:, :], r.acc[:, 0:NP], r.root_count[:, :], ALU.mult))
                if k > 1:
                    link(dve.scalar_tensor_tensor(t[k][:, :], t[k][:, :], 2.0, t[k - 2][:, :], ALU.mult, ALU.subtract))
            combine(nc, recur, None)
        project(nc, t, [w[:, k, :] for k in range(4)], r.x, load=[(w[:, :, :], d["l2_w"])], add=lambda b: r.x[:, b, :])


def relation_select(dve, r, values, picked, m, step, sem_done, sem_sum, tmp):
    hot = r.type_hot[:, bass.ds(m * G, G), :]
    dve.tensor_tensor(tmp[:, :, :, :], values.rearrange("p g (r h) -> p g h r", r=R),
                      hot.unsqueeze(2).to_broadcast([P, G, H3, R]), ALU.mult).then_inc(sem_done, 1)
    dve.wait_ge(sem_done, done(step))
    dve.tensor_reduce(picked[:, :, :], tmp[:, :, :, :], AX.X, ALU.add).then_inc(sem_sum, 1)
    dve.wait_ge(sem_sum, done(step))


def relation_scores(nc, d, r):
    with Memory(nc) as mem:
        b = edge_buffers(mem, r, True)
        idx = mem.two("idx", [P, G], I32)
        rows = mem.two("rows", [P, G, ROW])
        win = mem.two("win", [W, RH + 1])
        tmp = mem.sb("tmp", [P, G, H3, R])
        picked, total, slope, gated = (mem.sb(n, [P, G, H3]) for n in ("picked", "total", "slope", "gated"))
        placed, rest = mem.sb("placed", [P, G, RH]), mem.sb("rest", [P, G, RH])
        tagged = mem.two("tagged", [P, G, TAG], BF16)
        tagged_t = mem.two("tagged_t", [TAG, G * P], BF16)
        spread = mem.sb("spread", [TAG, GW, P], BF16)
        ident16 = mem.sb("ident16", [P, P], BF16)
        gwin = mem.sb("gwin", [P, GW * GN])
        best = mem.two("best", [P, GW, G])
        top = mem.two("top", [P, GX])
        top_rows = mem.sb("top_rows", [P, 4, P])
        ps_q = mem.ps("ps_q")
        look = ps_q[:, 0:G * (RH + 1)].rearrange("p (g c) -> p g c", g=G)
        ps_b = [mem.ps(f"ps_b{k}", [TAG, G * P], BF16) for k in range(2)]
        ps_m = [mem.ps(f"ps_m{n}") for n in range(GW)]
        idx_in = [mem.sem(f"idx_in{k}") for k in range(2)]
        rows_in = [mem.sem(f"rows_in{k}") for k in range(2)]
        spill_out = [mem.sem(f"spill_out{k}") for k in range(2)]
        (mul_done, pick_done, add_done, slope_done, gate_done, e_done, tag_done, tag_turn_done, tag_copy_done, max_done,
         best_done, spill_done, ticket, moved, gmoved, cleared, ones_set, made, top_ready, top_turned, top_copied, stored) = map(
            mem.sem, ("mul_done", "pick_done", "add_done", "slope_done", "gate_done", "e_done", "tag_done", "tag_turn_done",
                      "tag_copy_done", "max_done", "best_done", "spill_done", "ticket", "moved", "gmoved", "cleared",
                      "ones_set", "made", "top_ready", "top_turned", "top_copied", "stored"))
        reset_done, pe_ticket, split_done = map(mem.sem, ("reset_done", "pe_ticket", "split_done"))
        block = mem.block()

        @block.sync
        def _(sp):
            sp.wait_ge(ones_set, 2)

            def load(m, k, pair, step, q):
                sp.wait_ge(add_done, free(step))
                sp.dma_start(idx[k][:, :], d["key"][:, bass.ds(m * G, G)]).then_inc(idx_in[k], 16)
                load_window(sp, r, b, d["ed_table"], [w[:, 0:RH] for w in win], m, k, step, q)

            def spill(m, k, pair, step, q):
                sp.wait_ge(rows_in[k], (pair * 16 + 16) * G)
                sp.dma_start(d["spill"][bass.ds(m * P, P), :], rows[k][:, :, :].rearrange("p g f -> p (g f)")).then_inc(spill_out[k], 16)

            def confirm(m, k, pair, step, q):
                sp.wait_ge(spill_out[k], pair * 16 + 16)
                sp.sem_inc(spill_done, 1)
            passes_loop(sp, r, (spill_done,), [(0, load), (2, confirm), (1, spill)], cycles=True)
            sp.wait_ge(top_copied, 4)
            for n in range(4):
                width = min(P, NG - n * P)
                sp.dma_start(d["top_table"][n * P * GN:(n * P + width) * GN, :].rearrange("(g a) c -> g (a c)", a=GN), top_rows[0:width, n, :]).then_inc(stored, 16)
            sp.wait_ge(stored, 64)

        @block.gpsimd
        def _(pool):
            pool.memset(spread[:, :, :], 0.0).then_inc(made, 1)
            pool.wait_ge(made, 1)
            view = spread[:, :, :].rearrange("t g (a c) -> t g a c", c=RH)
            pool.affine_select(out=view, in_=view, compare_op=ALU.not_equal, fill=-BIG, base=0,
                               pattern=[[GN, GW], [1, GN], [0, RH]], channel_multiplier=-1).then_inc(made, 1)
            for n in range(PARTS):
                pool.wait_ge(made, n + 2)
                pool.affine_select(out=view, in_=view, compare_op=ALU.not_equal, fill=1.0, base=GW * GN + n * RH,
                                   pattern=[[0, GW], [0, GN], [1, RH]], channel_multiplier=-1).then_inc(made, 1)

            def gather(m, k, pair, step, q):
                pool.wait_ge(idx_in[k], pair * 16 + 16)
                pool.wait_ge(add_done, free(step))
                pool.wait_ge(spill_done, free(step))
                gather_rows(pool, rows[k], d["h_table"], idx[k], rows_in[k], ticket)
            passes_loop(pool, r, (), [(0, gather)], cycles=True)

        @block.scalar
        def _(act):
            def copy_tags(m, k, pair, step, q):
                act.wait_ge(tag_turn_done, done(step))
                act.wait_ge(max_done, free(step))
                act.activation(tagged_t[k][:, :], ps_b[k][:, :], ACT.Copy).then_inc(tag_copy_done, 1)
            passes_loop(act, r, (b.copy_done, tag_copy_done),
                        [(0, lambda m, k, pair, step, q: copy_hot(act, b, k, step)), (1, copy_tags)], cycles=True)
            act.wait_ge(top_turned, 1)
            for n in range(4):
                width = min(P, NG - n * P)
                act.activation(top_rows[0:width, n, :], ps_q[0:width, n * P:(n + 1) * P], ACT.Copy).then_inc(top_copied, 1)

        @block.tensor
        def _(pe):
            pe.wait_ge(made, PARTS + 2)
            pe.wait_ge(cleared, 4)

            def turn_tags(m, k, pair, step, q):
                pe.wait_ge(tag_done, done(step))
                pe.wait_ge(tag_copy_done, free(step))
                pe.sem_inc(pe_ticket, 1)
                for j in range(G):
                    last = pe.transpose(ps_b[k][:, j * P:(j + 1) * P], tagged[k][:, j, :], ident16[:, :])
                last.then_inc(tag_turn_done, 1)

            def turn(m, k, pair, step, q):
                turn_hot(pe, r, b, k, step)

            def look_up(m, k, pair, step, q):
                pe.wait_ge(b.copy_done, done(step))
                pe.wait_ge(b.win_in[k], pair * 16 + 16)
                pe.wait_ge(gate_done, prev_done(step))
                for j in range(G):
                    last = pe.matmul(look[:, j, :], b.hot_t[k][:, j * P:(j + 1) * P], win[k][:, :], start=True, stop=True)
                last.then_inc(b.look_done, 1)

            def spread_tags(m, k, pair, step, q):
                pe.wait_ge(tag_copy_done, done(step))
                first = pe.snap(step * (2 * GW))
                for half in range(2):
                    for g in range(GW):
                        pe.wait_ge(best_done, first + (half * GW + g + 1))
                        last = pe.matmul(ps_m[g][:, :], spread[:, g, :], tagged_t[k][:, half * CHUNK:(half + 1) * CHUNK], start=True, stop=True)
                        last.then_inc(b.unit_done, 1)
                pe.wait_ge(b.unit_done, first + 2 * GW)
                pe.sem_inc(max_done, 1)
            passes_loop(pe, r, (b.turn_done, b.look_done, tag_turn_done, max_done), [(0, turn), (2, spread_tags), (0, look_up), (1, turn_tags)], cycles=True)
            pe.wait_ge(top_ready, 1)
            for n in range(4):
                width = min(P, NG - n * P)
                last = pe.transpose(ps_q[0:width, n * P:(n + 1) * P], top[0][:, n * P:n * P + width], r.ident[:, :])
            last.then_inc(top_turned, 1)

        @block.vector
        def _(dve):
            for k in range(2):
                dve.memset(win[k][:, RH:RH + 1], 1.0).then_inc(ones_set, 1)
            dve.memset(r.e[:, :, :], 0.0).then_inc(cleared, 1)
            for k in range(2):
                dve.memset(top[k][:, :], 0.0).then_inc(cleared, 1)
            dve.tensor_copy(ident16[:, :], r.ident[:, :]).then_inc(cleared, 1)
            dve.wait_ge(cleared, 4)
            dve.sem_inc(best_done, GW)
            dve.sem_inc(b.part_done, 2 * G)
            dve.tensor_copy(gwin[:, :], r.iota_g[:, :]).then_inc(gmoved, 1)
            dve.wait_ge(gmoved, 1)
            start_window(dve, r, moved)

            def hot(m, k, pair, step, q):
                dve.wait_ge(b.turn_done, free(step))
                rel = r.rel[:, bass.ds(m, 1), :].rearrange("p o g -> p (o g)")
                dve.tensor_tensor(b.hot[k][:, :, :], bc(r.window[:, :], 1, [P, G, W]), bc(rel, 2, [P, G, W]),
                                  ALU.is_equal).then_inc(b.hot_done, 1)
                dve.wait_ge(tag_turn_done, free(step))
                rel = r.group_rel[:, bass.ds(m * G, G)]
                dve.tensor_tensor(tagged[k][:, :, 0:GW * GN], bc(gwin[:, :], 1, [P, G, GW * GN]),
                                  bc(rel, 2, [P, G, GW * GN]), ALU.not_equal)

            def scores(m, k, pair, step, q):
                dve.wait_ge(b.look_done, done(step))
                relation_select(dve, r, look[:, :, 0:RH], picked, m, step, mul_done, pick_done, tmp)
                dve.wait_ge(rows_in[k], (pair * 16 + 16) * G)
                dve.tensor_tensor(total[:, :, :], rows[k][:, :, P:ROW], picked[:, :, :], ALU.add).then_inc(add_done, 1)
                dve.wait_ge(add_done, done(step))
                dve.scalar_tensor_tensor(slope[:, :, :], total[:, :, :], 0.2, total[:, :, :], ALU.mult, ALU.max).then_inc(slope_done, 1)
                dve.wait_ge(slope_done, done(step))
                dve.tensor_tensor(gated[:, :, :], slope[:, :, :], look[:, :, RH:RH + 1].to_broadcast([P, G, H3]), ALU.mult).then_inc(gate_done, 1)
                dve.wait_ge(gate_done, done(step))
                dve.wait_ge(e_done, prev_done(step))
                e = r.e[:, bass.ds(m * G, G), :]
                dve.tensor_tensor(e, e, gated[:, :, :], ALU.add).then_inc(e_done, 1)
                dve.wait_ge(e_done, done(step))
                dve.tensor_tensor(placed[:, :, :].rearrange("p g (r h) -> p g r h", r=R),
                                  bc(r.type_hot[:, bass.ds(m * G, G), :], 3, [P, G, R, H3]),
                                  bc(e, 2, [P, G, R, H3]), ALU.mult).then_inc(split_done, 1)
                hi, mid, lo = (tagged[k][:, :, GW * GN + n * RH:GW * GN + (n + 1) * RH] for n in range(PARTS))
                dve.wait_ge(split_done, step * 4 + 1)
                dve.tensor_copy(hi, placed[:, :, :]).then_inc(split_done, 1)
                dve.wait_ge(split_done, step * 4 + 2)
                dve.tensor_tensor(mid, placed[:, :, :], hi, ALU.subtract).then_inc(split_done, 1)
                dve.tensor_tensor(rest[:, :, :], placed[:, :, :], hi, ALU.subtract).then_inc(split_done, 1)
                dve.wait_ge(split_done, step * 4 + 4)
                dve.tensor_tensor(lo, rest[:, :, :], mid, ALU.subtract).then_inc(tag_done, 1)

            def maxima(k, step, half):
                first = dve.snap(step * (2 * GW) + half * GW)
                for g in range(GW):
                    dve.wait_ge(b.unit_done, first + (g + 1))
                    dve.tensor_reduce(best[k][:, g, half * HALF:half * HALF + HALF], ps_m[g][:, :].rearrange("p (g e) -> p g e", g=HALF), AX.X, ALU.max).then_inc(best_done, 1)

            def half_maxima(m, k, step, q, half):
                _, groups = nc.values_load_multi_w_load_instructions(r.tile_group[0:1, bass.ds(m * G + half * HALF, HALF)],
                                                                     engines=[mybir.EngineType.DVE], min_val=0, max_val=NG - 1)
                if half == 0:
                    dve.wait_ge(b.part_done, step * G + G)
                maxima(k, step, half)
                shift = dve.snap(q * GW)
                dve.wait_ge(best_done, dve.snap(step * (2 * GW)) + (2 + half) * GW)
                for j in range(half * HALF, (half + 1) * HALF):
                    dve.wait_ge(b.part_done, step * G + (2 * G + j - 1))
                    part = top[j % 2][:, bass.ds(groups[j - half * HALF] + shift, GW)]
                    dve.tensor_tensor(part, part, best[k][:, :, j], ALU.max).then_inc(b.part_done, 1)

            def first_maxima(m, k, pair, step, q):
                half_maxima(m, k, step, q, 0)

            def last_maxima(m, k, pair, step, q):
                half_maxima(m, k, step, q, 1)
            passes_loop(dve, r, (b.hot_done, mul_done, pick_done, add_done, slope_done, gate_done, e_done, tag_done),
                        [(0, hot), (2, first_maxima), (1, scores), (2, last_maxima)],
                        each_pass=lambda n, q: (move_window(dve, r, moved, n),
                                                dve.tensor_scalar(gwin[:, :], gwin[:, :], float(GW * GN), None, ALU.add).then_inc(gmoved, 1),
                                                dve.wait_ge(gmoved, n + 2)), cycles=True,
                        each_cycle=lambda c: (dve.tensor_copy(gwin[:, :], r.iota_g[:, :]).then_inc(reset_done, 1),
                                              dve.wait_ge(reset_done, c + 1)))
            dve.tensor_tensor(top[0][:, :], top[0][:, :], top[1][:, :], ALU.max).then_inc(top_ready, 1)


def relation_edges(nc, d, r):
    with Memory(nc) as mem:
        b = edge_buffers(mem, r, True)
        rows = mem.two("rows", [P, G, ROW])
        msg = mem.two("msg", [P, G, P])
        typed = mem.two("typed", [P, G, R * W])
        win = mem.two("win", [W, RH + 1])
        tmp = mem.sb("tmp", [P, G, H3, R])
        picked, less = (mem.sb(n, [P, G, H3]) for n in ("picked", "less"))
        gated, power = mem.two("gated", [P, G, H3]), mem.two("power", [P, G, H3])
        placed = mem.two("placed", [P, G, R, H3])
        typed_window = mem.sb("typed_window", [P, R * W])
        ps_q = mem.ps("ps_q")
        look = ps_q[:, 0:G * (RH + 1)].rearrange("p (g c) -> p g c", g=G)
        ps_s = [mem.ps(f"ps_s{k}") for k in range(2)]
        ps_z = [mem.ps(f"ps_z{k}") for k in range(2)]
        rows_in = [mem.sem(f"rows_in{k}") for k in range(2)]
        (mul_done, pick_done, less_done, gate_done, exp_done, typed_done, place_done, msg_done, z_done, moved, tmoved, cleared, ones_set) = map(
            mem.sem, ("mul_done", "pick_done", "less_done", "gate_done", "exp_done", "typed_done", "place_done", "msg_done", "z_done",
                      "moved", "tmoved", "cleared", "ones_set"))
        block = mem.block()

        @block.sync
        def _(sp):
            sp.wait_ge(ones_set, 2)

            def load(m, k, pair, step, q):
                sp.wait_ge(msg_done, free(step))
                sp.dma_start(rows[k][:, :, :].rearrange("p g f -> p (g f)"), d["spill"][bass.ds(m * P, P), :]).then_inc(rows_in[k], 16)
                load_window(sp, r, b, d["top_table"], [w[:, 0:RH] for w in win], m, k, step, q)
            passes_loop(sp, r, (), [(0, load)])

        @block.scalar
        def _(act):
            def exps(m, k, pair, step, q):
                act.wait_ge(gate_done, done(step))
                act.wait_ge(msg_done, free(step))
                act.activation(power[k][:, :, :], gated[k][:, :, :], ACT.Exp).then_inc(exp_done, 1)
            passes_loop(act, r, (b.copy_done, exp_done), [(1, exps), (0, lambda m, k, pair, step, q: copy_hot(act, b, k, step))])

        @block.tensor
        def _(pe):
            def turn(m, k, pair, step, q):
                turn_hot(pe, r, b, k, step)

            def look_up(m, k, pair, step, q):
                pe.wait_ge(b.copy_done, done(step))
                pe.wait_ge(b.win_in[k], pair * 16 + 16)
                pe.wait_ge(gate_done, prev_done(step))
                for j in range(G):
                    last = pe.matmul(look[:, j, :], b.hot_t[k][:, j * P:(j + 1) * P], win[k][:, :], start=True, stop=True)
                last.then_inc(b.look_done, 1)

            def add_messages(k, tiles):
                for j in tiles:
                    last = pe.matmul(ps_s[k][:, 0:R * W], msg[k][:, j, :], typed[k][:, j, :], start=j == 0, stop=j == G - 1)
                return last

            def first_sums(m, k, pair, step, q):
                pe.wait_ge(place_done, done(step))
                pe.wait_ge(b.acc_done, free(step))
                for j in range(G):
                    last = pe.matmul(ps_z[k][0:RH, 0:W], placed[k][:, j, :, :].rearrange("p r h -> p (r h)"), b.hot[k][:, j, :], start=j == 0, stop=j == G - 1)
                last.then_inc(z_done, 1)
                pe.wait_ge(msg_done, done(step))
                pe.wait_ge(typed_done, done(step))
                add_messages(k, range(G // 2))

            def last_sums(m, k, pair, step, q):
                add_messages(k, range(G // 2, G)).then_inc(b.seg_done, 1)
            passes_loop(pe, r, (b.turn_done, b.look_done, z_done, b.seg_done), [(2, first_sums), (0, turn), (2, last_sums), (0, look_up)])

        @block.vector
        def _(dve):
            for k in range(2):
                dve.memset(win[k][:, RH:RH + 1], 1.0).then_inc(ones_set, 1)
            dve.memset(r.z[:, :], 0.0).then_inc(cleared, 1)
            dve.memset(r.acc4[:, :, :], 0.0).then_inc(cleared, 1)
            dve.wait_ge(cleared, 2)
            start_window(dve, r, moved)
            for n in range(R):
                dve.tensor_scalar(typed_window[:, n * W:(n + 1) * W], r.iota_w[:, :], float(n * KIND), None, ALU.add).then_inc(tmoved, 1)
            dve.wait_ge(tmoved, R)

            def hot(m, k, pair, step, q):
                make_hot(dve, r, b, m, k, step, used=z_done)

            def typed_hot(m, k, pair, step, q):
                dve.wait_ge(b.seg_done, free(step))
                for j in range(G):
                    last = dve.tensor_scalar(typed[k][:, j, :], typed_window[:, :], r.typed_rel[:, bass.ds(m * G + j, 1)], None, ALU.is_equal)
                last.then_inc(typed_done, 1)

            def scores(m, k, pair, step, q):
                dve.wait_ge(b.look_done, done(step))
                relation_select(dve, r, look[:, :, 0:RH], picked, m, step, mul_done, pick_done, tmp)
                dve.tensor_tensor(less[:, :, :], r.e[:, bass.ds(m * G, G), :], picked[:, :, :], ALU.subtract).then_inc(less_done, 1)
                dve.wait_ge(less_done, done(step))
                dve.tensor_tensor(gated[k][:, :, :], less[:, :, :], look[:, :, RH:RH + 1].to_broadcast([P, G, H3]), ALU.mult).then_inc(gate_done, 1)

            def messages(m, k, pair, step, q):
                dve.wait_ge(exp_done, done(step))
                dve.wait_ge(b.seg_done, free(step))
                dve.tensor_tensor(placed[k][:, :, :, :], bc(r.type_hot[:, bass.ds(m * G, G), :], 3, [P, G, R, H3]),
                                  bc(power[k][:, :, :], 2, [P, G, R, H3]), ALU.mult).then_inc(place_done, 1)
                dve.wait_ge(rows_in[k], pair * 16 + 16)
                dve.tensor_tensor(msg[k][:, :, :].rearrange("p g (h c) -> p g h c", h=H3),
                                  rows[k][:, :, 0:P].rearrange("p g (h c) -> p g h c", h=H3),
                                  power[k][:, :, :].unsqueeze(3).to_broadcast([P, G, H3, P // H3]), ALU.mult).then_inc(msg_done, 1)

            def accumulate(m, k, pair, step, q):
                base = load_base(dve, r, m, q)
                dve.wait_ge(b.seg_done, done(step))
                dve.wait_ge(b.acc_done, prev_done(step))
                z = r.z[0:RH, bass.ds(base, W)]
                dve.tensor_tensor(z, z, ps_z[k][0:RH, 0:W], ALU.add)
                a = r.acc4[:, :, bass.ds(base, W)]
                dve.tensor_tensor(a, a, ps_s[k][:, 0:R * W].rearrange("p (r w) -> p r w", r=R), ALU.add).then_inc(b.acc_done, 1)
            passes_loop(dve, r, (b.hot_done, mul_done, pick_done, less_done, gate_done, typed_done, place_done, msg_done, b.acc_done),
                        [(0, hot), (1, typed_hot), (1, scores), (1, messages), (2, accumulate)],
                        each_pass=lambda n, q: (move_window(dve, r, moved, n),
                                                dve.tensor_scalar(typed_window[:, :], typed_window[:, :], float(W), None, ALU.add).then_inc(tmoved, 1),
                                                dve.wait_ge(tmoved, n + (R + 1))))


def relation_nodes(nc, d, r, out, rows, load):
    with Memory(nc) as mem:
        head_rows = mem.sb("head_rows", [RH, R, P])
        inv, inv_t = mem.sb("inv", [P, NB * RH]), mem.sb("inv_t", [RH, NP])
        hb = mem.sb("hb", [P, NB, P])
        ps_z = mem.ps("ps_z")
        ps_t = mem.ps("ps_t")
        ps_i = [mem.ps(f"ps_i{k}") for k in range(3)]
        ps_o = [mem.ps(f"ps_o{k}") for k in range(3)]
        loaded, made, turned, order, inv_ready, back, copied, spread_done, scaled, summed, stored, hb_done = map(
            mem.sem, ("loaded", "made", "turned", "order", "inv_ready", "back", "copied", "spread_done", "scaled", "summed", "stored", "hb_done"))
        block = mem.block()
        parts = [(lo, width, n) for lo, width in chunks() for n in range(R)]
        blocks4 = [(b, min(4, NB - b)) for b in range(0, NB, 4)]

        @block.sync
        def _(sp):
            for to, of in load:
                sp.dma_start(to, of).then_inc(loaded, 16)
            sp.wait_ge(loaded, 16 * len(load))

        @block.gpsimd
        def _(pool):
            pool.memset(head_rows[:, :, :], 0.0).then_inc(made, 1)
            pool.wait_ge(made, 1)
            view = head_rows[:, :, :].rearrange("c n (h f) -> c n h f", h=H3)
            pool.affine_select(out=view, in_=view, compare_op=ALU.not_equal, fill=1.0, base=0,
                               pattern=[[H3, R], [1, H3], [0, P // H3]], channel_multiplier=-1).then_inc(made, 1)
            pool.wait_ge(loaded, 16 * len(load))
            pool.tensor_tensor(hb[:, :, :], r.h[:, :, :], bc(rows[:, 0, :], 1, [P, NB, P]), ALU.add).then_inc(hb_done, 1)

        @block.tensor
        def _(pe):
            for b in range(NB):
                last = pe.transpose(ps_z[:, b * RH:(b + 1) * RH], r.z[0:RH, b * P:(b + 1) * P], r.ident[0:RH, 0:RH])
            last.then_inc(turned, 1)
            pe.wait_ge(inv_ready, 1)
            for n, (b, width) in enumerate(blocks4):
                if n:
                    pe.wait_ge(copied, n)
                for j in range(width):
                    last = pe.transpose(ps_t[0:RH, j * P:(j + 1) * P], inv[:, (b + j) * RH:(b + j + 1) * RH], r.ident[:, :])
                last.then_inc(back, 1)
            pe.wait_ge(copied, len(blocks4))
            pe.wait_ge(made, 2)

            def spread(u):
                lo, width, n = parts[u]
                if u >= 3:
                    pe.wait_ge(scaled, u - 2)
                pe.matmul(ps_i[u % 3][:, 0:width], head_rows[:, n, :], inv_t[:, lo:lo + width], start=True, stop=True).then_inc(spread_done, 1)

            def collect(n):
                b, width = blocks4[n]
                pe.wait_ge(scaled, R * (n + 1))
                if n >= 3:
                    pe.wait_ge(summed, n - 2)
                for j in range(width):
                    for k in range(R):
                        last = pe.matmul(ps_o[n % 3][:, j * P:(j + 1) * P], r.acc4[:, k, (b + j) * P:(b + j + 1) * P], r.ident[:, :], start=k == 0, stop=k == R - 1)
                last.then_inc(stored, 1)
            for n in range(len(blocks4)):
                for k in range(R):
                    spread(n * R + k)
                if n:
                    collect(n - 1)
            collect(len(blocks4) - 1)

        @block.scalar
        def _(act):
            for n, (b, width) in enumerate(blocks4):
                act.wait_ge(back, n + 1)
                act.activation(inv_t[:, b * P:(b + width) * P], ps_t[0:RH, 0:width * P], ACT.Copy).then_inc(copied, 1)

        @block.vector
        def _(dve):
            link = chain(dve, order)
            dve.wait_ge(turned, 1)
            link(dve.tensor_scalar(inv[:, :], ps_z[:, 0:NB * RH], 1e-8, None, ALU.add))
            link(dve.reciprocal(inv[:, :], inv[:, :]))
            dve.sem_inc(inv_ready, 1)

            def take(n):
                b, width = blocks4[n]
                dve.wait_ge(stored, n + 1)
                dve.tensor_tensor(out[:, b:b + width, :].rearrange("p b f -> p (b f)"), ps_o[n % 3][:, 0:width * P],
                                  hb[:, b:b + width, :].rearrange("p b f -> p (b f)"), ALU.add).then_inc(summed, 1)
            dve.wait_ge(hb_done, 1)
            for u, (lo, width, n) in enumerate(parts):
                dve.wait_ge(spread_done, u + 1)
                a = r.acc4[:, n, lo:lo + width]
                dve.tensor_tensor(a, a, ps_i[u % 3][:, 0:width], ALU.mult).then_inc(scaled, 1)
                if n == R - 1 and u >= 2 * R - 1:
                    take(u // R - 1)
            take(len(blocks4) - 1)


def relation_layer(nc, d, r):
    with Memory(nc) as mem:
        w, attn = mem.sb("w", [P, R * P]), mem.sb("attn", [P, 2, R * P])
        w_a = mem.sb("w_a", [P, 2 * RH])
        tmp = mem.sb("tmp", [P, R * P])
        load = [(w[:, :], d["l3_w"])] + [(attn[:, n, :], v.partition_broadcast(P)) for n, v in enumerate((d["l3_attn_src"], d["l3_attn_dst"]))]
        with Memory(nc) as inner:
            loaded, order = inner.sem("loaded"), inner.sem("order")
            block = inner.block()

            @block.sync
            def _(sp):
                for to, of in load:
                    sp.dma_start(to, of).then_inc(loaded, 16)

            @block.vector
            def _(dve):
                link = chain(dve, order)
                dve.wait_ge(loaded, 48)
                for n in range(2):
                    link(dve.tensor_tensor(tmp[:, :], w[:, :], attn[:, n, :], ALU.mult))
                    link(dve.tensor_reduce(w_a[:, n * RH:(n + 1) * RH], tmp[:, :].rearrange("p (c k) -> p c k", k=P // H3), AX.X, ALU.add))
        with Memory(nc) as inner:
            out = inner.sb("out", [P, NB, R, ROW])
            ea = inner.sb("ea", [P, NB, RH])
            relation_tables(nc, d, r, w, w_a, out, ea)
    with Memory(nc) as mem:
        r.e = mem.sb("e", [P, T, H3])
        relation_scores(nc, d, r)
        relation_edges(nc, d, r)
    with Memory(nc) as mem:
        rows, out = mem.sb("rows", [P, 3, P]), mem.sb("out", [P, NB, P])
        relation_nodes(nc, d, r, out, rows, [(rows[:, n, :], v.partition_broadcast(P)) for n, v in
                                             enumerate((d["l3_bias"], d["l3_ln_gamma"], d["l3_ln_beta"]))])
        normalise(nc, r, out[:, :, :], None, weight=rows[:, 1, :], shift=rows[:, 2, :], residual=r.x[:, :, :])


def relation_tables(nc, d, r, w, w_a, out, ea):
    with Memory(nc) as mem:
        ps = [mem.ps(f"ps{k}") for k in range(3)]
        ps_a = [mem.ps(f"ps_a{k}") for k in range(3)]
        multiplied, copied, copied_a, stored = map(mem.sem, ("multiplied", "copied", "copied_a", "stored"))
        block = mem.block()

        @block.tensor
        def _(pe):
            for b in range(NB):
                if b >= 3:
                    pe.wait_ge(copied, b - 2)
                    pe.wait_ge(copied_a, b - 2)
                lhs = r.ht[:, b * P:(b + 1) * P]
                pe.matmul(ps[b % 3][:, :], lhs, w[:, :], start=True, stop=True)
                pe.matmul(ps_a[b % 3][:, 0:2 * RH], lhs, w_a[:, :], start=True, stop=True).then_inc(multiplied, 1)

        @block.scalar
        def _(act):
            for b in range(NB):
                act.wait_ge(multiplied, b + 1)
                act.activation(out[:, b, :, 0:P], ps[b % 3][:, :].rearrange("p (r f) -> p r f", r=R), ACT.Copy).then_inc(copied, 1)

        @block.vector
        def _(dve):
            for b in range(NB):
                dve.wait_ge(multiplied, b + 1)
                dve.tensor_copy(ea[:, b, :], ps_a[b % 3][:, RH:2 * RH])
                dve.tensor_copy(out[:, b, :, P:ROW], ps_a[b % 3][:, 0:RH].rearrange("p (r h) -> p r h", r=R)).then_inc(copied_a, 1)

        @block.sync
        def _(sp):
            n = 0
            for b in range(0, NB, 5):
                sp.wait_ge(copied, b + 5)
                sp.wait_ge(copied_a, b + 5)
                for k in range(R):
                    sp.dma_start(d["h_table"][k * NP + b * P:k * NP + (b + 5) * P, :].rearrange("(b p) f -> p b f", p=P),
                                 out[:, b:b + 5, k, :]).then_inc(stored, 16)
                    n += 1
            sp.dma_start(rows_of(d["ed_table"])(0, NB), ea[:, :, :]).then_inc(stored, 16)
            sp.wait_ge(stored, 16 * (n + 1))


def build(nc, d):
    r = Names()
    with Memory(nc) as mem:
        r.x = mem.sb("x_nodes", [P, NB, P])
        r.h = mem.sb("h_nodes", [P, NB, P])
        r.acc4 = mem.sb("acc4", [P, R, NX])
        r.acc = r.acc4[:, 0, :]
        r.ht = r.acc4[:, 1, 0:NP]
        r.inv_count = r.acc4[:, 2, 0:NP]
        r.root_count = r.acc4[:, 3, 0:NP]
        r.z = mem.sb("z", [RH, NX])
        r.rel = mem.sb("rel", [P, M, G])
        r.group_rel = mem.sb("group_rel", [P, T])
        r.type_hot = mem.sb("type_hot", [P, T, R])
        r.iota_w = mem.sb("iota_w", [P, W])
        r.iota_g = mem.sb("iota_g", [P, GW * GN])
        r.iota_r = mem.sb("iota_r", [P, R])
        r.window = mem.sb("window", [P, W])
        r.ident = mem.sb("ident", [P, P])
        r.typed_rel = mem.sb("typed_rel", [P, T])
        r.passes = mem.sb("passes", [P, 3], I32)
        r.base = mem.sb("base", [1, BASE_ROWS * M], I16)
        r.tile_group = mem.sb("tile_group", [1, T], I32)
        before = nc.snapshot_sems()
        prepare(nc, d, r)
        for layer in (attention_layer, mean_layer, chebyshev_layer, relation_layer):
            normalise(nc, r, r.x[:, :, :], r.h[:, :, :], relu=True)
            turn(nc, r, r.h[:, :, :], r.ht[:, :])
            layer(nc, d, r)
            nc.clear_and_free_semaphores(nc.allocated_since(before))
            nc.all_engine_barrier()
            before = nc.snapshot_sems()
        stored = mem.sem("out_stored")
        block = mem.block()

        @block.sync
        def _(sp):
            sp.dma_start(d["out"], r.x[:, :, :]).then_inc(stored, 16)
            sp.wait_ge(stored, 16)


def kernel(**inputs):
    import concourse.bacc as bacc
    from concourse.bass_utils import run_bass_kernel_spmd

    nc = bacc.Bacc("TRN2", target_bir_lowering=False, num_devices=1)
    d = {}
    arrays = {}

    def put(name, a):
        a = np.ascontiguousarray(a)
        arrays["in_" + name] = a
        d[name] = nc.dram_tensor("in_" + name, a.shape, mybir.dt.from_np(a.dtype), kind="ExternalInput").ap()

    def by_tile(a, value):
        return np.pad(np.asarray(a), (0, EP - E), constant_values=value).reshape(T, P).T

    g = {k: np.asarray(v) for k, v in inputs.items()}
    put("x", np.pad(g["x"], ((0, NP - N), (0, 0))).reshape(NB, P, P).transpose(1, 0, 2))
    put("src", by_tile(g["src"], 0))
    put("dst", by_tile(g["dst"], FAR))
    put("edge_type", by_tile(g["edge_type_4"], 0))
    put("dst_sorted", np.pad(g["dst"], (0, EP - E), mode="edge"))
    put("edge_attr", np.pad(g["edge_attr_3"], ((0, EP - E), (0, 0))).T)
    for name in ("Wq", "Wk", "Wv", "Wo", "bo", "ln1_g", "ln1_b", "W1", "b2", "ln2_g", "ln2_b"):
        put("l0_" + name.lower(), g["L0_gnn_" + name])
    put("l0_b1", g["L0_gnn_b1"].reshape(2, P).T)
    put("l0_w2", g["L0_gnn_W2"].reshape(2, P, P).transpose(1, 0, 2))
    put("l1_w1", g["L1_gnn_W1"].T)
    put("l1_w2", g["L1_gnn_W2"].T.reshape(2, P, P).transpose(1, 0, 2))
    put("l1_b1", g["L1_gnn_b1"])
    put("l1_b2", g["L1_gnn_b2"])
    put("l2_w", g["L2_gnn_weights"].transpose(1, 0, 2))
    put("l3_w", g["L3_gnn_W"].transpose(1, 0, 2).reshape(P, R * P))
    put("l3_attn_src", g["L3_gnn_attn_src"].reshape(-1))
    put("l3_attn_dst", g["L3_gnn_attn_dst"].reshape(-1))
    for name in ("bias", "ln_gamma", "ln_beta"):
        put("l3_" + name, g["L3_gnn_" + name])
    for name, shape, dtype in (("macro_bounds", [2 * M], I32), ("tile_bounds", [2 * T], I32), ("key", [P, T], I32),
                               ("kv_table", [NP, 2 * P], F32), ("q_table", [NX, P], F32), ("row_table", [NP, P], F32),
                               ("h_table", [R * NP, ROW], F32), ("spill", [M * P, G * ROW], F32), ("base_table", [BASE_ROWS * M], I16), ("ed_table", [NX, RH], F32),
                               ("top_table", [NX, RH], F32)):
        d[name] = nc.dram_tensor(name, shape, dtype).ap()
    d["out"] = nc.dram_tensor("out", (P, NB, P), F32, kind="ExternalOutput").ap()
    build(nc, d)
    res = run_bass_kernel_spmd(nc, [arrays], core_ids=[0])
    return res.results[0]["out"].transpose(1, 0, 2).reshape(NP, P)[:N]
```

```python
import numpy as np
from contextlib import ExitStack
import concourse.bass as bass
from concourse import mybir

F32, BF16, I32, I16 = mybir.dt.float32, mybir.dt.bfloat16, mybir.dt.int32, mybir.dt.int16
ALU, ACT, AX = mybir.AluOpType, mybir.ActivationFunctionType, mybir.AxisListType

P = 128
N = 3125
NB = -(-N // P)
NP = NB * P
NX = NP + P
E = 53125
G = 8
W = 96
M = -(-E // (2 * G * P)) * 2
T = M * G
U = T // 2
EP = T * P
Q_MAX = -(-N // W)
H0 = 8
Z0 = H0 + 1
R, H3 = 4, 4
RH = R * H3
HALF = G // 2
GN = 8
GW = 3
NG = NX // GN
GQ_MAX = -(-(-(-N // GN)) // GW)
GX = NG + GW * GQ_MAX + GW
PASS_MAX = GQ_MAX
BASE_ROWS = PASS_MAX + PASS_MAX % 2
ROW = P + H3
PARTS = 3
TAG = GW * GN + PARTS * RH
BIG = 1e30
KIND = 1 << 13
FAR = 1 << 20
CHUNK = 512
EPS = 1e-5


def done(step):
    return step + 3


def prev_done(step):
    return step + 2


def free(step):
    return step + 1


def bc(ap, axis, shape):
    return ap.unsqueeze(axis).to_broadcast(shape)


def chunks():
    return [(lo, min(CHUNK, NP - lo)) for lo in range(0, NP, CHUNK)]


def chain(engine, semaphore):
    n = [0]

    def link(instruction):
        n[0] += 1
        instruction.then_inc(semaphore, 1)
        engine.wait_ge(semaphore, n[0])
    return link


class Names:
    pass


class Memory:

    def __init__(self, nc):
        self.nc, self.stack = nc, ExitStack()
        self.stage = f"{nc.next_id()}"

    def __enter__(self):
        return self

    def __exit__(self, *error):
        return self.stack.__exit__(*error)

    def sb(self, name, shape, dtype=F32):
        return self.stack.enter_context(self.nc.sbuf_tensor(f"{name}_{self.stage}", shape, dtype))

    def two(self, name, shape, dtype=F32):
        return [self.sb(f"{name}{k}", shape, dtype) for k in range(2)]

    def ps(self, name, shape=(P, CHUNK), dtype=F32):
        return self.stack.enter_context(self.nc.psum_tensor(f"{name}_{self.stage}", list(shape), dtype))

    def sem(self, name):
        return self.nc.alloc_semaphore(f"{name}_{self.stage}")

    def block(self):
        return self.stack.enter_context(self.nc.Block())


def prepare(nc, d, r):
    with Memory(nc) as mem:
        macro_dst = mem.sb("macro_dst", [M, G * P], I32)
        pair_dst = mem.sb("pair_dst", [U // 2, 2, 2 * P], I32)
        macro_f = mem.sb("macro_f", [M, 2])
        macro_i = mem.sb("macro_i", [M, 2], I32)
        pair_f = mem.sb("pair_f", [U // 2, 2, 2])
        pair_i = mem.sb("pair_i", [U // 2, 2, 2], I32)
        macro_row = mem.sb("macro_row", [P, M, 2], I32)
        pair_row = mem.sb("pair_row", [P, U, 2], I32)
        macro_rf = mem.sb("macro_rf", [P, M, 2])
        pair_rf = mem.sb("pair_rf", [P, U, 2])
        span = mem.sb("span", [P, M])
        gspan = mem.sb("gspan", [P, U])
        widest = mem.sb("widest", [P, 2])
        offset = mem.sb("offset", [BASE_ROWS // 2, 2])
        offset_lo = mem.sb("offset_lo", [BASE_ROWS // 2, 2, M])
        base_rows = mem.sb("base_rows", [BASE_ROWS // 2, 2, M], I16)
        steps = mem.sb("steps", [P, Q_MAX])
        gsteps = mem.sb("gsteps", [P, GQ_MAX])
        count = mem.sb("count", [P, 3])
        dst_f = mem.sb("dst_f", [P, T])
        src_f = mem.sb("src_f", [P, T])
        type_f = mem.sb("type_f", [P, T])
        dst_i = mem.sb("dst_i", [P, T], I32)
        src_i = mem.sb("src_i", [P, T], I32)
        type_i = mem.sb("type_i", [P, T], I32)
        key_i = mem.sb("key_i", [P, T], I32)
        iota_p = mem.sb("iota_p", [P, P])
        iota_q = mem.sb("iota_q", [P, 1])
        zero = mem.sb("zero", [P, P])
        loaded, order, extremes, stored, back, iotas, key_done, zero_done, bases_made, base_out = map(
            mem.sem, ("loaded", "order", "extremes", "stored", "back", "iotas", "key_done", "zero_done", "bases_made", "base_out"))
        block = mem.block()

        @block.sync
        def _(sp):
            sp.dma_start(macro_dst[:, :], d["dst_sorted"].rearrange("(m e) -> m e", m=M)).then_inc(loaded, 16)
            sp.dma_start(pair_dst[:, :, :], d["dst_sorted"].rearrange("(a b e) -> a b e", b=2, e=2 * P)).then_inc(loaded, 16)
            sp.dma_start(dst_i[:, :], d["dst"]).then_inc(loaded, 16)
            sp.dma_start(src_i[:, :], d["src"]).then_inc(loaded, 16)
            sp.dma_start(type_i[:, :], d["edge_type"]).then_inc(loaded, 16)
            sp.dma_start(r.x[:, :, :], d["x"]).then_inc(loaded, 16)
            sp.wait_ge(zero_done, 1)
            for table in (d["q_table"], d["ed_table"]):
                width = table.shape[1]
                sp.dma_start(table[NP:NX, :], zero[:, 0:width]).then_inc(stored, 16)
            sp.wait_ge(extremes, 1)
            sp.dma_start(d["macro_bounds"].rearrange("(m k) -> m k", k=2), macro_i[:, :]).then_inc(stored, 16)
            sp.dma_start(d["pair_bounds"].rearrange("(a b) -> a b", b=4), pair_i[:, :, :].rearrange("a b k -> a (b k)")).then_inc(stored, 16)
            sp.wait_ge(stored, 64)
            sp.dma_start(macro_row[:, :, :].rearrange("p m k -> p (m k)"), d["macro_bounds"].partition_broadcast(P)).then_inc(back, 16)
            sp.dma_start(pair_row[:, :, :].rearrange("p t k -> p (t k)"), d["pair_bounds"].partition_broadcast(P)).then_inc(back, 16)
            sp.wait_ge(bases_made, 1)
            sp.dma_start(d["base_table"].rearrange("(p k) -> p k", p=BASE_ROWS // 2), base_rows[:, :, :].rearrange("p j m -> p (j m)")).then_inc(base_out, 16)
            sp.wait_ge(base_out, 16)
            sp.dma_start(r.base[:, :], d["base_table"].unsqueeze(0)).then_inc(base_out, 16)
            sp.wait_ge(base_out, 32)
            sp.wait_ge(key_done, 1)
            sp.dma_start(d["key"], key_i[:, :]).then_inc(stored, 16)
            sp.wait_ge(stored, 80)

        @block.gpsimd
        def _(pool):
            for out, step in ((r.iota_w[:, :], 1), (r.iota_g[:, :], 1), (steps[:, :], W), (gsteps[:, :], GW),
                              (r.iota_r[:, :], 1), (iota_p[:, :], 1)):
                pool.iota(out, [[step, out.shape[1]]], base=0, channel_multiplier=0,
                          allow_small_or_imprecise_dtypes=True).then_inc(iotas, 1)
            pool.iota(offset[:, :], [[W, 2]], base=0, channel_multiplier=2 * W,
                      allow_small_or_imprecise_dtypes=True).then_inc(iotas, 1)
            pool.iota(iota_q[:, :], [[0, 1]], base=0, channel_multiplier=1,
                      allow_small_or_imprecise_dtypes=True).then_inc(iotas, 1)

        @block.vector
        def _(dve):
            link = chain(dve, order)
            link(dve.memset(zero[:, :], 0.0))
            dve.sem_inc(zero_done, 1)
            dve.wait_ge(loaded, 96)
            dve.tensor_reduce(macro_f[:, 0:1], macro_dst[:, :], AX.X, ALU.min)
            dve.tensor_reduce(macro_f[:, 1:2], macro_dst[:, :], AX.X, ALU.max)
            dve.tensor_reduce(pair_f[:, :, 0], pair_dst[:, :, :], AX.X, ALU.min)
            link(dve.tensor_reduce(pair_f[:, :, 1], pair_dst[:, :, :], AX.X, ALU.max))
            dve.tensor_copy(macro_i[:, :], macro_f[:, :])
            link(dve.tensor_copy(pair_i[:, :, :], pair_f[:, :, :]))
            link(dve.tensor_scalar(pair_i[:, :, :], pair_i[:, :, :], 3, None, ALU.arith_shift_right))
            dve.sem_inc(extremes, 1)
            dve.tensor_copy(src_f[:, :], src_i[:, :])
            dve.tensor_copy(dst_f[:, :], dst_i[:, :])
            link(dve.tensor_copy(type_f[:, :], type_i[:, :]))
            link(dve.scalar_tensor_tensor(src_f[:, :], type_f[:, :], float(NP), src_f[:, :], ALU.mult, ALU.add))
            link(dve.tensor_copy(key_i[:, :], src_f[:, :]))
            dve.sem_inc(key_done, 1)
            dve.wait_ge(iotas, 8)
            dve.tensor_tensor(r.type_hot[:, :, :], bc(type_f[:, :], 2, [P, T, R]), bc(r.iota_r[:, :], 1, [P, T, R]), ALU.is_equal)
            dve.tensor_scalar(r.ident[:, :], iota_p[:, :], iota_q[:, :], None, ALU.is_equal)
            dve.wait_ge(back, 32)
            dve.tensor_copy(macro_rf[:, :, :], macro_row[:, :, :])
            dve.tensor_copy(r.pair_group[:, :], pair_row[0:1, :, 0])
            link(dve.tensor_copy(pair_rf[:, :, :], pair_row[:, :, :]))
            half = BASE_ROWS // 2
            for j in range(2):
                last = dve.tensor_scalar(offset_lo[:, j, :], macro_rf[0:half, :, 0], offset[:, j:j + 1], float(NP), ALU.add, ALU.min)
            link(last)
            link(dve.tensor_copy(base_rows[:, :, :], offset_lo[:, :, :]))
            dve.sem_inc(bases_made, 1)
            dve.tensor_tensor(r.rel[:, :, :], dst_f[:, :].rearrange("p (m g) -> p m g", g=G),
                              bc(macro_rf[:, :, 0], 2, [P, M, G]), ALU.subtract)
            dve.scalar_tensor_tensor(r.group_rel[:, :].rearrange("p (u a) -> p u a", a=2), bc(pair_rf[:, :, 0], 2, [P, U, 2]), -float(GN),
                                     dst_f[:, :].rearrange("p (u a) -> p u a", a=2), ALU.mult, ALU.add)
            dve.tensor_tensor(span[:, :], macro_rf[:, :, 1], macro_rf[:, :, 0], ALU.subtract)
            link(dve.tensor_tensor(gspan[:, :], pair_rf[:, :, 1], pair_rf[:, :, 0], ALU.subtract))
            dve.tensor_reduce(widest[:, 0:1], span[:, :], AX.X, ALU.max)
            link(dve.tensor_reduce(widest[:, 1:2], gspan[:, :], AX.X, ALU.max))
            dve.tensor_scalar(steps[:, :], steps[:, :], widest[:, 0:1], None, ALU.is_le)
            link(dve.tensor_scalar(gsteps[:, :], gsteps[:, :], widest[:, 1:2], None, ALU.is_le))
            dve.tensor_reduce(count[:, 0:1], steps[:, :], AX.X, ALU.add)
            link(dve.tensor_reduce(count[:, 1:2], gsteps[:, :], AX.X, ALU.add))
            link(dve.tensor_tensor(count[:, 1:2], count[:, 0:1], count[:, 1:2], ALU.max))
            link(dve.tensor_scalar(count[:, 2:3], count[:, 1:2], 1.5, 1.0, ALU.is_gt, ALU.add))
            dve.tensor_copy(r.passes[:, :], count[:, :])
            dve.scalar_tensor_tensor(r.typed_rel[:, :], type_f[:, :], float(KIND), r.rel[:, :, :].rearrange("p m g -> p (m g)"), ALU.mult, ALU.add)


def normalise(nc, r, src, out, relu=False, weight=None, shift=None, residual=None, load=()):
    with Memory(nc) as mem:
        centred, square = mem.sb("centred", [P, NB, P]), mem.sb("square", [P, NB, P])
        total, var, root, inv = (mem.sb(n, [P, NB]) for n in ("total", "var", "root", "inv"))
        order, centre_done, square_done, var_done, root_done, shift_done, loaded = map(
            mem.sem, ("order", "centre_done", "square_done", "var_done", "root_done", "shift_done", "loaded"))
        block = mem.block()
        parts = [slice(b, b + 5) for b in range(0, NB, 5)]

        @block.sync
        def _(sp):
            for to, of in load:
                sp.dma_start(to, of).then_inc(loaded, 16)
            if load:
                sp.wait_ge(loaded, 16 * len(load))

        @block.gpsimd
        def _(pool):
            if residual is not None:
                if load:
                    pool.wait_ge(loaded, 16 * len(load))
                pool.tensor_tensor(residual, residual, bc(shift, 1, [P, NB, P]), ALU.add).then_inc(shift_done, 1)

        @block.vector
        def _(dve):
            link = chain(dve, order)
            link(dve.tensor_reduce(total[:, :], src, AX.X, ALU.add))
            for part in parts:
                dve.scalar_tensor_tensor(centred[:, part, :], bc(total[:, part], 2, [P, 5, P]), -1.0 / P, src[:, part, :],
                                         ALU.mult, ALU.add).then_inc(centre_done, 1)
            for n, part in enumerate(parts):
                dve.wait_ge(square_done, n + 1)
                last = dve.tensor_reduce(var[:, part], square[:, part, :], AX.X, ALU.add)
            link(last)
            link(dve.tensor_scalar(var[:, :], var[:, :], 1.0 / P, EPS, ALU.mult, ALU.add))
            dve.sem_inc(var_done, 1)
            dve.wait_ge(root_done, 1)
            link(dve.reciprocal(inv[:, :], root[:, :]))
            if relu:
                link(dve.scalar_tensor_tensor(out, centred[:, :, :], 0.0, bc(inv[:, :], 2, [P, NB, P]), ALU.max, ALU.mult))
                return
            if load:
                dve.wait_ge(loaded, 16 * len(load))
            for b in range(NB):
                last = dve.scalar_tensor_tensor(square[:, b, :], centred[:, b, :], inv[:, b:b + 1], weight, ALU.mult, ALU.mult)
            link(last)
            if residual is None:
                link(dve.tensor_tensor(out, square[:, :, :], bc(shift, 1, [P, NB, P]), ALU.add))
            else:
                dve.wait_ge(shift_done, 1)
                link(dve.tensor_tensor(residual, residual, square[:, :, :], ALU.add))

        @block.scalar
        def _(act):
            for n, part in enumerate(parts):
                act.wait_ge(centre_done, n + 1)
                act.activation(square[:, part, :], centred[:, part, :], ACT.Square).then_inc(square_done, 1)
            act.wait_ge(var_done, 1)
            act.activation(root[:, :], var[:, :], ACT.Sqrt).then_inc(root_done, 1)


def turn(nc, r, src, out, scale=None, back=False, store=None):
    groups = [(b, min(4, NB - b)) for b in range(0, NB, 4)]
    with Memory(nc) as mem:
        scaled = mem.sb("scaled", [P, NP]) if scale is not None else None
        ps = [mem.ps(f"turned{k}") for k in range(2)]
        scale_done, turned, copied, stored = map(mem.sem, ("scale_done", "turned", "copied", "stored"))
        block = mem.block()
        source = scaled[:, :] if scale is not None else src
        if len(source.shape) == 3:
            source = source.rearrange("p b f -> p (b f)")
        if len(out.shape) == 3:
            out = out.rearrange("p b f -> p (b f)")

        @block.tensor
        def _(pe):
            for n, (b, width) in enumerate(groups):
                if scale is not None:
                    pe.wait_ge(scale_done, n + 1)
                if n >= 2:
                    pe.wait_ge(copied, n - 1)
                for j in range(width):
                    last = pe.transpose(ps[n % 2][:, j * P:(j + 1) * P], source[:, (b + j) * P:(b + j + 1) * P], r.ident[:, :])
                last.then_inc(turned, 1)

        @block.scalar
        def _(act):
            for n, (b, width) in enumerate(groups):
                act.wait_ge(turned, n + 1)
                act.activation(out[:, b * P:(b + width) * P], ps[n % 2][:, 0:width * P], ACT.Copy).then_inc(copied, 1)

        @block.vector
        def _(dve):
            if scale is not None:
                for b, width in groups:
                    part = slice(b * P, (b + width) * P)
                    dve.tensor_tensor(scaled[:, part], src[:, part], scale[:, part], ALU.mult).then_inc(scale_done, 1)

        @block.sync
        def _(sp):
            if store is not None:
                for n, (b, width) in enumerate(groups):
                    sp.wait_ge(copied, n + 1)
                    sp.dma_start(store[b * P:(b + width) * P, :].rearrange("(b p) f -> p b f", p=P),
                                 out[:, b * P:(b + width) * P].rearrange("p (b f) -> p b f", f=P)).then_inc(stored, 16)
                sp.wait_ge(stored, 16 * len(groups))


def project(nc, left, right, out, load=(), add=None, stores=()):
    width = right[0].shape[1]
    with Memory(nc) as mem:
        ps = [mem.ps(f"product{k}") for k in range(4)]
        loaded, multiplied, copied, stored = map(mem.sem, ("loaded", "multiplied", "copied", "stored"))
        block = mem.block()

        @block.sync
        def _(sp):
            for to, of in load:
                sp.dma_start(to, of).then_inc(loaded, 16)
            n = 0
            for b0 in range(0, NB, 5):
                sp.wait_ge(copied, b0 + 5)
                for to, of in stores:
                    sp.dma_start(to(b0, b0 + 5), of(b0, b0 + 5)).then_inc(stored, 16)
                    n += 1
            if n:
                sp.wait_ge(stored, 16 * n)

        @block.tensor
        def _(pe):
            if load:
                pe.wait_ge(loaded, 16 * len(load))
            for b in range(NB):
                if b >= 4:
                    pe.wait_ge(copied, b - 3)
                for n, (lhs, rhs) in enumerate(zip(left, right)):
                    last = pe.matmul(ps[b % 4][:, 0:width], lhs[:, b * P:(b + 1) * P], rhs, start=n == 0, stop=n == len(left) - 1)
                last.then_inc(multiplied, 1)

        @block.vector
        def _(dve):
            if load:
                dve.wait_ge(loaded, 16 * len(load))
            for b in range(NB):
                dve.wait_ge(multiplied, b + 1)
                if add is None:
                    dve.tensor_copy(out[:, b, :], ps[b % 4][:, 0:width]).then_inc(copied, 1)
                else:
                    dve.tensor_tensor(out[:, b, :], ps[b % 4][:, 0:width], add(b), ALU.add).then_inc(copied, 1)


def rows_of(table):
    return lambda lo, hi: table[lo * P:hi * P, :].rearrange("(b p) f -> p b f", p=P)


def edge_buffers(mem, r, transposed):
    b = Names()
    b.hot = mem.two("hot", [P, G, W])
    b.hot_done, b.seg_done, b.acc_done, b.unit_done, b.part_done = map(mem.sem, ("hot_done", "seg_done", "acc_done", "unit_done", "part_done"))
    if transposed:
        b.hot_t = mem.two("hot_t", [W, G * P])
        b.turn_done, b.copy_done, b.look_done = map(mem.sem, ("turn_done", "copy_done", "look_done"))
        b.win_in = [mem.sem(f"win_in{k}") for k in range(2)]
        b.ps_t = mem.ps("ps_t", [W, G * P])
    return b


def make_hot(dve, r, b, m, k, step, hot=None, used=None, made=None):
    hot, used, made = hot or b.hot, used or b.seg_done, made or b.hot_done
    dve.wait_ge(used, free(step))
    rel = r.rel[:, bass.ds(m, 1), :].rearrange("p o g -> p (o g)")
    dve.tensor_tensor(hot[k][:, :, :], bc(r.window[:, :], 1, [P, G, W]), bc(rel, 2, [P, G, W]),
                      ALU.is_equal).then_inc(made, 1)


def turn_hot(pe, r, b, k, step, hot=None, made=None):
    pe.wait_ge(made or b.hot_done, done(step))
    pe.wait_ge(b.copy_done, prev_done(step))
    for j in range(G):
        last = pe.transpose(b.ps_t[:, j * P:(j + 1) * P], (hot or b.hot)[k][:, j, :], r.ident[:, :])
    last.then_inc(b.turn_done, 1)


def copy_hot(act, b, k, step):
    act.wait_ge(b.turn_done, done(step))
    act.wait_ge(b.look_done, free(step))
    act.activation(b.hot_t[k][:, :], b.ps_t[:, :], ACT.Copy).then_inc(b.copy_done, 1)


def load_window(sp, r, b, table, to, m, k, step, q):
    base = load_base(sp, r, m, q)
    sp.wait_ge(b.look_done, free(step))
    sp.dma_start(to[k], table[bass.ds(base, W), :]).then_inc(b.win_in[k], 16)


def load_base(engine, r, m, q):
    return engine.value_load(r.base[0:1, bass.ds(q * M + m, 1)], min_val=0, max_val=NP)


def passes_loop(engine, r, credits, stages, each_pass=None, cycles=False, each_cycle=None):
    which = 1 if cycles else 0
    count = engine.value_load(r.passes[0:1, which:which + 1], min_val=1, max_val=PASS_MAX)
    for semaphore in credits:
        engine.sem_inc(semaphore, 2)

    def passes(n0):
        with engine.Fori(0, count) as q:
            n = q if n0 is None else engine.snap(n0 + q)
            pairs, steps = engine.snap(n * (M // 2)), engine.snap(n * M)

            def tick(t, k, i):
                for lag, stage in stages:
                    if i is None:
                        m = t - lag
                        if 0 <= m < M:
                            stage(m, m % 2, pairs + m // 2, steps + m, q)
                    else:
                        m, par = i * 2 + (k - lag), (k - lag) % 2
                        stage(m, par, pairs + (i + (k - lag - par) // 2), steps + m, q)
            tick(0, 0, None)
            tick(1, 1, None)
            with engine.Fori(1, M // 2) as i:
                for k in range(2):
                    tick(None, k, i)
            if max(lag for lag, _ in stages):
                tick(M, 0, None)
                tick(M + 1, 1, None)
            if each_pass is not None:
                each_pass(n, q)
    if not cycles:
        passes(None)
        return
    rounds = engine.value_load(r.passes[0:1, 2:3], min_val=1, max_val=2)
    with engine.Fori(0, rounds) as c:
        passes(engine.snap(c * count))
        if each_cycle is not None:
            each_cycle(c)


def gather_rows(pool, rows, table, idx, rows_in, ticket):
    pool.sem_inc(ticket, 1)
    for j in range(G):
        pool.indirect_dma_start(rows[:, j, :], None, table, bass.IndirectOffsetOnAxis(idx[:, j:j + 1], 0)).then_inc(rows_in, 16)


def rows_count(m, k):
    return (m - k) * (8 * G) + 16 * G


def reset_rows(pool, rows_in, used, reset_done, n, ticket):
    for semaphore in used:
        pool.wait_ge(semaphore, n * M + (M + 2))
    pool.sem_inc(ticket, 1)
    for k in range(2):
        pool.wait_ge(rows_in[k], rows_count(M - 2 + k, k))
        pool.dma_reset(range(rows_in[k].num, rows_in[k].num + 1))
        pool.sem_clear(rows_in[k])
    pool.sem_inc(reset_done, 1)


def move_window(dve, r, moved, q):
    dve.tensor_scalar(r.window[:, :], r.window[:, :], float(W), None, ALU.add).then_inc(moved, 1)
    dve.wait_ge(moved, q + 2)


def start_window(dve, r, moved):
    dve.tensor_copy(r.window[:, :], r.iota_w[:, :]).then_inc(moved, 1)
    dve.wait_ge(moved, 1)


def attention_edges(nc, d, r):
    with Memory(nc) as mem:
        b = edge_buffers(mem, r, True)
        turned_hot = mem.two("turned_hot", [P, G, W])
        idx = mem.two("idx", [P, G], I32)
        kv = mem.two("kv", [P, G, 2 * P])
        q_win = mem.two("q_win", [W, P])
        prod = mem.sb("prod", [P, G * H0, P // H0])
        score = mem.sb("score", [P, G, H0])
        clipped = mem.two("clipped", [P, G, H0])
        weight = mem.two("weight", [P, G, Z0])
        msg = mem.two("msg", [P, G, P])
        ps_q = mem.ps("ps_q", [P, G * P])
        ps_s = [mem.ps(f"ps_s{k}") for k in range(2)]
        ps_z = [mem.ps(f"ps_z{k}") for k in range(2)]
        idx_in = [mem.sem(f"idx_in{k}") for k in range(2)]
        rows_in, reset_done = [mem.sem(f"rows_in{k}") for k in range(2)], mem.sem("rows_reset_done")
        turned_hot_done, prod_done, sum_done, clip_done, exp_done, msg_done, ticket, moved, ones_set, cleared = map(
            mem.sem, ("turned_hot_done", "prod_done", "sum_done", "clip_done", "exp_done", "msg_done", "ticket", "moved", "ones_set", "cleared"))
        block = mem.block()

        @block.sync
        def _(sp):
            def load(m, k, pair, step, q):
                sp.wait_ge(prod_done, free(step))
                sp.dma_start(idx[k][:, :], d["src"][:, bass.ds(m * G, G)]).then_inc(idx_in[k], 16)
                load_window(sp, r, b, d["q_table"], [w[:, :] for w in q_win], m, k, step, q)
            passes_loop(sp, r, (), [(0, load)])

        @block.gpsimd
        def _(pool):
            def gather(m, k, pair, step, q):
                pool.wait_ge(idx_in[k], pair * 16 + 16)
                pool.wait_ge(msg_done, free(step))
                gather_rows(pool, kv[k], d["kv_table"], idx[k], rows_in[k], ticket)
            passes_loop(pool, r, (), [(0, gather)], lambda n, q: reset_rows(pool, rows_in, (msg_done,), reset_done, n, ticket))

        @block.vector
        def _(dve):
            for k in range(2):
                dve.memset(weight[k][:, :, H0:Z0], 1.0).then_inc(ones_set, 1)
            dve.memset(r.acc[:, :], 0.0).then_inc(cleared, 1)
            dve.memset(r.z[:, :], 0.0).then_inc(cleared, 1)
            dve.wait_ge(cleared, 2)
            start_window(dve, r, moved)

            def hot_to_turn(m, k, pair, step, q):
                make_hot(dve, r, b, m, k, step, turned_hot, b.turn_done, turned_hot_done)

            def hot(m, k, pair, step, q):
                make_hot(dve, r, b, m, k, step, b.hot, b.seg_done, b.hot_done)

            def messages(m, k, pair, step, q):
                dve.wait_ge(b.look_done, done(step))
                dve.wait_ge(rows_in[k], rows_count(m, k))
                dve.tensor_tensor(prod[:, :, :], kv[k][:, :, 0:P].rearrange("p g (h c) -> p g h c", h=H0),
                                  ps_q[:, :].rearrange("p (g h c) -> p g h c", g=G, h=H0), ALU.mult).then_inc(prod_done, 1)
                dve.wait_ge(prod_done, done(step))
                dve.tensor_reduce(score[:, :, :].rearrange("p g h -> p (g h)"), prod[:, :, :], AX.X, ALU.add).then_inc(sum_done, 1)
                dve.wait_ge(sum_done, done(step))
                dve.tensor_scalar(clipped[k][:, :, :], score[:, :, :], 20.0, -20.0, ALU.min, ALU.max).then_inc(clip_done, 1)
                dve.wait_ge(exp_done, done(step))
                dve.tensor_tensor(msg[k][:, :, :].rearrange("p g (h c) -> p g h c", h=H0),
                                  kv[k][:, :, P:2 * P].rearrange("p g (h c) -> p g h c", h=H0),
                                  weight[k][:, :, 0:H0].unsqueeze(3).to_broadcast([P, G, H0, P // H0]), ALU.mult).then_inc(msg_done, 1)

            def accumulate(m, k, pair, step, q):
                base = load_base(dve, r, m, q)
                dve.wait_ge(b.seg_done, done(step))
                dve.wait_ge(b.acc_done, prev_done(step))
                z = r.z[0:Z0, bass.ds(base, W)]
                dve.tensor_tensor(z, z, ps_z[k][0:Z0, 0:W], ALU.add)
                a = r.acc[:, bass.ds(base, W)]
                dve.tensor_tensor(a, a, ps_s[k][:, 0:W], ALU.add).then_inc(b.acc_done, 1)
            passes_loop(dve, r, (b.hot_done, turned_hot_done, prod_done, sum_done, clip_done, msg_done, b.acc_done),
                        [(0, hot_to_turn), (1, messages), (1, hot), (2, accumulate)], lambda n, q: (dve.wait_ge(reset_done, n + 1), move_window(dve, r, moved, n)))

        @block.scalar
        def _(act):
            act.wait_ge(ones_set, 2)

            def copy(m, k, pair, step, q):
                copy_hot(act, b, k, step)

            def exps(m, k, pair, step, q):
                act.wait_ge(clip_done, done(step))
                act.wait_ge(b.seg_done, free(step))
                act.activation(weight[k][:, :, 0:H0], clipped[k][:, :, :], ACT.Exp, scale=0.25).then_inc(exp_done, 1)
            passes_loop(act, r, (b.copy_done, exp_done), [(0, copy), (1, exps)])

        @block.tensor
        def _(pe):
            def turn(m, k, pair, step, q):
                turn_hot(pe, r, b, k, step, turned_hot, turned_hot_done)

            def look_up(m, k, pair, step, q):
                pe.wait_ge(b.copy_done, done(step))
                pe.wait_ge(b.win_in[k], pair * 16 + 16)
                pe.wait_ge(prod_done, prev_done(step))
                for j in range(G):
                    last = pe.matmul(ps_q[:, j * P:(j + 1) * P], b.hot_t[k][:, j * P:(j + 1) * P], q_win[k][:, :], start=True, stop=True)
                last.then_inc(b.look_done, 1)

            def sums(m, k, pair, step, q):
                pe.wait_ge(msg_done, done(step))
                pe.wait_ge(b.hot_done, done(step))
                pe.wait_ge(b.acc_done, free(step))
                for j in range(G):
                    pe.matmul(ps_s[k][:, 0:W], msg[k][:, j, :], b.hot[k][:, j, :], start=j == 0, stop=j == G - 1)
                for j in range(G):
                    last = pe.matmul(ps_z[k][0:Z0, 0:W], weight[k][:, j, :], b.hot[k][:, j, :], start=j == 0, stop=j == G - 1)
                last.then_inc(b.seg_done, 1)
            passes_loop(pe, r, (b.turn_done, b.look_done, b.seg_done), [(0, turn), (2, sums), (0, look_up)])


def attention_nodes(nc, d, r):
    with Memory(nc) as mem:
        head_rows, count_rows = mem.sb("head_rows", [Z0, P]), mem.sb("count_rows", [Z0, P])
        inv, inv_t = mem.sb("inv", [P, NB, Z0]), mem.sb("inv_t", [Z0, NP])
        ps_z = mem.ps("ps_z")
        ps_t = [mem.ps(f"ps_t{k}") for k in range(2)]
        ps_h = [mem.ps(f"ps_h{k}") for k in range(2)]
        ps_c = [mem.ps(f"ps_c{k}") for k in range(2)]
        made, turned, order, inv_ready, back, copied, multiplied, attn_done, count_done = map(
            mem.sem, ("made", "turned", "order", "inv_ready", "back", "copied", "multiplied", "attn_done", "count_done"))
        block = mem.block()

        @block.gpsimd
        def _(pool):
            pool.memset(head_rows[:, :], 1.0).then_inc(made, 1)
            pool.memset(count_rows[:, :], 1.0).then_inc(made, 1)
            pool.wait_ge(made, 2)
            pool.affine_select(out=head_rows[:, :], in_=head_rows[:, :], compare_op=ALU.is_ge, fill=0.0, base=0,
                               pattern=[[1, P]], channel_multiplier=-(P // H0)).then_inc(made, 1)
            pool.wait_ge(made, 3)
            pool.affine_select(out=head_rows[:, :], in_=head_rows[:, :], compare_op=ALU.is_ge, fill=0.0, base=P // H0 - 1,
                               pattern=[[-1, P]], channel_multiplier=P // H0).then_inc(made, 1)
            pool.affine_select(out=count_rows[:, :], in_=count_rows[:, :], compare_op=ALU.is_ge, fill=0.0, base=-H0,
                               pattern=[[0, P]], channel_multiplier=1).then_inc(made, 1)

        @block.tensor
        def _(pe):
            for b in range(NB):
                last = pe.transpose(ps_z[:, b * Z0:(b + 1) * Z0], r.z[0:Z0, b * P:(b + 1) * P], r.ident[0:Z0, 0:Z0])
            last.then_inc(turned, 1)
            pe.wait_ge(made, 5)
            pe.wait_ge(inv_ready, 1)

            def turn_back(n):
                lo, width = chunks()[n]
                if n >= 2:
                    pe.wait_ge(copied, n - 1)
                for j in range(width // P):
                    last = pe.transpose(ps_t[n % 2][0:Z0, j * P:(j + 1) * P], inv[:, lo // P + j, :], r.ident[:, :])
                last.then_inc(back, 1)
            turn_back(0)
            for n, (lo, width) in enumerate(chunks()):
                if n + 1 < len(chunks()):
                    turn_back(n + 1)
                pe.wait_ge(copied, n + 1)
                if n >= 2:
                    pe.wait_ge(attn_done, n - 1)
                    pe.wait_ge(count_done, n - 1)
                pe.matmul(ps_h[n % 2][:, 0:width], head_rows[:, :], inv_t[:, lo:lo + width], start=True, stop=True)
                pe.matmul(ps_c[n % 2][:, 0:width], count_rows[:, :], inv_t[:, lo:lo + width], start=True, stop=True).then_inc(multiplied, 1)

        @block.vector
        def _(dve):
            link = chain(dve, order)
            dve.wait_ge(turned, 1)
            sums = ps_z[:, 0:NB * Z0].rearrange("p (b z) -> p b z", z=Z0)
            dve.tensor_scalar(inv[:, :, 0:H0], sums[:, :, 0:H0], 1e-6, None, ALU.add)
            link(dve.tensor_scalar(inv[:, :, H0:Z0], sums[:, :, H0:Z0], 1.0, None, ALU.max))
            link(dve.reciprocal(inv[:, :, :], inv[:, :, :]))
            dve.sem_inc(inv_ready, 1)
            for n, (lo, width) in enumerate(chunks()):
                dve.wait_ge(multiplied, n + 1)
                dve.tensor_tensor(r.attn[:, lo:lo + width], r.acc[:, lo:lo + width], ps_h[n % 2][:, 0:width], ALU.mult).then_inc(attn_done, 1)

        @block.scalar
        def _(act):
            def copy_back(n):
                lo, width = chunks()[n]
                act.wait_ge(back, n + 1)
                act.activation(inv_t[:, lo:lo + width], ps_t[n % 2][0:Z0, 0:width], ACT.Copy).then_inc(copied, 1)
            copy_back(0)
            for n, (lo, width) in enumerate(chunks()):
                if n + 1 < len(chunks()):
                    copy_back(n + 1)
                act.wait_ge(multiplied, n + 1)
                act.activation(r.root_count[:, lo:lo + width], ps_c[n % 2][:, 0:width], ACT.Sqrt)
                act.activation(r.inv_count[:, lo:lo + width], ps_c[n % 2][:, 0:width], ACT.Copy).then_inc(count_done, 1)


def hidden(nc, r, src, weights, bias, out):
    with Memory(nc) as mem:
        ps = [mem.ps(f"ps{k}") for k in range(4)]
        multiplied, copied = map(mem.sem, ("multiplied", "copied"))
        block = mem.block()
        parts = [(half, lo, width) for lo, width in chunks() for half in range(2)]

        @block.tensor
        def _(pe):
            for n, (half, lo, width) in enumerate(parts):
                if n >= 4:
                    pe.wait_ge(copied, n - 3)
                pe.matmul(ps[n % 4][:, 0:width], weights[:, half * P:(half + 1) * P], src[:, lo:lo + width], start=True, stop=True).then_inc(multiplied, 1)

        @block.scalar
        def _(act):
            for n, (half, lo, width) in enumerate(parts):
                act.wait_ge(multiplied, n + 1)
                act.activation(out[half][:, lo:lo + width], ps[n % 4][:, 0:width], ACT.Relu, bias=bias[:, half:half + 1]).then_inc(copied, 1)


def attention_layer(nc, d, r):
    with Memory(nc) as mem:
        w = mem.sb("w_qkv", [P, 3 * P])
        out = mem.sb("kvq", [P, NB, 3 * P])
        project(nc, [r.ht], [w[:, :]], out, load=[(w[:, 0:P], d["l0_wk"]), (w[:, P:2 * P], d["l0_wv"]), (w[:, 2 * P:3 * P], d["l0_wq"])],
                stores=[(rows_of(d["kv_table"]), lambda lo, hi: out[:, lo:hi, 0:2 * P]),
                        (rows_of(d["q_table"]), lambda lo, hi: out[:, lo:hi, 2 * P:3 * P])])
    attention_edges(nc, d, r)
    with Memory(nc) as mem:
        r.attn = mem.sb("attn", [P, NP])
        attention_nodes(nc, d, r)
        w_o, x1, sums = mem.sb("w_o", [P, P]), mem.sb("x1", [P, NB, P]), None
        rows = mem.sb("rows", [P, 6, P])
        w_1, w_2, bias = mem.sb("w_1", [P, 2 * P]), mem.sb("w_2", [P, 2, P]), mem.sb("bias", [P, 2])
        ready = mem.sem("ready")
        load = [(rows[:, n, :], v.partition_broadcast(P)) for n, v in
                enumerate((d["l0_bo"], d["l0_ln1_g"], d["l0_ln1_b"], d["l0_b2"], d["l0_ln2_g"], d["l0_ln2_b"]))]
        load += [(w_o[:, :], d["l0_wo"]), (w_1[:, :], d["l0_w1"]), (w_2[:, :, :], d["l0_w2"]), (bias[:, :], d["l0_b1"])]
        add_rows(nc, r.h, rows[:, 0, :], load)
        project(nc, [r.attn], [w_o[:, :]], x1, add=lambda b: r.h[:, b, :])
        normalise(nc, r, x1[:, :, :], x1[:, :, :], weight=rows[:, 1, :], shift=rows[:, 2, :])
        turn(nc, r, x1[:, :, :], r.ht[:, :])
        hid = mem.two("hid", [P, NP])
        hidden(nc, r, r.ht, w_1, bias, hid)
        add_rows(nc, x1, rows[:, 3, :])
        project(nc, hid, [w_2[:, 0, :], w_2[:, 1, :]], x1, add=lambda b: x1[:, b, :])
        normalise(nc, r, x1[:, :, :], None, weight=rows[:, 4, :], shift=rows[:, 5, :], residual=r.x[:, :, :])


def add_rows(nc, to, row, load=()):
    with Memory(nc) as mem:
        loaded = mem.sem("loaded")
        added = mem.sem("added")
        block = mem.block()

        @block.sync
        def _(sp):
            for out, of in load:
                sp.dma_start(out, of).then_inc(loaded, 16)
            if load:
                sp.wait_ge(loaded, 16 * len(load))

        @block.vector
        def _(dve):
            if load:
                dve.wait_ge(loaded, 16 * len(load))
            dve.tensor_tensor(to[:, :, :], to[:, :, :], bc(row, 1, [P, NB, P]), ALU.add).then_inc(added, 1)
            dve.wait_ge(added, 1)


def mean_edges(nc, d, r, w_e):
    with Memory(nc) as mem:
        b = edge_buffers(mem, r, False)
        idx = mem.two("idx", [P, G], I32)
        rows = mem.two("rows", [P, G, P])
        attr = mem.two("attr", [3, G * P])
        pre = mem.two("pre", [P, G, P])
        msg = mem.two("msg", [P, G, P])
        ps_e = [mem.ps(f"ps_e{k}", [P, G * P]) for k in range(2)]
        ps_s = [mem.ps(f"ps_s{k}") for k in range(2)]
        idx_in = [mem.sem(f"idx_in{k}") for k in range(2)]
        rows_in, reset_done = [mem.sem(f"rows_in{k}") for k in range(2)], mem.sem("rows_reset_done")
        attr_in = [mem.sem(f"attr_in{k}") for k in range(2)]
        edge_done, pre_done, msg_done, ticket, moved, cleared = map(
            mem.sem, ("edge_done", "pre_done", "msg_done", "ticket", "moved", "cleared"))
        block = mem.block()

        @block.sync
        def _(sp):
            def load(m, k, pair, step, q):
                sp.wait_ge(pre_done, free(step))
                sp.dma_start(idx[k][:, :], d["src"][:, bass.ds(m * G, G)]).then_inc(idx_in[k], 16)
                sp.dma_start(attr[k][:, :], d["edge_attr"][:, bass.ds(m * (G * P), G * P)]).then_inc(attr_in[k], 16)
            passes_loop(sp, r, (), [(0, load)])

        @block.gpsimd
        def _(pool):
            def gather(m, k, pair, step, q):
                pool.wait_ge(idx_in[k], pair * 16 + 16)
                pool.wait_ge(pre_done, free(step))
                gather_rows(pool, rows[k], d["row_table"], idx[k], rows_in[k], ticket)
            passes_loop(pool, r, (), [(0, gather)], lambda n, q: reset_rows(pool, rows_in, (pre_done,), reset_done, n, ticket))

        @block.tensor
        def _(pe):
            def edges(m, k, pair, step, q):
                pe.wait_ge(attr_in[k], pair * 16 + 16)
                pe.wait_ge(pre_done, free(step))
                for j in range(G):
                    last = pe.matmul(ps_e[k][:, j * P:(j + 1) * P], attr[k][:, j * P:(j + 1) * P], w_e[:, :], start=True, stop=True)
                last.then_inc(edge_done, 1)

            def sums(m, k, pair, step, q):
                pe.wait_ge(msg_done, done(step))
                pe.wait_ge(b.hot_done, done(step))
                pe.wait_ge(b.acc_done, free(step))
                for j in range(G):
                    last = pe.matmul(ps_s[k][:, 0:W], msg[k][:, j, :], b.hot[k][:, j, :], start=j == 0, stop=j == G - 1)
                last.then_inc(b.seg_done, 1)
            passes_loop(pe, r, (edge_done, b.seg_done), [(0, edges), (1, sums)])

        @block.vector
        def _(dve):
            dve.memset(r.acc[:, :], 0.0).then_inc(cleared, 1)
            dve.wait_ge(cleared, 1)
            start_window(dve, r, moved)

            def hot(m, k, pair, step, q):
                make_hot(dve, r, b, m, k, step)

            def leaky(m, k, pair, step, q):
                dve.wait_ge(edge_done, done(step))
                dve.wait_ge(rows_in[k], rows_count(m, k))
                dve.tensor_tensor(pre[k][:, :, :], rows[k][:, :, :], ps_e[k][:, :].rearrange("p (g f) -> p g f", g=G), ALU.add).then_inc(pre_done, 1)
                dve.wait_ge(pre_done, done(step))
                dve.wait_ge(b.seg_done, free(step))
                dve.scalar_tensor_tensor(msg[k][:, :, :], pre[k][:, :, :], 0.01, pre[k][:, :, :], ALU.mult, ALU.max).then_inc(msg_done, 1)

            def accumulate(m, k, pair, step, q):
                add_window(dve, r, b, ps_s[k][:, 0:W], r.acc, m, step, q)
            passes_loop(dve, r, (b.hot_done, pre_done, msg_done, b.acc_done), [(0, hot), (1, leaky), (2, accumulate)],
                        lambda n, q: (dve.wait_ge(reset_done, n + 1), move_window(dve, r, moved, n)))


def add_window(dve, r, b, sums, to, m, step, q):
    base = load_base(dve, r, m, q)
    dve.wait_ge(b.seg_done, done(step))
    dve.wait_ge(b.acc_done, prev_done(step))
    part = to[0:sums.shape[0], bass.ds(base, W)]
    dve.tensor_tensor(part, part, sums, ALU.add).then_inc(b.acc_done, 1)


def combine(nc, terms, out):
    with Memory(nc) as mem:
        order = mem.sem("order")
        block = mem.block()

        @block.vector
        def _(dve):
            terms(dve, chain(dve, order))


def mean_layer(nc, d, r):
    with Memory(nc) as mem:
        w_x, w_e, w_2 = mem.sb("w_x", [P, P]), mem.sb("w_e", [3, P]), mem.sb("w_2", [P, 2, P])
        rows, out = mem.sb("rows", [P, 2, P]), mem.sb("out", [P, NB, P])
        project(nc, [r.ht], [w_x[:, :]], out,
                load=[(w_x[:, :], d["l1_w1"][0:P, :]), (w_e[:, :], d["l1_w1"][P:P + 3, :]), (w_2[:, :, :], d["l1_w2"]),
                      (rows[:, 0, :], d["l1_b1"].partition_broadcast(P)), (rows[:, 1, :], d["l1_b2"].partition_broadcast(P))],
                add=lambda b: rows[:, 0, :], stores=[(rows_of(d["row_table"]), lambda lo, hi: out[:, lo:hi, :])])
        mean_edges(nc, d, r, w_e)
        mean = mem.sb("mean", [P, NP])

        def divide(dve, link):
            link(dve.tensor_tensor(mean[:, :], r.acc[:, 0:NP], r.inv_count[:, :], ALU.mult))
        combine(nc, divide, None)
        project(nc, [r.ht, mean], [w_2[:, 0, :], w_2[:, 1, :]], out, add=lambda b: rows[:, 1, :])

        def finish(dve, link):
            link(dve.scalar_tensor_tensor(r.x[:, :, :], out[:, :, :], 0.0, r.x[:, :, :], ALU.max, ALU.add))
        combine(nc, finish, None)


def sum_edges(nc, d, r):
    with Memory(nc) as mem:
        b = edge_buffers(mem, r, False)
        idx = mem.two("idx", [P, G], I32)
        rows = mem.two("rows", [P, G, P])
        ps_s = [mem.ps(f"ps_s{k}") for k in range(2)]
        idx_in = [mem.sem(f"idx_in{k}") for k in range(2)]
        rows_in, reset_done = [mem.sem(f"rows_in{k}") for k in range(2)], mem.sem("rows_reset_done")
        ticket, moved, cleared = map(mem.sem, ("ticket", "moved", "cleared"))
        block = mem.block()

        @block.sync
        def _(sp):
            def load(m, k, pair, step, q):
                sp.wait_ge(b.seg_done, free(step))
                sp.dma_start(idx[k][:, :], d["src"][:, bass.ds(m * G, G)]).then_inc(idx_in[k], 16)
            passes_loop(sp, r, (), [(0, load)])

        @block.gpsimd
        def _(pool):
            def gather(m, k, pair, step, q):
                pool.wait_ge(idx_in[k], pair * 16 + 16)
                pool.wait_ge(b.seg_done, free(step))
                gather_rows(pool, rows[k], d["row_table"], idx[k], rows_in[k], ticket)
            passes_loop(pool, r, (), [(0, gather)], lambda n, q: reset_rows(pool, rows_in, (b.seg_done,), reset_done, n, ticket))

        @block.tensor
        def _(pe):
            def sums(m, k, pair, step, q):
                pe.wait_ge(b.hot_done, done(step))
                pe.wait_ge(b.acc_done, free(step))
                pe.wait_ge(rows_in[k], rows_count(m, k))
                for j in range(G):
                    last = pe.matmul(ps_s[k][:, 0:W], rows[k][:, j, :], b.hot[k][:, j, :], start=j == 0, stop=j == G - 1)
                last.then_inc(b.seg_done, 1)
            passes_loop(pe, r, (b.seg_done,), [(0, sums)], lambda n, q: pe.wait_ge(reset_done, n + 1))

        @block.vector
        def _(dve):
            dve.memset(r.acc[:, :], 0.0).then_inc(cleared, 1)
            dve.wait_ge(cleared, 1)
            start_window(dve, r, moved)

            def hot(m, k, pair, step, q):
                make_hot(dve, r, b, m, k, step)

            def accumulate(m, k, pair, step, q):
                add_window(dve, r, b, ps_s[k][:, 0:W], r.acc, m, step, q)
            passes_loop(dve, r, (b.hot_done, b.acc_done), [(0, hot), (1, accumulate)],
                        lambda n, q: move_window(dve, r, moved, n))


def chebyshev_layer(nc, d, r):
    with Memory(nc) as mem:
        w = mem.sb("w", [P, 4, P])
        t = [r.ht] + [mem.sb(f"t{k}", [P, NP]) for k in range(1, 4)]
        out = mem.sb("out", [P, NB, P])
        for k in range(1, 4):
            turn(nc, r, t[k - 1], out[:, :, :], scale=r.root_count, store=d["row_table"])
            sum_edges(nc, d, r)

            def recur(dve, link):
                link(dve.tensor_tensor(t[k][:, :], r.acc[:, 0:NP], r.root_count[:, :], ALU.mult))
                if k > 1:
                    link(dve.scalar_tensor_tensor(t[k][:, :], t[k][:, :], 2.0, t[k - 2][:, :], ALU.mult, ALU.subtract))
            combine(nc, recur, None)
        project(nc, t, [w[:, k, :] for k in range(4)], r.x, load=[(w[:, :, :], d["l2_w"])], add=lambda b: r.x[:, b, :])


def relation_select(dve, r, values, picked, m, step, sem_done, sem_sum, tmp):
    hot = r.type_hot[:, bass.ds(m * G, G), :]
    dve.tensor_tensor(tmp[:, :, :, :], values.rearrange("p g (r h) -> p g h r", r=R),
                      hot.unsqueeze(2).to_broadcast([P, G, H3, R]), ALU.mult).then_inc(sem_done, 1)
    dve.wait_ge(sem_done, done(step))
    dve.tensor_reduce(picked[:, :, :], tmp[:, :, :, :], AX.X, ALU.add).then_inc(sem_sum, 1)
    dve.wait_ge(sem_sum, done(step))


def relation_scores(nc, d, r):
    with Memory(nc) as mem:
        b = edge_buffers(mem, r, True)
        idx = mem.two("idx", [P, G], I32)
        rows = mem.two("rows", [P, G, ROW])
        win = mem.two("win", [W, RH + 1])
        tmp = mem.sb("tmp", [P, G, H3, R])
        picked, total, slope, gated = (mem.sb(n, [P, G, H3]) for n in ("picked", "total", "slope", "gated"))
        placed, rest = mem.sb("placed", [P, G, RH]), mem.sb("rest", [P, G, RH])
        tagged = mem.two("tagged", [P, G, TAG], BF16)
        tagged_t = mem.two("tagged_t", [TAG, G * P], BF16)
        spread = mem.sb("spread", [TAG, GW, P], BF16)
        ident16 = mem.sb("ident16", [P, P], BF16)
        gwin = mem.sb("gwin", [P, GW * GN])
        best = mem.two("best", [P, GW, G // 2])
        top = mem.two("top", [P, GX])
        top_rows = mem.sb("top_rows", [P, 4, P])
        ps_q = mem.ps("ps_q")
        look = ps_q[:, 0:G * (RH + 1)].rearrange("p (g c) -> p g c", g=G)
        ps_b = [mem.ps(f"ps_b{k}", [TAG, G * P], BF16) for k in range(2)]
        ps_m = [mem.ps(f"ps_m{n}") for n in range(GW)]
        idx_in = [mem.sem(f"idx_in{k}") for k in range(2)]
        rows_in, reset_done = [mem.sem(f"rows_in{k}") for k in range(2)], mem.sem("rows_reset_done")
        spill_out = [mem.sem(f"spill_out{k}") for k in range(2)]
        (mul_done, pick_done, add_done, slope_done, gate_done, e_done, tag_done, tag_turn_done, tag_copy_done, max_done,
         best_done, spill_done, ticket, moved, gmoved, cleared, ones_set, made, top_ready, top_turned, top_copied, stored) = map(
            mem.sem, ("mul_done", "pick_done", "add_done", "slope_done", "gate_done", "e_done", "tag_done", "tag_turn_done",
                      "tag_copy_done", "max_done", "best_done", "spill_done", "ticket", "moved", "gmoved", "cleared",
                      "ones_set", "made", "top_ready", "top_turned", "top_copied", "stored"))
        groups_reset_done, pe_ticket, pass_ticket, split_done = map(mem.sem, ("groups_reset_done", "pe_ticket", "pass_ticket", "split_done"))
        block = mem.block()

        @block.sync
        def _(sp):
            sp.wait_ge(ones_set, 2)

            def load(m, k, pair, step, q):
                sp.wait_ge(add_done, free(step))
                sp.dma_start(idx[k][:, :], d["key"][:, bass.ds(m * G, G)]).then_inc(idx_in[k], 16)
                load_window(sp, r, b, d["ed_table"], [w[:, 0:RH] for w in win], m, k, step, q)

            def spill(m, k, pair, step, q):
                sp.wait_ge(rows_in[k], rows_count(m, k))
                sp.dma_start(d["spill"][bass.ds(m * P, P), :], rows[k][:, :, :].rearrange("p g f -> p (g f)")).then_inc(spill_out[k], 16)

            def confirm(m, k, pair, step, q):
                sp.wait_ge(spill_out[k], pair * 16 + 16)
                sp.sem_inc(spill_done, 1)
            passes_loop(sp, r, (spill_done,), [(0, load), (2, confirm), (1, spill)], lambda n, q: (sp.wait_ge(reset_done, n + 1), sp.sem_inc(pass_ticket, 1)), cycles=True)
            sp.wait_ge(top_copied, 4)
            for n in range(4):
                width = min(P, NG - n * P)
                sp.dma_start(d["top_table"][n * P * GN:(n * P + width) * GN, :].rearrange("(g a) c -> g (a c)", a=GN), top_rows[0:width, n, :]).then_inc(stored, 16)
            sp.wait_ge(stored, 64)

        @block.gpsimd
        def _(pool):
            pool.memset(spread[:, :, :], 0.0).then_inc(made, 1)
            pool.wait_ge(made, 1)
            view = spread[:, :, :].rearrange("t g (a c) -> t g a c", c=RH)
            pool.affine_select(out=view, in_=view, compare_op=ALU.not_equal, fill=-BIG, base=0,
                               pattern=[[GN, GW], [1, GN], [0, RH]], channel_multiplier=-1).then_inc(made, 1)
            for n in range(PARTS):
                pool.wait_ge(made, n + 2)
                pool.affine_select(out=view, in_=view, compare_op=ALU.not_equal, fill=1.0, base=GW * GN + n * RH,
                                   pattern=[[0, GW], [0, GN], [1, RH]], channel_multiplier=-1).then_inc(made, 1)

            def gather(m, k, pair, step, q):
                pool.wait_ge(idx_in[k], pair * 16 + 16)
                pool.wait_ge(add_done, free(step))
                pool.wait_ge(spill_done, free(step))
                gather_rows(pool, rows[k], d["h_table"], idx[k], rows_in[k], ticket)
            passes_loop(pool, r, (), [(0, gather)], lambda n, q: reset_rows(pool, rows_in, (add_done, spill_done,), reset_done, n, ticket), cycles=True)

        @block.scalar
        def _(act):
            def copy_tags(m, k, pair, step, q):
                act.wait_ge(tag_turn_done, done(step))
                act.wait_ge(max_done, free(step))
                act.activation(tagged_t[k][:, :], ps_b[k][:, :], ACT.Copy).then_inc(tag_copy_done, 1)
            passes_loop(act, r, (b.copy_done, tag_copy_done),
                        [(0, lambda m, k, pair, step, q: copy_hot(act, b, k, step)), (1, copy_tags)], cycles=True)
            act.wait_ge(top_turned, 1)
            for n in range(4):
                width = min(P, NG - n * P)
                act.activation(top_rows[0:width, n, :], ps_q[0:width, n * P:(n + 1) * P], ACT.Copy).then_inc(top_copied, 1)

        @block.tensor
        def _(pe):
            pe.wait_ge(made, PARTS + 2)
            pe.wait_ge(cleared, 4)

            def turn_tags(m, k, pair, step, q):
                pe.wait_ge(tag_done, done(step))
                pe.wait_ge(tag_copy_done, free(step))
                pe.sem_inc(pe_ticket, 1)
                for j in range(G):
                    last = pe.transpose(ps_b[k][:, j * P:(j + 1) * P], tagged[k][:, j, :], ident16[:, :])
                last.then_inc(tag_turn_done, 1)

            def turn(m, k, pair, step, q):
                turn_hot(pe, r, b, k, step)

            def look_up(m, k, pair, step, q):
                pe.wait_ge(b.copy_done, done(step))
                pe.wait_ge(b.win_in[k], pair * 16 + 16)
                pe.wait_ge(gate_done, prev_done(step))
                for j in range(G):
                    last = pe.matmul(look[:, j, :], b.hot_t[k][:, j * P:(j + 1) * P], win[k][:, :], start=True, stop=True)
                last.then_inc(b.look_done, 1)

            def spread_half(k, step, half):
                first = pe.snap(step * (2 * GW) + half * GW)
                for g in range(GW):
                    pe.wait_ge(best_done, first + (g + 1))
                    pe.matmul(ps_m[g][:, :], spread[:, g, :], tagged_t[k][:, half * CHUNK:(half + 1) * CHUNK], start=True, stop=True).then_inc(b.unit_done, 1)
                return first

            def first_spread(m, k, pair, step, q):
                pe.wait_ge(tag_copy_done, done(step))
                spread_half(k, step, 0)

            def last_spread(m, k, pair, step, q):
                first = spread_half(k, step, 1)
                pe.wait_ge(b.unit_done, first + GW)
                pe.sem_inc(max_done, 1)
            passes_loop(pe, r, (b.turn_done, b.look_done, tag_turn_done, max_done), [(2, first_spread), (0, turn), (2, last_spread), (1, turn_tags), (0, look_up)], cycles=True)
            pe.wait_ge(top_ready, 1)
            for n in range(4):
                width = min(P, NG - n * P)
                last = pe.transpose(ps_q[0:width, n * P:(n + 1) * P], top[0][:, n * P:n * P + width], r.ident[:, :])
            last.then_inc(top_turned, 1)

        @block.vector
        def _(dve):
            for k in range(2):
                dve.memset(win[k][:, RH:RH + 1], 1.0).then_inc(ones_set, 1)
            dve.memset(r.e[:, :, :], 0.0).then_inc(cleared, 1)
            for k in range(2):
                dve.memset(top[k][:, :], 0.0).then_inc(cleared, 1)
            dve.tensor_copy(ident16[:, :], r.ident[:, :]).then_inc(cleared, 1)
            dve.wait_ge(cleared, 4)
            dve.sem_inc(best_done, GW)
            dve.sem_inc(b.part_done, 2 * HALF)
            dve.tensor_copy(gwin[:, :], r.iota_g[:, :]).then_inc(gmoved, 1)
            dve.wait_ge(gmoved, 1)
            start_window(dve, r, moved)

            def hot(m, k, pair, step, q):
                dve.wait_ge(b.turn_done, free(step))
                rel = r.rel[:, bass.ds(m, 1), :].rearrange("p o g -> p (o g)")
                dve.tensor_tensor(b.hot[k][:, :, :], bc(r.window[:, :], 1, [P, G, W]), bc(rel, 2, [P, G, W]),
                                  ALU.is_equal).then_inc(b.hot_done, 1)
                dve.wait_ge(tag_turn_done, free(step))
                rel = r.group_rel[:, bass.ds(m * G, G)]
                dve.tensor_tensor(tagged[k][:, :, 0:GW * GN], bc(gwin[:, :], 1, [P, G, GW * GN]),
                                  bc(rel, 2, [P, G, GW * GN]), ALU.not_equal)

            def scores(m, k, pair, step, q):
                dve.wait_ge(b.look_done, done(step))
                relation_select(dve, r, look[:, :, 0:RH], picked, m, step, mul_done, pick_done, tmp)
                dve.wait_ge(rows_in[k], rows_count(m, k))
                dve.tensor_tensor(total[:, :, :], rows[k][:, :, P:ROW], picked[:, :, :], ALU.add).then_inc(add_done, 1)
                dve.wait_ge(add_done, done(step))
                dve.scalar_tensor_tensor(slope[:, :, :], total[:, :, :], 0.2, total[:, :, :], ALU.mult, ALU.max).then_inc(slope_done, 1)
                dve.wait_ge(slope_done, done(step))
                dve.tensor_tensor(gated[:, :, :], slope[:, :, :], look[:, :, RH:RH + 1].to_broadcast([P, G, H3]), ALU.mult).then_inc(gate_done, 1)
                dve.wait_ge(gate_done, done(step))
                dve.wait_ge(e_done, prev_done(step))
                e = r.e[:, bass.ds(m * G, G), :]
                dve.tensor_tensor(e, e, gated[:, :, :], ALU.add).then_inc(e_done, 1)
                dve.wait_ge(e_done, done(step))
                dve.tensor_tensor(placed[:, :, :].rearrange("p g (r h) -> p g r h", r=R),
                                  bc(r.type_hot[:, bass.ds(m * G, G), :], 3, [P, G, R, H3]),
                                  bc(e, 2, [P, G, R, H3]), ALU.mult).then_inc(split_done, 1)
                hi, mid, lo = (tagged[k][:, :, GW * GN + n * RH:GW * GN + (n + 1) * RH] for n in range(PARTS))
                dve.wait_ge(split_done, step * 4 + 1)
                dve.tensor_copy(hi, placed[:, :, :]).then_inc(split_done, 1)
                dve.wait_ge(split_done, step * 4 + 2)
                dve.tensor_tensor(mid, placed[:, :, :], hi, ALU.subtract).then_inc(split_done, 1)
                dve.tensor_tensor(rest[:, :, :], placed[:, :, :], hi, ALU.subtract).then_inc(split_done, 1)
                dve.wait_ge(split_done, step * 4 + 4)
                dve.tensor_tensor(lo, rest[:, :, :], mid, ALU.subtract).then_inc(tag_done, 1)

            def half_maxima(m, k, step, q, half):
                _, groups = nc.values_load_multi_w_load_instructions(r.pair_group[0:1, bass.ds(m * HALF + half * 2, 2)],
                                                                     engines=[mybir.EngineType.DVE], min_val=0, max_val=NG - 1)
                if half == 0:
                    dve.wait_ge(b.part_done, step * HALF + HALF)
                first = dve.snap(step * (2 * GW) + half * GW)
                for g in range(GW):
                    dve.wait_ge(b.unit_done, first + (g + 1))
                    dve.tensor_reduce(best[k][:, g, half * 2:half * 2 + 2], ps_m[g][:, :].rearrange("p (u e) -> p u e", u=2), AX.X, ALU.max).then_inc(best_done, 1)
                shift = dve.snap(q * GW)
                dve.wait_ge(best_done, first + 2 * GW)
                for u in range(2):
                    dve.wait_ge(b.part_done, step * HALF + (2 * HALF + 2 * half + u - 1))
                    part = top[u][:, bass.ds(groups[u] + shift, GW)]
                    dve.tensor_tensor(part, part, best[k][:, :, 2 * half + u], ALU.max).then_inc(b.part_done, 1)

            def first_maxima(m, k, pair, step, q):
                half_maxima(m, k, step, q, 0)

            def last_maxima(m, k, pair, step, q):
                half_maxima(m, k, step, q, 1)
            passes_loop(dve, r, (b.hot_done, mul_done, pick_done, add_done, slope_done, gate_done, e_done, tag_done),
                        [(0, hot), (2, first_maxima), (1, scores), (2, last_maxima)],
                        each_pass=lambda n, q: (dve.wait_ge(reset_done, n + 1), move_window(dve, r, moved, n),
                                                dve.tensor_scalar(gwin[:, :], gwin[:, :], float(GW * GN), None, ALU.add).then_inc(gmoved, 1),
                                                dve.wait_ge(gmoved, n + 2)), cycles=True,
                        each_cycle=lambda c: (dve.tensor_copy(gwin[:, :], r.iota_g[:, :]).then_inc(groups_reset_done, 1),
                                              dve.wait_ge(groups_reset_done, c + 1)))
            dve.tensor_tensor(top[0][:, :], top[0][:, :], top[1][:, :], ALU.max).then_inc(top_ready, 1)


def relation_edges(nc, d, r):
    with Memory(nc) as mem:
        b = edge_buffers(mem, r, True)
        rows = mem.two("rows", [P, G, ROW])
        msg = mem.two("msg", [P, G, P])
        typed = mem.two("typed", [P, G, R * W])
        win = mem.two("win", [W, RH + 1])
        tmp = mem.sb("tmp", [P, G, H3, R])
        picked, less = (mem.sb(n, [P, G, H3]) for n in ("picked", "less"))
        gated, power = mem.two("gated", [P, G, H3]), mem.two("power", [P, G, H3])
        placed = mem.two("placed", [P, G, R, H3])
        typed_window = mem.sb("typed_window", [P, R * W])
        ps_q = mem.ps("ps_q")
        look = ps_q[:, 0:G * (RH + 1)].rearrange("p (g c) -> p g c", g=G)
        ps_s = [mem.ps(f"ps_s{k}") for k in range(2)]
        ps_z = [mem.ps(f"ps_z{k}") for k in range(2)]
        rows_in = [mem.sem(f"rows_in{k}") for k in range(2)]
        (mul_done, pick_done, less_done, gate_done, exp_done, typed_done, place_done, msg_done, z_done, moved, tmoved, cleared, ones_set) = map(
            mem.sem, ("mul_done", "pick_done", "less_done", "gate_done", "exp_done", "typed_done", "place_done", "msg_done", "z_done",
                      "moved", "tmoved", "cleared", "ones_set"))
        block = mem.block()

        @block.sync
        def _(sp):
            sp.wait_ge(ones_set, 2)

            def load(m, k, pair, step, q):
                sp.wait_ge(msg_done, free(step))
                sp.dma_start(rows[k][:, :, :].rearrange("p g f -> p (g f)"), d["spill"][bass.ds(m * P, P), :]).then_inc(rows_in[k], 16)
                load_window(sp, r, b, d["top_table"], [w[:, 0:RH] for w in win], m, k, step, q)
            passes_loop(sp, r, (), [(0, load)])

        @block.gpsimd
        def _(pool):
            pool.memset(r.z[:, :], 0.0).then_inc(cleared, 1)
            pool.memset(r.acc4[:, :, :], 0.0).then_inc(cleared, 1)

        @block.scalar
        def _(act):
            def exps(m, k, pair, step, q):
                act.wait_ge(gate_done, done(step))
                act.wait_ge(msg_done, free(step))
                act.activation(power[k][:, :, :], gated[k][:, :, :], ACT.Exp).then_inc(exp_done, 1)
            passes_loop(act, r, (b.copy_done, exp_done), [(1, exps), (0, lambda m, k, pair, step, q: copy_hot(act, b, k, step))])

        @block.tensor
        def _(pe):
            def turn(m, k, pair, step, q):
                turn_hot(pe, r, b, k, step)

            def look_up(m, k, pair, step, q):
                pe.wait_ge(b.copy_done, done(step))
                pe.wait_ge(b.win_in[k], pair * 16 + 16)
                pe.wait_ge(gate_done, prev_done(step))
                for j in range(G):
                    last = pe.matmul(look[:, j, :], b.hot_t[k][:, j * P:(j + 1) * P], win[k][:, :], start=True, stop=True)
                last.then_inc(b.look_done, 1)

            def add_messages(k, tiles):
                for j in tiles:
                    last = pe.matmul(ps_s[k][:, 0:R * W], msg[k][:, j, :], typed[k][:, j, :], start=j == 0, stop=j == G - 1)
                return last

            def first_sums(m, k, pair, step, q):
                pe.wait_ge(place_done, done(step))
                pe.wait_ge(b.acc_done, free(step))
                for j in range(G):
                    last = pe.matmul(ps_z[k][0:RH, 0:W], placed[k][:, j, :, :].rearrange("p r h -> p (r h)"), b.hot[k][:, j, :], start=j == 0, stop=j == G - 1)
                last.then_inc(z_done, 1)
                pe.wait_ge(msg_done, done(step))
                pe.wait_ge(typed_done, done(step))
                add_messages(k, range(G // 2))

            def last_sums(m, k, pair, step, q):
                add_messages(k, range(G // 2, G)).then_inc(b.seg_done, 1)
            passes_loop(pe, r, (b.turn_done, b.look_done, z_done, b.seg_done), [(2, first_sums), (0, turn), (2, last_sums), (0, look_up)])

        @block.vector
        def _(dve):
            for k in range(2):
                dve.memset(win[k][:, RH:RH + 1], 1.0).then_inc(ones_set, 1)
            start_window(dve, r, moved)
            for n in range(R):
                dve.tensor_scalar(typed_window[:, n * W:(n + 1) * W], r.iota_w[:, :], float(n * KIND), None, ALU.add).then_inc(tmoved, 1)
            dve.wait_ge(tmoved, R)

            def hot(m, k, pair, step, q):
                make_hot(dve, r, b, m, k, step, used=z_done)

            def typed_hot(m, k, pair, step, q):
                dve.wait_ge(b.seg_done, free(step))
                for j in range(G):
                    last = dve.tensor_scalar(typed[k][:, j, :], typed_window[:, :], r.typed_rel[:, bass.ds(m * G + j, 1)], None, ALU.is_equal)
                last.then_inc(typed_done, 1)

            def scores(m, k, pair, step, q):
                dve.wait_ge(b.look_done, done(step))
                relation_select(dve, r, look[:, :, 0:RH], picked, m, step, mul_done, pick_done, tmp)
                dve.tensor_tensor(less[:, :, :], r.e[:, bass.ds(m * G, G), :], picked[:, :, :], ALU.subtract).then_inc(less_done, 1)
                dve.wait_ge(less_done, done(step))
                dve.tensor_tensor(gated[k][:, :, :], less[:, :, :], look[:, :, RH:RH + 1].to_broadcast([P, G, H3]), ALU.mult).then_inc(gate_done, 1)

            def messages(m, k, pair, step, q):
                dve.wait_ge(exp_done, done(step))
                dve.wait_ge(b.seg_done, free(step))
                dve.tensor_tensor(placed[k][:, :, :, :], bc(r.type_hot[:, bass.ds(m * G, G), :], 3, [P, G, R, H3]),
                                  bc(power[k][:, :, :], 2, [P, G, R, H3]), ALU.mult).then_inc(place_done, 1)
                dve.wait_ge(rows_in[k], pair * 16 + 16)
                dve.tensor_tensor(msg[k][:, :, :].rearrange("p g (h c) -> p g h c", h=H3),
                                  rows[k][:, :, 0:P].rearrange("p g (h c) -> p g h c", h=H3),
                                  power[k][:, :, :].unsqueeze(3).to_broadcast([P, G, H3, P // H3]), ALU.mult).then_inc(msg_done, 1)

            def accumulate(m, k, pair, step, q):
                base = load_base(dve, r, m, q)
                dve.wait_ge(b.seg_done, done(step))
                dve.wait_ge(b.acc_done, prev_done(step))
                dve.wait_ge(cleared, 2)
                z = r.z[0:RH, bass.ds(base, W)]
                dve.tensor_tensor(z, z, ps_z[k][0:RH, 0:W], ALU.add)
                a = r.acc4[:, :, bass.ds(base, W)]
                dve.tensor_tensor(a, a, ps_s[k][:, 0:R * W].rearrange("p (r w) -> p r w", r=R), ALU.add).then_inc(b.acc_done, 1)
            passes_loop(dve, r, (b.hot_done, mul_done, pick_done, less_done, gate_done, typed_done, place_done, msg_done, b.acc_done),
                        [(0, hot), (1, typed_hot), (1, scores), (1, messages), (2, accumulate)],
                        each_pass=lambda n, q: (move_window(dve, r, moved, n),
                                                dve.tensor_scalar(typed_window[:, :], typed_window[:, :], float(W), None, ALU.add).then_inc(tmoved, 1),
                                                dve.wait_ge(tmoved, n + (R + 1))))


def relation_nodes(nc, d, r, out, rows, load):
    with Memory(nc) as mem:
        head_rows = mem.sb("head_rows", [PARTS * RH, R, P], BF16)
        inv, rest = mem.sb("inv", [P, NB, RH]), mem.sb("rest", [P, NB, RH])
        inv_parts, inv_t = mem.sb("inv_parts", [P, NB, PARTS * RH], BF16), mem.sb("inv_t", [PARTS * RH, NP], BF16)
        ident16 = mem.sb("ident16", [P, P], BF16)
        hb = mem.sb("hb", [P, NB, P])
        ps_z = mem.ps("ps_z")
        ps_t = mem.ps("ps_t", [PARTS * RH, CHUNK], BF16)
        ps_i = [mem.ps(f"ps_i{k}") for k in range(3)]
        ps_o = [mem.ps(f"ps_o{k}") for k in range(3)]
        loaded, made, turned, order, inv_ready, back, copied, spread_done, scaled, pool_added, added, folded, turned_back, summed, hb_done = map(
            mem.sem, ("loaded", "made", "turned", "order", "inv_ready", "back", "copied", "spread_done", "scaled", "pool_added", "added", "folded", "turned_back", "summed", "hb_done"))
        block = mem.block()
        parts = [(lo, width, n) for lo, width in chunks() for n in range(R)]
        blocks4 = [(b, min(4, NB - b)) for b in range(0, NB, 4)]

        @block.sync
        def _(sp):
            for to, of in load:
                sp.dma_start(to, of).then_inc(loaded, 16)
            sp.wait_ge(loaded, 16 * len(load))

        @block.gpsimd
        def _(pool):
            pool.memset(head_rows[:, :, :], 0.0).then_inc(made, 1)
            view = head_rows[:, :, :].rearrange("c n (h f) -> c n h f", h=H3)
            for n in range(PARTS):
                pool.wait_ge(made, n + 1)
                pool.affine_select(out=view, in_=view, compare_op=ALU.not_equal, fill=1.0, base=n * RH,
                                   pattern=[[H3, R], [1, H3], [0, P // H3]], channel_multiplier=-1).then_inc(made, 1)
            pool.wait_ge(loaded, 16 * len(load))
            pool.tensor_tensor(hb[:, :, :], r.h[:, :, :], bc(rows[:, 0, :], 1, [P, NB, P]), ALU.add).then_inc(hb_done, 1)
            for n, (lo, width) in enumerate(chunks()):
                pool.wait_ge(scaled, R * (n + 1))
                pool.tensor_tensor(r.acc4[:, 2, lo:lo + width], r.acc4[:, 2, lo:lo + width], r.acc4[:, 3, lo:lo + width], ALU.add).then_inc(pool_added, 1)

        @block.tensor
        def _(pe):
            for b in range(NB):
                last = pe.transpose(ps_z[:, b * RH:(b + 1) * RH], r.z[0:RH, b * P:(b + 1) * P], r.ident[0:RH, 0:RH])
            last.then_inc(turned, 1)
            pe.wait_ge(inv_ready, 1)
            for n, (b, width) in enumerate(blocks4):
                if n:
                    pe.wait_ge(copied, n)
                for j in range(width):
                    last = pe.transpose(ps_t[:, j * P:(j + 1) * P], inv_parts[:, b + j, :], ident16[:, :])
                last.then_inc(back, 1)
            pe.wait_ge(copied, len(blocks4))
            pe.wait_ge(made, PARTS + 1)

            def spread(u):
                lo, width, n = parts[u]
                if u >= 3:
                    pe.wait_ge(scaled, u - 2)
                pe.matmul(ps_i[u % 3][:, 0:width], head_rows[:, n, :], inv_t[:, lo:lo + width], start=True, stop=True).then_inc(spread_done, 1)

            def turn_back(n):
                b, width = blocks4[n]
                pe.wait_ge(folded, n + 1)
                if n >= 3:
                    pe.wait_ge(summed, n - 2)
                for j in range(width):
                    last = pe.transpose(ps_o[n % 3][:, j * P:(j + 1) * P], r.acc4[:, 0, (b + j) * P:(b + j + 1) * P], r.ident[:, :])
                last.then_inc(turned_back, 1)
            for n in range(len(blocks4)):
                for k in range(R):
                    spread(n * R + k)
                if n >= 2:
                    turn_back(n - 2)
            for n in range(len(blocks4) - 2, len(blocks4)):
                turn_back(n)

        @block.scalar
        def _(act):
            for n, (b, width) in enumerate(blocks4):
                act.wait_ge(back, n + 1)
                act.activation(inv_t[:, b * P:(b + width) * P], ps_t[:, 0:width * P], ACT.Copy).then_inc(copied, 1)

        @block.vector
        def _(dve):
            link = chain(dve, order)
            link(dve.tensor_copy(ident16[:, :], r.ident[:, :]))
            dve.wait_ge(turned, 1)
            link(dve.tensor_scalar(inv[:, :, :], ps_z[:, 0:NB * RH].rearrange("p (b c) -> p b c", c=RH), 1e-8, None, ALU.add))
            link(dve.reciprocal(inv[:, :, :], inv[:, :, :]))
            hi, mid, lo = (inv_parts[:, :, n * RH:(n + 1) * RH] for n in range(PARTS))
            link(dve.tensor_copy(hi, inv[:, :, :]))
            dve.tensor_tensor(mid, inv[:, :, :], hi, ALU.subtract)
            link(dve.tensor_tensor(rest[:, :, :], inv[:, :, :], hi, ALU.subtract))
            link(dve.tensor_tensor(lo, rest[:, :, :], mid, ALU.subtract))
            dve.sem_inc(inv_ready, 1)

            def fold(n):
                lo, width = chunks()[n]
                a = r.acc4[:, 0, lo:lo + width]
                dve.wait_ge(added, n + 1)
                dve.wait_ge(pool_added, n + 1)
                dve.tensor_tensor(a, a, r.acc4[:, 2, lo:lo + width], ALU.add).then_inc(folded, 1)

            def take(n):
                b, width = blocks4[n]
                dve.wait_ge(turned_back, n + 1)
                dve.tensor_tensor(out[:, b:b + width, :].rearrange("p b f -> p (b f)"), ps_o[n % 3][:, 0:width * P],
                                  hb[:, b:b + width, :].rearrange("p b f -> p (b f)"), ALU.add).then_inc(summed, 1)
            dve.wait_ge(hb_done, 1)
            for n, (lo, width) in enumerate(chunks()):
                for k in range(R):
                    u = n * R + k
                    dve.wait_ge(spread_done, u + 1)
                    a = r.acc4[:, k, lo:lo + width]
                    dve.tensor_tensor(a, a, ps_i[u % 3][:, 0:width], ALU.mult).then_inc(scaled, 1)
                if n >= 1:
                    fold(n - 1)
                dve.wait_ge(scaled, R * n + 2)
                a = r.acc4[:, 0, lo:lo + width]
                dve.tensor_tensor(a, a, r.acc4[:, 1, lo:lo + width], ALU.add).then_inc(added, 1)
                if n >= 2:
                    take(n - 2)
            fold(len(blocks4) - 1)
            for n in range(len(blocks4) - 2, len(blocks4)):
                take(n)


def relation_layer(nc, d, r):
    with Memory(nc) as mem:
        w, attn = mem.sb("w", [P, R * P]), mem.sb("attn", [P, 2, R * P])
        w_a = mem.sb("w_a", [P, 2 * RH])
        tmp = mem.sb("tmp", [P, R * P])
        load = [(w[:, :], d["l3_w"])] + [(attn[:, n, :], v.partition_broadcast(P)) for n, v in enumerate((d["l3_attn_src"], d["l3_attn_dst"]))]
        with Memory(nc) as inner:
            loaded, order = inner.sem("loaded"), inner.sem("order")
            block = inner.block()

            @block.sync
            def _(sp):
                for to, of in load:
                    sp.dma_start(to, of).then_inc(loaded, 16)

            @block.vector
            def _(dve):
                link = chain(dve, order)
                dve.wait_ge(loaded, 48)
                for n in range(2):
                    link(dve.tensor_tensor(tmp[:, :], w[:, :], attn[:, n, :], ALU.mult))
                    link(dve.tensor_reduce(w_a[:, n * RH:(n + 1) * RH], tmp[:, :].rearrange("p (c k) -> p c k", k=P // H3), AX.X, ALU.add))
        with Memory(nc) as inner:
            out = inner.sb("out", [P, NB, R, ROW])
            ea = inner.sb("ea", [P, NB, RH])
            relation_tables(nc, d, r, w, w_a, out, ea)
    with Memory(nc) as mem:
        r.e = mem.sb("e", [P, T, H3])
        relation_scores(nc, d, r)
        relation_edges(nc, d, r)
    with Memory(nc) as mem:
        rows, out = mem.sb("rows", [P, 3, P]), mem.sb("out", [P, NB, P])
        relation_nodes(nc, d, r, out, rows, [(rows[:, n, :], v.partition_broadcast(P)) for n, v in
                                             enumerate((d["l3_bias"], d["l3_ln_gamma"], d["l3_ln_beta"]))])
        normalise(nc, r, out[:, :, :], None, weight=rows[:, 1, :], shift=rows[:, 2, :], residual=r.x[:, :, :])


def relation_tables(nc, d, r, w, w_a, out, ea):
    with Memory(nc) as mem:
        ps = [mem.ps(f"ps{k}") for k in range(3)]
        ps_a = [mem.ps(f"ps_a{k}") for k in range(3)]
        multiplied, copied, copied_a, stored = map(mem.sem, ("multiplied", "copied", "copied_a", "stored"))
        block = mem.block()

        @block.tensor
        def _(pe):
            for b in range(NB):
                if b >= 3:
                    pe.wait_ge(copied, b - 2)
                    pe.wait_ge(copied_a, b - 2)
                lhs = r.ht[:, b * P:(b + 1) * P]
                pe.matmul(ps[b % 3][:, :], lhs, w[:, :], start=True, stop=True)
                pe.matmul(ps_a[b % 3][:, 0:2 * RH], lhs, w_a[:, :], start=True, stop=True).then_inc(multiplied, 1)

        @block.scalar
        def _(act):
            for b in range(NB):
                act.wait_ge(multiplied, b + 1)
                act.activation(out[:, b, :, 0:P], ps[b % 3][:, :].rearrange("p (r f) -> p r f", r=R), ACT.Copy).then_inc(copied, 1)

        @block.vector
        def _(dve):
            for b in range(NB):
                dve.wait_ge(multiplied, b + 1)
                dve.tensor_copy(ea[:, b, :], ps_a[b % 3][:, RH:2 * RH])
                dve.tensor_copy(out[:, b, :, P:ROW], ps_a[b % 3][:, 0:RH].rearrange("p (r h) -> p r h", r=R)).then_inc(copied_a, 1)

        @block.sync
        def _(sp):
            n = 0
            for b in range(0, NB, 5):
                sp.wait_ge(copied, b + 5)
                sp.wait_ge(copied_a, b + 5)
                for k in range(R):
                    sp.dma_start(d["h_table"][k * NP + b * P:k * NP + (b + 5) * P, :].rearrange("(b p) f -> p b f", p=P),
                                 out[:, b:b + 5, k, :]).then_inc(stored, 16)
                    n += 1
            sp.dma_start(rows_of(d["ed_table"])(0, NB), ea[:, :, :]).then_inc(stored, 16)
            sp.wait_ge(stored, 16 * (n + 1))


def build(nc, d):
    r = Names()
    with Memory(nc) as mem:
        r.x = mem.sb("x_nodes", [P, NB, P])
        r.h = mem.sb("h_nodes", [P, NB, P])
        r.acc4 = mem.sb("acc4", [P, R, NX])
        r.acc = r.acc4[:, 0, :]
        r.ht = r.acc4[:, 1, 0:NP]
        r.inv_count = r.acc4[:, 2, 0:NP]
        r.root_count = r.acc4[:, 3, 0:NP]
        r.z = mem.sb("z", [RH, NX])
        r.rel = mem.sb("rel", [P, M, G])
        r.group_rel = mem.sb("group_rel", [P, T])
        r.type_hot = mem.sb("type_hot", [P, T, R])
        r.iota_w = mem.sb("iota_w", [P, W])
        r.iota_g = mem.sb("iota_g", [P, GW * GN])
        r.iota_r = mem.sb("iota_r", [P, R])
        r.window = mem.sb("window", [P, W])
        r.ident = mem.sb("ident", [P, P])
        r.typed_rel = mem.sb("typed_rel", [P, T])
        r.passes = mem.sb("passes", [P, 3], I32)
        r.base = mem.sb("base", [1, BASE_ROWS * M], I16)
        r.pair_group = mem.sb("pair_group", [1, U], I32)
        before = nc.snapshot_sems()
        prepare(nc, d, r)
        for layer in (attention_layer, mean_layer, chebyshev_layer, relation_layer):
            normalise(nc, r, r.x[:, :, :], r.h[:, :, :], relu=True)
            turn(nc, r, r.h[:, :, :], r.ht[:, :])
            layer(nc, d, r)
            nc.clear_and_free_semaphores(nc.allocated_since(before))
            nc.all_engine_barrier()
            before = nc.snapshot_sems()
        stored = mem.sem("out_stored")
        block = mem.block()

        @block.sync
        def _(sp):
            sp.dma_start(d["out"], r.x[:, :, :]).then_inc(stored, 16)
            sp.wait_ge(stored, 16)


def kernel(**inputs):
    import concourse.bacc as bacc
    from concourse.bass_utils import run_bass_kernel_spmd

    nc = bacc.Bacc("TRN2", target_bir_lowering=False, num_devices=1)
    d = {}
    arrays = {}

    def put(name, a):
        a = np.ascontiguousarray(a)
        arrays["in_" + name] = a
        d[name] = nc.dram_tensor("in_" + name, a.shape, mybir.dt.from_np(a.dtype), kind="ExternalInput").ap()

    def by_tile(a, value):
        return np.pad(np.asarray(a), (0, EP - E), constant_values=value).reshape(T, P).T

    g = {k: np.asarray(v) for k, v in inputs.items()}
    put("x", np.pad(g["x"], ((0, NP - N), (0, 0))).reshape(NB, P, P).transpose(1, 0, 2))
    put("src", by_tile(g["src"], 0))
    put("dst", by_tile(g["dst"], FAR))
    put("edge_type", by_tile(g["edge_type_4"], 0))
    put("dst_sorted", np.pad(g["dst"], (0, EP - E), mode="edge"))
    put("edge_attr", np.pad(g["edge_attr_3"], ((0, EP - E), (0, 0))).T)
    for name in ("Wq", "Wk", "Wv", "Wo", "bo", "ln1_g", "ln1_b", "W1", "b2", "ln2_g", "ln2_b"):
        put("l0_" + name.lower(), g["L0_gnn_" + name])
    put("l0_b1", g["L0_gnn_b1"].reshape(2, P).T)
    put("l0_w2", g["L0_gnn_W2"].reshape(2, P, P).transpose(1, 0, 2))
    put("l1_w1", g["L1_gnn_W1"].T)
    put("l1_w2", g["L1_gnn_W2"].T.reshape(2, P, P).transpose(1, 0, 2))
    put("l1_b1", g["L1_gnn_b1"])
    put("l1_b2", g["L1_gnn_b2"])
    put("l2_w", g["L2_gnn_weights"].transpose(1, 0, 2))
    put("l3_w", g["L3_gnn_W"].transpose(1, 0, 2).reshape(P, R * P))
    put("l3_attn_src", g["L3_gnn_attn_src"].reshape(-1))
    put("l3_attn_dst", g["L3_gnn_attn_dst"].reshape(-1))
    for name in ("bias", "ln_gamma", "ln_beta"):
        put("l3_" + name, g["L3_gnn_" + name])
    for name, shape, dtype in (("macro_bounds", [2 * M], I32), ("pair_bounds", [2 * U], I32), ("key", [P, T], I32),
                               ("kv_table", [NP, 2 * P], F32), ("q_table", [NX, P], F32), ("row_table", [NP, P], F32),
                               ("h_table", [R * NP, ROW], F32), ("spill", [M * P, G * ROW], F32), ("base_table", [BASE_ROWS * M], I16), ("ed_table", [NX, RH], F32),
                               ("top_table", [NX, RH], F32)):
        d[name] = nc.dram_tensor(name, shape, dtype).ap()
    d["out"] = nc.dram_tensor("out", (P, NB, P), F32, kind="ExternalOutput").ap()
    build(nc, d)
    res = run_bass_kernel_spmd(nc, [arrays], core_ids=[0])
    return res.results[0]["out"].transpose(1, 0, 2).reshape(NP, P)[:N]
```
